# Optimizing a Trainium2 kernel written in Bass

```python
import numpy as np
import jax
import jax.numpy as jnp

def _softmax(x, axis=-1):
    return jax.nn.softmax(x, axis=axis)

def _gelu(x):
    return jax.nn.gelu(x, approximate=True)

def _silu(x):
    return jax.nn.silu(x)

def _sigmoid(x):
    return jax.nn.sigmoid(x)

def _layernorm(x, axis=-1, eps=1e-05):
    m = jnp.mean(x, axis=axis, keepdims=True)
    v = jnp.var(x, axis=axis, keepdims=True)
    return (x - m) / jnp.sqrt(v + eps)

def _scatter_add(tgt, idx, src, axis=0):
    return tgt.at[idx].add(src)

def _segment_sum(src, seg, n):
    return jax.ops.segment_sum(src, seg, n)
kernel_name = 'mk_adaln_d1_jaxref_r4_345ef3'

def setup_inputs(seed: int=0):
    np.random.seed(seed)
    _w = jnp.asarray

    def _L0_attn_setup():
        import jax, jax.numpy as jnp
        import numpy as np
        MAX_WAVELENGTH = 10000.0
        NEG_INF = -1000000000.0

        def apply_rope(x):
            S, D = (x.shape[1], x.shape[-1])
            inv_freq = 1.0 / MAX_WAVELENGTH ** (jnp.arange(0, D, 2, dtype=jnp.float32) / D)
            t = jnp.arange(S, dtype=jnp.float32)[:, None] * inv_freq[None, :]
            emb = jnp.concatenate([t, t], axis=-1)
            cos = jnp.cos(emb)[None, :, None, :].astype(x.dtype)
            sin = jnp.sin(emb)[None, :, None, :].astype(x.dtype)
            x1, x2 = jnp.split(x, 2, axis=-1)
            rotated = jnp.concatenate([-x2, x1], axis=-1)
            return x * cos + rotated * sin
        key = jax.random.key(seed)
        k1, k2, k3 = jax.random.split(key, 3)
        B, S, dim = (2, 512, 256)
        x = jax.random.normal(k1, (B, S, dim), dtype=jnp.float32)
        w_qkv = jax.random.normal(k2, (dim, 3 * dim), dtype=jnp.float32) * dim ** (-0.5)
        w_proj = jax.random.normal(k3, (dim, dim), dtype=jnp.float32) * dim ** (-0.5)
        b_proj = jnp.zeros((dim,), dtype=jnp.float32)
        return {'x': x, 'w_qkv': w_qkv, 'w_proj': w_proj, 'b_proj': b_proj}
    _L0_attn_in = _L0_attn_setup()

    def _L0_ffn_setup():
        import jax, jax.numpy as jnp
        import numpy as np
        from jax import lax
        TOP_K = 4
        N_GROUP = 4
        TOPK_GROUP = 2
        ROUTED_SCALE = 2.5
        NEG_INF = -1000000000.0

        def _route(xf, router_weight, router_bias):
            T = xf.shape[0]
            E = router_weight.shape[0]
            logits = xf @ router_weight.T
            scores = jax.nn.sigmoid(logits)
            s_choice = scores + router_bias
            per_group = E // N_GROUP
            sg = s_choice.reshape(T, N_GROUP, per_group)
            group_scores = lax.top_k(sg, 2)[0].sum(-1)
            _, gidx = lax.top_k(group_scores, TOPK_GROUP)
            gmask = jnp.zeros((T, N_GROUP), dtype=bool).at[jnp.arange(T)[:, None], gidx].set(True)
            masked = jnp.where(gmask[:, :, None], sg, NEG_INF).reshape(T, E)
            _, topk_idx = lax.top_k(masked, TOP_K)
            w = jnp.take_along_axis(scores, topk_idx, axis=1)
            w = w / (w.sum(-1, keepdims=True) + 1e-20) * ROUTED_SCALE
            combine = jnp.zeros((T, E), dtype=xf.dtype).at[jnp.arange(T)[:, None], topk_idx].add(w)
            return combine
        key = jax.random.key(seed)
        ks = jax.random.split(key, 6)
        B, S, H, I, E = (2, 512, 256, 128, 16)
        x = jax.random.normal(ks[0], (B, S, H), dtype=jnp.float32)
        router_weight = jax.random.normal(ks[1], (E, H), dtype=jnp.float32) * 0.02
        router_bias = jnp.zeros((E,), dtype=jnp.float32)
        w_gate = jax.random.normal(ks[2], (E, I, H), dtype=jnp.float32) * 0.02
        w_up = jax.random.normal(ks[3], (E, I, H), dtype=jnp.float32) * 0.02
        w_down = jax.random.normal(ks[4], (E, H, I), dtype=jnp.float32) * 0.02
        return {'x': x, 'router_weight': router_weight, 'router_bias': router_bias, 'w_gate': w_gate, 'w_up': w_up, 'w_down': w_down}
    _L0_ffn_in = _L0_ffn_setup()
    _L0_c = _w((lambda *s: np.random.randn(*s).astype(np.float32) * 0.05)(16, 256))
    _L0_wmod = _w((lambda *s: np.random.randn(*s).astype(np.float32) * 0.05)(256, 6 * 256) * 256 ** (-0.5))
    _d = {'L0_attn_x': _L0_attn_in['x'], 'L0_attn_w_qkv': _L0_attn_in['w_qkv'], 'L0_attn_w_proj': _L0_attn_in['w_proj'], 'L0_attn_b_proj': _L0_attn_in['b_proj'], 'L0_ffn_router_weight': _L0_ffn_in['router_weight'], 'L0_ffn_router_bias': _L0_ffn_in['router_bias'], 'L0_ffn_w_gate': _L0_ffn_in['w_gate'], 'L0_ffn_w_up': _L0_ffn_in['w_up'], 'L0_ffn_w_down': _L0_ffn_in['w_down'], 'L0_c': _L0_c, 'L0_wmod': _L0_wmod}
    _x0 = _d['L0_attn_x']
    _d['L0_attn_x'] = jax.random.normal(jax.random.fold_in(jax.random.key(seed), 1), (16, 512, 256), dtype=_x0.dtype)
    del _x0
    return _d

def reference(L0_attn_x, L0_attn_w_qkv, L0_attn_w_proj, L0_attn_b_proj, L0_ffn_router_weight, L0_ffn_router_bias, L0_ffn_w_gate, L0_ffn_w_up, L0_ffn_w_down, L0_c, L0_wmod):

    def _L0_attn_ref(x, w_qkv, w_proj, b_proj):
        import jax, jax.numpy as jnp
        import numpy as np
        MAX_WAVELENGTH = 10000.0
        NEG_INF = -1000000000.0

        def apply_rope(x):
            S, D = (x.shape[1], x.shape[-1])
            inv_freq = 1.0 / MAX_WAVELENGTH ** (jnp.arange(0, D, 2, dtype=jnp.float32) / D)
            t = jnp.arange(S, dtype=jnp.float32)[:, None] * inv_freq[None, :]
            emb = jnp.concatenate([t, t], axis=-1)
            cos = jnp.cos(emb)[None, :, None, :].astype(x.dtype)
            sin = jnp.sin(emb)[None, :, None, :].astype(x.dtype)
            x1, x2 = jnp.split(x, 2, axis=-1)
            rotated = jnp.concatenate([-x2, x1], axis=-1)
            return x * cos + rotated * sin
        B, S, dim = x.shape
        heads = 16
        head_dim = dim // heads
        scale = head_dim ** (-0.5)
        qkv = x @ w_qkv
        qkv = qkv.reshape(B, S, 3, heads, head_dim)
        Q, K, V = (qkv[:, :, 0], qkv[:, :, 1], qkv[:, :, 2])
        Q = apply_rope(Q)
        K = apply_rope(K)
        attn = jnp.einsum('bqhd,bkhd->bhqk', Q, K) * scale
        causal = jnp.tril(jnp.ones((S, S), dtype=bool))[None, None]
        attn = jnp.where(causal, attn, jnp.asarray(NEG_INF, attn.dtype))
        attn = jax.nn.softmax(attn, axis=-1)
        out = jnp.einsum('bhqk,bkhd->bqhd', attn, V).reshape(B, S, dim)
        return out @ w_proj + b_proj

    def _L0_ffn_ref(x, router_weight, router_bias, w_gate, w_up, w_down):
        import jax, jax.numpy as jnp
        import numpy as np
        from jax import lax
        TOP_K = 4
        N_GROUP = 4
        TOPK_GROUP = 2
        ROUTED_SCALE = 2.5
        NEG_INF = -1000000000.0

        def _route(xf, router_weight, router_bias):
            T = xf.shape[0]
            E = router_weight.shape[0]
            logits = xf @ router_weight.T
            scores = jax.nn.sigmoid(logits)
            s_choice = scores + router_bias
            per_group = E // N_GROUP
            sg = s_choice.reshape(T, N_GROUP, per_group)
            group_scores = lax.top_k(sg, 2)[0].sum(-1)
            _, gidx = lax.top_k(group_scores, TOPK_GROUP)
            gmask = jnp.zeros((T, N_GROUP), dtype=bool).at[jnp.arange(T)[:, None], gidx].set(True)
            masked = jnp.where(gmask[:, :, None], sg, NEG_INF).reshape(T, E)
            _, topk_idx = lax.top_k(masked, TOP_K)
            w = jnp.take_along_axis(scores, topk_idx, axis=1)
            w = w / (w.sum(-1, keepdims=True) + 1e-20) * ROUTED_SCALE
            combine = jnp.zeros((T, E), dtype=xf.dtype).at[jnp.arange(T)[:, None], topk_idx].add(w)
            return combine
        B, S, H = x.shape
        E = w_gate.shape[0]
        xf = x.reshape(-1, H)
        combine = _route(xf, router_weight, router_bias)
        out = jnp.zeros_like(xf)
        for e in range(E):
            g = xf @ w_gate[e].T
            u = xf @ w_up[e].T
            y_e = jax.nn.silu(g) * u @ w_down[e].T
            out = out + combine[:, e:e + 1] * y_e
        return out.reshape(B, S, H)
    x = L0_attn_x
    mod = (_silu(L0_c) @ L0_wmod).reshape(L0_c.shape[0], 6, 1, -1)
    sa, ca, ga, sb, cb, gb = (mod[:, 0], mod[:, 1], mod[:, 2], mod[:, 3], mod[:, 4], mod[:, 5])
    ga = (2 * (ga >= 0) - 1) * jnp.maximum(jnp.abs(ga), 0.25)
    gb = (2 * (gb >= 0) - 1) * jnp.maximum(jnp.abs(gb), 0.25)
    h = _layernorm(x, axis=-1) * (1 + ca) + sa
    x = x + ga * _L0_attn_ref(h, L0_attn_w_qkv, L0_attn_w_proj, L0_attn_b_proj)
    h = _layernorm(x, axis=-1) * (1 + cb) + sb
    x = x + gb * _L0_ffn_ref(h, L0_ffn_router_weight, L0_ffn_router_bias, L0_ffn_w_gate, L0_ffn_w_up, L0_ffn_w_down)
    return x

_drawn_inputs = setup_inputs


def setup_inputs(seed=0):
    import zlib

    import numpy as np

    out = dict(_drawn_inputs(seed))
    spreads = {'L0_attn_b_proj': (0.0, 0.304), 'L0_ffn_router_bias': (0.0, 0.8)}
    factors = {'L0_ffn_router_weight': 8.0,
     'L0_ffn_w_gate': 8.0,
     'L0_ffn_w_up': 8.0,
     'L0_ffn_w_down': 8.0}
    for name, (base, spread) in spreads.items():
        noise = np.random.default_rng([zlib.crc32(name.encode()), seed]).standard_normal(out[name].shape)
        drawn = base * np.exp(spread * noise) if base else spread * noise
        out[name] = jnp.asarray(drawn.astype(out[name].dtype))
    for name, factor in factors.items():
        out[name] = (out[name] * factor).astype(out[name].dtype)
    return out
```

```python
from contextlib import ExitStack

import numpy as np

import concourse.bass as bass
from concourse import mybir

ALU = mybir.AluOpType
ACT = mybir.ActivationFunctionType
F32 = mybir.dt.float32
F32R = mybir.dt.float32r
BF16 = mybir.dt.bfloat16
AX_X = mybir.AxisListType.X

P = 128
BATCH, SEQ, DIM = 16, 512, 256
HEADS, HD = 16, 16
EXPERTS, INNER = 16, 128
GROUPS, TOP_GROUPS, TOP_K = 4, 2, 4
ROUTED_SCALE = 2.5
EPS = 1e-5
TILES = SEQ // P
KC = DIM // P
PAIRS = HEADS // 2
STRIP = 64
MROW = 48
OG = 4
SCALE = HD ** -0.5
NEG = -1e9

S_FILLS = 7
T_FILLS = 3
KT_AT = {0: 0, 1: SEQ, 3: SEQ + 3 * P, 2: 2 * SEQ}
PROBS = 2 * SEQ + 2 * P
ROUTER_STEPS = 36


class Signal:

    def __init__(self, sem, per):
        self.sem, self.per = sem, per

    def at(self, b, k):
        return b * self.per + k


def wait(eng, signal, b, k):
    value = signal.at(b, k)
    if isinstance(value, int) and value <= 0:
        return
    eng.wait_ge(signal.sem, value)


def wait_apart(eng, signal, b, k, passed):
    wait(eng, signal, b, k)
    eng.sem_inc(passed.sem, 1)


def build(nc, x, wqkv, wproj, bproj, rw, rbias, wgu, wd, ct, wmod, cosq, sinq, tril_bias, ident, pick, out):
    with ExitStack() as ctx:
        def sb(name, shape, dt=F32):
            return ctx.enter_context(nc.sbuf_tensor(name, shape, dt))

        def ps(name, shape):
            return ctx.enter_context(nc.psum_tensor(name, shape, F32))

        def signal(name, per):
            return Signal(ctx.enter_context(nc.semaphore(name)), per)

        w_qkv = sb("w_qkv", [P, KC, 3 * DIM])
        w_proj = sb("w_proj", [P, KC, DIM])
        w_router = sb("w_router", [P, KC, EXPERTS])
        w_gu = sb("w_gu", [P, EXPERTS, 2, KC, INNER])
        w_down = sb("w_down", [P, EXPERTS, DIM])
        cos_t = sb("cos_t", [P, TILES, HD // 2])
        sin_t = sb("sin_t", [P, TILES, 2, HD // 2])
        mask = sb("mask", [P, SEQ])
        idn = sb("idn", [P, P])
        pick_f = sb("pick_f", [2 * EXPERTS, EXPERTS])
        pick_r = sb("pick_r", [2 * EXPERTS, EXPERTS], F32R)
        rb = sb("rb", [P, EXPERTS])
        half = sb("half", [P, TILES])
        mods = sb("mods", [P, BATCH, 8])
        act = sb("act", [P, EXPERTS, SEQ])
        x_in = sb("x_in", [P, TILES, DIM])
        x1 = sb("x1", [P, TILES, DIM])
        x1_prev = sb("x1_prev", [P, TILES, DIM])
        xn = sb("xn", [P, TILES, DIM])
        h1T = sb("h1T", [P, KC, SEQ])
        h2T = sb("h2T", [P, KC, SEQ])
        QT = sb("QT", [P, PAIRS, SEQ], F32R)
        KT = sb("KT", [P, PAIRS, SEQ], F32R)
        V = sb("V", [P, TILES, HEADS, 32])
        probs = sb("probs", [P, 2, PROBS])
        QS = sb("QS", [P, HEADS, STRIP])
        KS = sb("KS", [P, HEADS, STRIP])
        work = sb("work", [P, 4, SEQ])
        OT = sb("OT", [P, HEADS // OG, SEQ])
        o_tok = sb("o_tok", [P, 2, DIM])
        gates = sb("gates", [P, 2, DIM])
        gate_b = sb("gate_b", [P, DIM])
        mmax = sb("mmax", [P, HEADS, TILES])
        mt = sb("mt", [P, TILES, P])
        cT = sb("cT", [2 * EXPERTS, SEQ], F32R)
        modA = sb("modA", [P, 4])
        modB = sb("modB", [P, 4])
        stats = sb("stats", [P, TILES, 6])
        mv = sb("mv", [P, TILES, 2])
        vare = sb("vare", [P, TILES])
        rstd = sb("rstd", [P, TILES])
        lin = sb("lin", [P, 2, HEADS])
        R = sb("R", [P, 16, TILES * EXPERTS])
        before = sb("before", [P, TILES * GROUPS * GROUPS])
        pfx = sb("pfx", [P, 2, TILES, 8 + EXPERTS])
        m8 = sb("m8", [P, TILES, 8])
        cs = sb("cs", [P, TILES, 2 * EXPERTS])
        flat = probs[:, :, :].rearrange("p a n -> p (a n)")
        onT = flat[:, 0:KC * SEQ].rearrange("p (c n) -> p c n", c=KC)
        y_sb = flat[:, KC * SEQ:(KC + 1) * SEQ]
        out_sb = flat[:, (KC + 1) * SEQ:(KC + 3) * SEQ].rearrange("p (t n) -> p t n", t=TILES)
        aflat = act[:, :, :].rearrange("p e n -> p (e n)")
        w_mod = aflat[:, 0:KC * 6 * DIM].rearrange("p (c n) -> p c n", c=KC)
        o0 = KC * 6 * DIM
        c_sb, c_e, c_d, c_r, c_s = (aflat[:, o0 + i * 32:o0 + i * 32 + 32] for i in range(5))
        g16, sg16 = (aflat[0:BATCH, 4096 + i * 512:4608 + i * 512] for i in range(2))
        gfin = aflat[0:BATCH, 5120:5120 + 768].rearrange("p (t n) -> p t n", t=3)
        b16 = aflat[0:BATCH, 6144:6144 + DIM]

        ps_s = ps("ps_s", [P, 2, SEQ])
        ps_t = ps("ps_t", [P, 2, SEQ])
        ps_o = ps("ps_o", [P, SEQ])
        ps_g = ps("ps_g", [P, SEQ])
        ps_u = ps("ps_u", [P, SEQ])
        ps_c = ps("ps_c", [P, SEQ])
        gate_dram = nc.dram_tensor("gate_dram", (BATCH, 3, DIM), F32).ap()

        weights_in = signal("weights_in", 0)
        consts_in = signal("consts_in", 0)
        mod_in = signal("mod_in", 0)
        experts_in = signal("experts_in", 0)
        setup_v = signal("setup_v", 0)
        setup_p = signal("setup_p", 0)
        setup_a = signal("setup_a", 0)
        setup_t = signal("setup_t", 0)
        gates_out = signal("gates_out", 0)
        x_loaded = signal("x_loaded", 16)
        xres_loaded = signal("xres_loaded", 16)
        prev_copied = signal("prev_copied", 16)
        gates_loaded = signal("gates_loaded", 32)
        gateb_loaded = signal("gateb_loaded", 16)
        stored = signal("stored", 32)
        s_filled = signal("s_filled", PAIRS * S_FILLS)
        t_filled = signal("t_filled", HEADS * T_FILLS)
        pv_done = signal("pv_done", HEADS)
        g_done, u_done, c_done = (signal(n, EXPERTS) for n in ("g_done", "u_done", "c_done"))
        h1_tr = signal("h1_tr", KC)
        o_tr = signal("o_tr", TILES)
        qkv_done = signal("qkv_done", TILES)
        on_tr = signal("on_tr", 2)
        proj_done = signal("proj_done", 2)
        h2_tr = signal("h2_tr", KC)
        logits_done = signal("logits_done", 1)
        c_tr = signal("c_tr", 1)
        down_done = signal("down_done", 2)
        stack_tr = signal("stack_tr", 4 * TILES)
        exp_done = signal("exp_done", HEADS * T_FILLS)
        ot_ready = signal("ot_ready", HEADS // OG)
        tanh_done = signal("tanh_done", EXPERTS)
        h1_ready = signal("h1_ready", KC)
        rounded = signal("rounded", 2 * TILES)
        v_ready = signal("v_ready", TILES)
        on_ready = signal("on_ready", 2)
        stack_ready = signal("stack_ready", 4 * TILES)
        h2_ready = signal("h2_ready", KC)
        rexp_done = signal("rexp_done", 1)
        ct_ready = signal("ct_ready", 1)
        s_used = signal("s_used", PAIRS * S_FILLS)
        m_high = signal("m_high", PAIRS)
        m_ready = signal("m_ready", PAIRS)
        gt_done, gu_done, a_ready = (signal(n, EXPERTS) for n in ("gt_done", "gu_done", "a_ready"))
        ln1 = signal("ln1", 4)
        ln2 = signal("ln2", 4)
        mod_a = signal("mod_a", 1)
        mod_b = signal("mod_b", 1)
        linv = signal("linv", TILES)
        o_tok_ready = signal("o_tok_ready", TILES)
        roped = signal("roped", TILES)
        low_ready = signal("low_ready", TILES)
        ga_mul = signal("ga_mul", 2)
        xg_add = signal("xg_add", 2)
        x1_ready = signal("x1_ready", 2)
        router = signal("router", ROUTER_STEPS)
        y_ready = signal("y_ready", 2)
        masked = signal("masked", 2 * HEADS)
        rope_sum = signal("rope_sum", TILES)
        rstd1 = signal("rstd1", 1)
        rstd2 = signal("rstd2", 1)
        out_ready = signal("out_ready", 2)

        ve_passed = signal("ve_passed", 0)
        po_passed = signal("po_passed", 0)

        LAST = BATCH - 1

        def every_batch(eng, first, middle, last):
            first(0)
            with eng.Fori(1, LAST) as b:
                middle(b)
            last(LAST)

        block = ctx.enter_context(nc.Block())

        @block.sync
        def _(sp):
            def dram_x(b):
                return x[b].rearrange("(t p) d -> p t d", p=P)

            def gate_rows(b, lo, hi):
                src = gate_dram[b, lo:hi, :]
                return bass.AP(src.tensor, src.offset, [[0, P], [DIM, hi - lo], [1, DIM]]) if isinstance(b, int) \
                    else gate_dram[bass.ds(b, 1), lo:hi, :].broadcast_to([P, hi - lo, DIM])

            sp.dma_start(x_in[:], dram_x(0)).then_inc(x_loaded.sem, 16)
            sp.dma_start(idn[:], ident).then_inc(consts_in.sem, 16)
            sp.dma_start(c_sb, ct).then_inc(mod_in.sem, 16)
            sp.dma_start(w_mod, wmod).then_inc(mod_in.sem, 16)
            sp.dma_start(b16, bproj.broadcast_to([BATCH, DIM])).then_inc(mod_in.sem, 16)
            sp.dma_start(cos_t[:], cosq).then_inc(consts_in.sem, 16)
            sp.dma_start(sin_t[:], sinq).then_inc(consts_in.sem, 16)
            sp.dma_start(mask[:], tril_bias).then_inc(consts_in.sem, 16)
            sp.dma_start(pick_f[:], pick).then_inc(consts_in.sem, 16)
            sp.dma_start(rb[:], rbias.broadcast_to([P, EXPERTS])).then_inc(consts_in.sem, 16)
            sp.dma_start(w_qkv[:], wqkv).then_inc(weights_in.sem, 16)
            sp.dma_start(w_proj[:], wproj).then_inc(weights_in.sem, 16)
            sp.dma_start(w_router[:], rw).then_inc(weights_in.sem, 16)
            sp.dma_start(w_gu[:], wgu).then_inc(experts_in.sem, 16)
            sp.dma_start(w_down[:], wd).then_inc(experts_in.sem, 16)
            sp.wait_ge(setup_v.sem, 10)
            sp.dma_start(gate_dram, gfin).then_inc(gates_out.sem, 16)
            sp.wait_ge(gates_out.sem, 16)

            def batch(b, moe, more):
                if more:
                    wait(sp, ln1, b + 1 - 1, 4)
                    sp.dma_start(x_in[:], dram_x(b + 1)).then_inc(x_loaded.sem, 16)
                if moe:
                    wait(sp, x1_ready, b - 1, 2)
                    wait(sp, ln2, b - 1, 4)
                    wait(sp, out_ready, b - 2, 2)
                    sp.dma_start(x1_prev[:], x1[:]).then_inc(prev_copied.sem, 16)
                    wait(sp, prev_copied, b - 1, 16)
                    wait(sp, y_ready, b - 2, 2)
                    sp.dma_start(gate_b[:], gate_rows(b - 1, 1, 2).rearrange("p o d -> p (o d)")).then_inc(gateb_loaded.sem, 16)
                sp.dma_start(x1[:], dram_x(b)).then_inc(xres_loaded.sem, 16)
                wait(sp, x1_ready, b - 1, 2)
                sp.dma_start(gates[:, 0, :], gate_rows(b, 0, 1).rearrange("p o d -> p (o d)")).then_inc(gates_loaded.sem, 16)
                sp.dma_start(gates[:, 1, :], gate_rows(b, 2, 3).rearrange("p o d -> p (o d)")).then_inc(gates_loaded.sem, 16)
                if moe:
                    store(b - 1)

            def store(b):
                dst = out[b].rearrange("(t p) d -> p t d", p=P)
                for f in range(2):
                    wait(sp, out_ready, b, f + 1)
                    sp.dma_start(dst[:, 2 * f:2 * f + 2, :], out_sb[:, 2 * f:2 * f + 2, :]).then_inc(stored.sem, 16)

            every_batch(sp, lambda b: batch(b, False, True), lambda b: batch(b, True, True),
                        lambda b: batch(b, True, False))
            wait(sp, x1_ready, LAST, 2)
            wait(sp, ln2, LAST, 4)
            wait(sp, out_ready, LAST - 1, 2)
            sp.dma_start(x1_prev[:], x1[:]).then_inc(prev_copied.sem, 16)
            wait(sp, y_ready, LAST - 1, 2)
            sp.dma_start(gate_b[:], gate_rows(LAST, 1, 2).rearrange("p o d -> p (o d)")).then_inc(gateb_loaded.sem, 16)
            store(LAST)
            sp.wait_ge(stored.sem, 32 * BATCH)

        @block.tensor
        def _(pe):
            mm = nc.tensor.matmul

            def fill_s(b, p, k):
                f = p * S_FILLS + k
                wait(pe, s_used, b, f - 1)
                bank = ps_s[:, f % 2, :]
                if k == S_FILLS - 1:
                    wait(pe, m_ready, b, p + 1)
                    for t in range(TILES):
                        ins = nc.tensor.transpose(bank[:, t * P:(t + 1) * P], mt[:, t, :], idn[:])
                else:
                    r0 = STRIP * (k // 3)
                    for qt, at, n in (((3, 0, SEQ),), ((2, 0, 3 * P),), ((0, 0, 2 * P), (1, 2 * P, 2 * P)))[k % 3]:
                        ins = mm(bank[:, at:at + n], QT[r0:r0 + MROW, p, qt * P:(qt + 1) * P],
                                 KT[r0:r0 + MROW, p, 0:n], start=True, stop=True)
                ins.then_inc(s_filled.sem, 1)

            def fill_t(b, h, k):
                f = h * T_FILLS + k
                if k == 0 and h % 2 == 0:
                    wait(pe, s_used, b, (h // 2 + 1) * S_FILLS)
                wait(pe, exp_done, b, f - 1)
                if f < 2:
                    wait(pe, ct_ready, b - 1, 1)
                bank = ps_t[:, f % 2, :]
                r0, p = STRIP * (h % 2), h // 2
                for kt, at, q0 in (((0, 0, 0),), ((3, 2 * P, 2 * P), (1, 0, P)), ((2, 0, 2 * P),))[k]:
                    ins = mm(bank[:, at:at + SEQ - q0], KT[r0:r0 + STRIP, p, kt * P:(kt + 1) * P],
                             QT[r0:r0 + STRIP, p, q0:SEQ], start=True, stop=True)
                ins.then_inc(t_filled.sem, 1)

            def values(b, h):
                wait(pe, masked, b, 2 * h + 2)
                wait(pe, exp_done, b, T_FILLS * (h + 1))
                if h == 0:
                    wait(pe, v_ready, b, TILES)
                if h % OG == 0:
                    wait(pe, ot_ready, b, h // OG)
                if h == 0:
                    wait(pe, y_ready, b - 2, 2)
                r0 = 32 * (h % OG)
                for kt in range(TILES):
                    n = SEQ - kt * P
                    ins = mm(ps_o[r0:r0 + 32, kt * P:SEQ], V[:, kt, h, :], probs[:, h % 2, KT_AT[kt]:KT_AT[kt] + n],
                             start=kt == 0, stop=kt == TILES - 1)
                ins.then_inc(pv_done.sem, 1)

            def gate(b, e):
                if e == 0:
                    wait(pe, h2_ready, b, KC)
                wait(pe, gt_done, b, e)
                for c in range(KC):
                    ins = mm(ps_g[:], w_gu[:, e, 0, c, :], h2T[:, c, :], start=c == 0, stop=c == KC - 1)
                ins.then_inc(g_done.sem, 1)

            def up(b, e):
                wait(pe, gu_done, b, e)
                for c in range(KC):
                    ins = mm(ps_u[:], w_gu[:, e, 1, c, :], h2T[:, c, :], start=c == 0, stop=c == KC - 1)
                ins.then_inc(u_done.sem, 1)

            def weight(b, e):
                if e == 0:
                    wait(pe, ct_ready, b, 1)
                wait(pe, a_ready, b, e)
                mm(ps_c[:], pick_r[:, e:e + 1].broadcast_to([2 * EXPERTS, P]), cT[:], start=True, stop=True)\
                    .then_inc(c_done.sem, 1)

            def attention(b, moe):
                m = b - 1
                wait(pe, stack_ready, b, 4 * TILES)
                for k in range(S_FILLS):
                    fill_s(b, 0, k)
                for p in range(PAIRS):
                    h0, h1, more = 2 * p, 2 * p + 1, p + 1 < PAIRS
                    if more:
                        fill_s(b, p + 1, 0)
                    fill_t(b, h0, 0)
                    if moe:
                        gate(m, h0)
                    if more:
                        fill_s(b, p + 1, 1)
                    fill_t(b, h0, 1)
                    if moe:
                        up(m, h0)
                    if more:
                        fill_s(b, p + 1, 2)
                    fill_t(b, h0, 2)
                    if more:
                        fill_s(b, p + 1, 3)
                    if moe:
                        weight(m, h0)
                    if more:
                        fill_s(b, p + 1, 4)
                    if p:
                        values(b, h0 - 1)
                    if more:
                        fill_s(b, p + 1, 5)
                    fill_t(b, h1, 0)
                    if moe:
                        gate(m, h1)
                    fill_t(b, h1, 1)
                    if moe:
                        up(m, h1)
                    fill_t(b, h1, 2)
                    if more:
                        fill_s(b, p + 1, 6)
                    if moe:
                        weight(m, h1)
                    values(b, h0)
                values(b, HEADS - 1)

            def h1_transposes(b, early):
                wait(pe, ln1, b, 4)
                for c in range(KC):
                    bank = (ps_g, ps_u)[c]
                    for t in range(TILES):
                        ins = nc.tensor.transpose(bank[:, t * P:(t + 1) * P], xn[:, t, c * P:(c + 1) * P], idn[:])
                    ins.then_inc(h1_tr.sem, 1)

            def qkv(b, t):
                if t == 0:
                    wait(pe, h1_ready, b, KC)
                wait(pe, roped, b, t)
                wait(pe, v_ready, b, t)
                hT = [h1T[:, c, t * P:(t + 1) * P] for c in range(KC)]
                for c in range(KC):
                    mm(ps_s[:, 0, :], hT[c], w_qkv[:, c, 0:2 * DIM], start=c == 0, stop=c == KC - 1)
                at = (t % 2) * DIM
                for c in range(KC):
                    ins = mm(ps_s[:, 1, at:at + DIM], hT[c], w_qkv[:, c, 2 * DIM:3 * DIM], start=c == 0, stop=c == KC - 1)
                ins.then_inc(qkv_done.sem, 1)

            def stack(b, t):
                wait(pe, rounded, b, 2 * t + 2)
                wait(pe, low_ready, b, t + 1)
                for k in range(4):
                    f = 4 * t + k
                    if f >= 2:
                        wait(pe, stack_ready, b, f - 1)
                    bank, src = (ps_g, ps_u)[f % 2], (QS, KS)[k // 2]
                    for j in range(4):
                        p = 4 * (k % 2) + j
                        ins = nc.tensor.transpose(
                            bank[:, j * P:(j + 1) * P], src[:, 2 * p:2 * p + 2, :].rearrange("p h r -> p (h r)"), idn[:])
                    ins.then_inc(stack_tr.sem, 1)

            def o_transposes(b, t):
                if t == 0:
                    wait(pe, ot_ready, b, HEADS // OG)
                if t >= 2:
                    wait(pe, o_tok_ready, b, t - 1)
                for g in range(HEADS // OG):
                    ins = nc.tensor.transpose(ps_t[:, t % 2, g * P:(g + 1) * P], OT[:, g, t * P:(t + 1) * P], idn[:])
                ins.then_inc(o_tr.sem, 1)

            def on_transposes(b, f):
                for t in (2 * f, 2 * f + 1):
                    wait(pe, o_tok_ready, b, t + 1)
                    if t == 2:
                        wait(pe, on_ready, b, 1)
                    for c in range(KC):
                        at = (t % 2) * DIM + c * P
                        ins = nc.tensor.transpose(ps_c[:, at:at + P], o_tok[:, t % 2, c * P:(c + 1) * P], idn[:])
                    if t % 2:
                        ins.then_inc(on_tr.sem, 1)

            def project(b, f):
                wait(pe, on_ready, b, f + 1)
                if f == 0:
                    wait(pe, o_tok_ready, b, TILES)
                for t in (2 * f, 2 * f + 1):
                    for c in range(KC):
                        ins = mm(ps_t[:, f, (t % 2) * DIM:(t % 2 + 1) * DIM], onT[:, c, t * P:(t + 1) * P],
                                 w_proj[:, c, :], start=c == 0, stop=c == KC - 1)
                ins.then_inc(proj_done.sem, 1)

            def h2_transposes(b, c):
                if c == 0:
                    wait(pe, ln2, b, 4)
                wait(pe, h2_ready, b, c)
                for t in range(TILES):
                    ins = nc.tensor.transpose(ps_c[:, t * P:(t + 1) * P], xn[:, t, c * P:(c + 1) * P], idn[:])
                ins.then_inc(h2_tr.sem, 1)

            def logits(b):
                wait(pe, h2_ready, b, KC)
                for t in range(TILES):
                    for c in range(KC):
                        ins = mm(ps_t[:, 0, t * EXPERTS:(t + 1) * EXPERTS], h2T[:, c, t * P:(t + 1) * P],
                                 w_router[:, c, :], start=c == 0, stop=c == KC - 1)
                ins.then_inc(logits_done.sem, 1)

            def weight_transposes(b):
                wait(pe, router, b, ROUTER_STEPS)
                for t in range(TILES):
                    ins = nc.tensor.transpose(ps_t[0:2 * EXPERTS, 1, t * P:(t + 1) * P], cs[:, t, :], idn[:])
                ins.then_inc(c_tr.sem, 1)

            def down(b, t):
                if t == 0:
                    wait(pe, a_ready, b, EXPERTS)
                if t == 2:
                    wait(pe, y_ready, b, 1)
                at = (t % 2) * DIM
                for e in range(EXPERTS):
                    ins = mm(ps_o[:, at:at + DIM], act[:, e, t * P:(t + 1) * P], w_down[:, e, :],
                             start=e == 0, stop=e == EXPERTS - 1)
                if t % 2:
                    ins.then_inc(down_done.sem, 1)

            def tail(b, moe, more):
                n, m = b + 1, b - 1
                if more:
                    wait(pe, s_used, b, PAIRS * S_FILLS)
                    wait(pe, gt_done, m, EXPERTS)
                    wait(pe, gu_done, m, EXPERTS)
                    h1_transposes(n, False)
                wait(pe, exp_done, b, HEADS * T_FILLS)
                o_transposes(b, 0)
                o_transposes(b, 1)
                if more:
                    qkv(n, 0)
                o_transposes(b, 2)
                o_transposes(b, 3)
                wait(pe, a_ready, m, EXPERTS)
                if moe:
                    down(m, 0)
                on_transposes(b, 0)
                if more:
                    stack(n, 0)
                    qkv(n, 1)
                on_transposes(b, 1)
                project(b, 0)
                if moe:
                    down(m, 1)
                project(b, 1)
                if more:
                    stack(n, 1)
                    qkv(n, 2)
                if moe:
                    down(m, 2)
                h2_transposes(b, 0)
                if more:
                    stack(n, 2)
                    qkv(n, 3)
                h2_transposes(b, 1)
                logits(b)
                if moe:
                    down(m, 3)
                if more:
                    stack(n, 3)
                weight_transposes(b)

            pe.wait_ge(mod_in.sem, 48)
            pe.wait_ge(setup_v.sem, 3)
            scT = c_s.rearrange("p (c b) -> p c b", c=KC)
            for i, (a, col) in enumerate([(1, 0), (1, 1), (0, 0), (0, 1), (4, 0), (4, 1), (3, 0), (3, 1)]):
                for c in range(KC):
                    ins = mm(ps_c[:, i * BATCH:(i + 1) * BATCH], w_mod[:, c, a * DIM + col * P:a * DIM + (col + 1) * P],
                             scT[:, c, :], start=c == 0, stop=c == KC - 1)
            ins.then_inc(setup_t.sem, 1)
            for i, a in enumerate((2, 5)):
                for c in range(KC):
                    ins = mm(ps_o[0:BATCH, i * DIM:(i + 1) * DIM], scT[:, c, :], w_mod[:, c, a * DIM:(a + 1) * DIM],
                             start=c == 0, stop=c == KC - 1)
            ins.then_inc(setup_t.sem, 1)
            pe.wait_ge(consts_in.sem, 96)
            pe.wait_ge(weights_in.sem, 48)
            h1_transposes(0, True)
            for t in range(TILES):
                qkv(0, t)
                stack(0, t)
            pe.wait_ge(experts_in.sem, 32)
            pe.wait_ge(setup_v.sem, 14)

            def batch(b, moe, more):
                attention(b, moe)
                tail(b, moe, more)

            every_batch(pe, lambda b: batch(b, False, True), lambda b: batch(b, True, True),
                        lambda b: batch(b, True, False))
            for e in range(EXPERTS):
                gate(LAST, e)
                up(LAST, e)
                weight(LAST, e)
            for t in range(TILES):
                down(LAST, t)

        @block.scalar
        def _(ac):
            def copy(dst, src):
                return nc.scalar.activation(dst, src, ACT.Copy)

            def exps(b, h, k):
                f = h * T_FILLS + k
                wait(ac, t_filled, b, f + 1)
                if k == 0:
                    wait(ac, pv_done, b, h - 1)
                    if h < 2:
                        wait(ac, stored, b - 2, 32)
                at, n = ((0, SEQ), (SEQ, SEQ), (2 * SEQ, 2 * P))[k]
                nc.scalar.activation(probs[:, h % 2, at:at + n], ps_t[:, f % 2, 0:n], ACT.Exp, scale=SCALE)\
                    .then_inc(exp_done.sem, 1)

            def tanh(b, e):
                wait(ac, g_done, b, e + 1)
                if e >= 1:
                    wait(ac, gt_done, b, e)
                nc.scalar.activation(work[:, 0, :], ps_g[:], ACT.Tanh, scale=0.5).then_inc(tanh_done.sem, 1)

            def o_out(b, g):
                wait(ac, pv_done, b, OG * (g + 1))
                wait(ac, o_tr, b - 1, TILES)
                copy(OT[:, g, :], ps_o[:]).then_inc(ot_ready.sem, 1)

            def attention(b, moe):
                m = b - 1
                for p in range(PAIRS):
                    exps(b, 2 * p, 0)
                    if moe:
                        tanh(m, 2 * p)
                    exps(b, 2 * p, 1)
                    exps(b, 2 * p, 2)
                    if p and (2 * p - 1) % OG == OG - 1:
                        o_out(b, (2 * p - 1) // OG)
                    exps(b, 2 * p + 1, 0)
                    if moe:
                        tanh(m, 2 * p + 1)
                    exps(b, 2 * p + 1, 1)
                    exps(b, 2 * p + 1, 2)
                o_out(b, HEADS // OG - 1)

            def h1_out(b):
                wait(ac, mod_a, b, 1)
                wait(ac, qkv_done, b - 1, TILES)
                for c in range(KC):
                    wait(ac, h1_tr, b, c + 1)
                    nc.scalar.activation(h1T[:, c, :], (ps_g, ps_u)[c][:], ACT.Identity,
                                         scale=modA[:, c:c + 1], bias=modA[:, 2 + c:3 + c]).then_inc(h1_ready.sem, 1)

            def v_out(b, t):
                wait(ac, qkv_done, b, t + 1)
                wait(ac, pv_done, b - 1, HEADS)
                copy(V[:, t, :, 0:HD], ps_s[:, 1, (t % 2) * DIM:(t % 2 + 1) * DIM].rearrange("p (h d) -> p h d", d=HD))\
                    .then_inc(v_ready.sem, 1)

            def round_qk(b, t):
                wait(ac, rope_sum, b, t + 1)
                wait(ac, stack_tr, b, 4 * t)
                src = work[:, 1 + t % 2, :].rearrange("p (s h d) -> p s h d", s=2, d=HD)
                for i, (dst, step) in enumerate(((QS, 2), (KS, 1))):
                    view = dst[:, :, 0:MROW].rearrange("p h (s d) -> p s h d", d=HD)[:, 0:step + 1:step]
                    nc.scalar.activation(view.bitcast(F32R), src[:, i:i + 1].broadcast_to([P, 2, HEADS, HD]), ACT.Copy)\
                        .then_inc(rounded.sem, 1)

            def stack_out(b, t):
                for k in range(4):
                    f = 4 * t + k
                    wait(ac, stack_tr, b, f + 1)
                    if t == 0 and k == 0:
                        wait(ac, t_filled, b - 1, HEADS * T_FILLS)
                    dst = (QT, KT)[k // 2][:, 4 * (k % 2):4 * (k % 2) + 4, t * P:(t + 1) * P]
                    copy(dst, (ps_g, ps_u)[f % 2][:].rearrange("p (j n) -> p j n", j=4)).then_inc(stack_ready.sem, 1)

            def on_out(b, f):
                wait(ac, on_tr, b, f + 1)
                src = ps_c[:].rearrange("p (t c n) -> p c t n", t=2, c=KC)
                dst = onT[:, :, 2 * f * P:(2 * f + 2) * P].rearrange("p c (t n) -> p c t n", t=2)
                copy(dst, src).then_inc(on_ready.sem, 1)

            def h2_out(b, c):
                if c == 0:
                    wait(ac, mod_b, b, 1)
                    wait(ac, u_done, b - 1, EXPERTS)
                wait(ac, h2_tr, b, c + 1)
                nc.scalar.activation(h2T[:, c, :], ps_c[:], ACT.Identity,
                                     scale=modB[:, c:c + 1], bias=modB[:, 2 + c:3 + c]).then_inc(h2_ready.sem, 1)

            def tail(b, moe, more):
                n = b + 1
                if more:
                    h1_out(n)
                    v_out(n, 0)
                    round_qk(n, 0)
                on_out(b, 0)
                if more:
                    stack_out(n, 0)
                    v_out(n, 1)
                    round_qk(n, 1)
                on_out(b, 1)
                if more:
                    stack_out(n, 1)
                    v_out(n, 2)
                    round_qk(n, 2)
                h2_out(b, 0)
                if more:
                    stack_out(n, 2)
                    v_out(n, 3)
                    round_qk(n, 3)
                h2_out(b, 1)
                wait(ac, logits_done, b, 1)
                nc.scalar.activation(R[:, 0, :], ps_t[:, 0, 0:TILES * EXPERTS], ACT.Exp, scale=-1.0)\
                    .then_inc(rexp_done.sem, 1)
                if more:
                    stack_out(n, 3)
                wait(ac, c_tr, b, 1)
                wait(ac, c_done, b - 1, EXPERTS)
                copy(cT[:], ps_t[0:2 * EXPERTS, 1, :]).then_inc(ct_ready.sem, 1)

            ac.wait_ge(mod_in.sem, 48)
            nc.scalar.activation(c_e, c_sb, ACT.Exp, scale=-1.0).then_inc(setup_a.sem, 1)
            ac.wait_ge(setup_p.sem, 5)
            h1_out(0)
            for t in range(TILES):
                v_out(0, t)
                round_qk(0, t)
                stack_out(0, t)

            def batch(b, moe, more):
                attention(b, moe)
                tail(b, moe, more)

            every_batch(ac, lambda b: batch(b, False, True), lambda b: batch(b, True, True),
                        lambda b: batch(b, True, False))
            for e in range(EXPERTS):
                tanh(LAST, e)

        @block.vector
        def _(ve):
            tt, ts, stt = nc.vector.tensor_tensor, nc.vector.tensor_scalar, nc.vector.scalar_tensor_tensor

            def row_max(b, p, k):
                f = p * S_FILLS + k
                wait_apart(ve, s_filled, b, f + 1, ve_passed)
                h = 2 * p + k // 3
                for qt, at in (((3, 0),), ((2, 0),), ((0, 0), (1, 2 * P)))[k % 3]:
                    n = (qt + 1) * P
                    ins = nc.vector.tensor_tensor_reduce(
                        out=ps_s[:, f % 2, at:at + n], in0=ps_s[:, f % 2, at:at + n], in1=mask[:, SEQ - n:SEQ], scale=1.0,
                        scalar=-3.0e38, op0=ALU.add, op1=ALU.max, accum_out=mmax[:, h, qt:qt + 1])
                ins.then_inc(s_used.sem, 1)

            def maxima(b, p):
                wait(ve, s_used, b, p * S_FILLS + 6)
                wait(ve, s_filled, b, p * S_FILLS)
                src = mmax[:, 2 * p:2 * p + 2, :]
                dst = mt[:, :, :].rearrange("p t (h r) -> p h t r", h=2)
                high, low = dst[:, :, :, MROW:MROW + 1], dst[:, :, :, MROW + 1:MROW + 2]
                src = src.unsqueeze(3)
                ts(high.bitcast(F32R), src, -1.0, None, ALU.mult).then_inc(m_high.sem, 1)
                wait(ve, m_high, b, p + 1)
                stt(out=low.bitcast(F32R).rearrange("p h t o -> p h (t o)"), in0=src.rearrange("p h t o -> p h (t o)"),
                    scalar=-1.0, in1=high.rearrange("p h t o -> p h (t o)"), op0=ALU.mult, op1=ALU.subtract)\
                    .then_inc(m_ready.sem, 1)

            def maxima_in(b, p):
                f = p * S_FILLS + S_FILLS - 1
                wait(ve, s_filled, b, f + 1)
                tt(QT[:, p, :], ps_s[:, f % 2, :], QT[:, p, :].bitcast(F32), ALU.add).then_inc(s_used.sem, 1)

            def gate_tanh(b, e):
                wait(ve, tanh_done, b, e + 1)
                if e:
                    wait(ve, gu_done, b, e)
                stt(out=work[:, 1, :], in0=work[:, 0, :], scalar=1.0, in1=ps_g[:], op0=ALU.add, op1=ALU.mult)\
                    .then_inc(gt_done.sem, 1)

            def gate_up(b, e):
                wait(ve, u_done, b, e + 1)
                wait(ve, gt_done, b, e + 1)
                if e:
                    wait(ve, a_ready, b, e)
                tt(work[:, 2, :], work[:, 1, :], ps_u[:], ALU.mult).then_inc(gu_done.sem, 1)

            def weigh(b, e):
                wait(ve, c_done, b, e + 1)
                wait(ve, gu_done, b, e + 1)
                if e == 0:
                    wait(ve, down_done, b - 1, 2)
                tt(act[:, e, :], work[:, 2, :], ps_c[:], ALU.mult).then_inc(a_ready.sem, 1)

            def norm(b, src, sig, rs, first):
                if first:
                    for t in range(TILES):
                        ins = nc.vector.bn_stats(stats[:, t, :], src[:, t, :])
                    ins.then_inc(sig.sem, 1)
                    wait_apart(ve, sig, b, 1, ve_passed)
                    for t in range(TILES):
                        ins = nc.vector.bn_aggr(mv[:, t, :], stats[:, t, :])
                    ins.then_inc(sig.sem, 1)
                    wait(ve, sig, b, 2)
                    ts(vare[:], mv[:, :, 1], EPS, None, ALU.add).then_inc(sig.sem, 1)
                else:
                    wait(ve, rs, b, 1)
                    for t in range(TILES):
                        ins = ts(xn[:, t, :], src[:, t, :], mv[:, t, 0:1], rstd[:, t:t + 1], ALU.subtract, ALU.mult)
                    ins.then_inc(sig.sem, 1)

            def norm1(b, first):
                if first:
                    wait(ve, x_loaded, b, 16)
                    wait(ve, rstd2, b - 2, 1)
                elif not isinstance(b, int) or b > 1:
                    wait(ve, h2_tr, b - 2, KC)
                norm(b, x_in, ln1, rstd1, first)

            def attention(b, moe, more):
                m = b - 1
                def reds(*ks):
                    if p + 1 < PAIRS:
                        for k in ks:
                            row_max(b, p + 1, k)
                if moe:
                    wait(ve, h2_ready, b - 1, KC)
                for k in range(S_FILLS - 1):
                    row_max(b, 0, k)
                maxima(b, 0)
                maxima_in(b, 0)
                for p in range(PAIRS):
                    e = 2 * p
                    reds(0, 1)
                    if moe:
                        gate_tanh(m, e)
                    reds(2, 3)
                    if moe:
                        gate_up(m, e)
                    reds(4)
                    if moe:
                        weigh(m, e)
                    reds(5)
                    if p + 1 < PAIRS:
                        maxima(b, p + 1)
                    if moe:
                        gate_tanh(m, e + 1)
                    if moe:
                        gate_up(m, e + 1)
                    if p + 1 < PAIRS:
                        maxima_in(b, p + 1)
                    if moe:
                        weigh(m, e + 1)
                    if more and p == 2:
                        norm1(b + 1, True)
                    if more and p == 4:
                        norm1(b + 1, False)
                    if more and p == 5:
                        wait(ve, h1_ready, b, KC)
                        nc.vector.tensor_copy(modA[:], mods_of(b + 1, 0)).then_inc(mod_a.sem, 1)
                    if p == 5:
                        wait(ve, h2_ready, b - 1, KC)
                        nc.vector.tensor_copy(modB[:], mods_of(b, 4)).then_inc(mod_b.sem, 1)

            def mods_of(b, lo):
                if isinstance(b, int):
                    return mods[:, b, lo:lo + 4]
                return mods[:, bass.ds(b, 1), lo:lo + 4].rearrange("p o n -> p (o n)")

            def o_token(b, t):
                wait(ve, o_tr, b, t + 1)
                if t >= 2:
                    wait(ve, on_tr, b, t // 2)
                elif True:
                    wait(ve, on_tr, b - 1, 2)
                src = ps_t[:, t % 2, :].rearrange("p (h r) -> p h r", r=32)
                nc.vector.reciprocal(lin[:, t % 2, :].unsqueeze(2), src[:, :, HD:HD + 1]).then_inc(linv.sem, 1)
                wait(ve, linv, b, t + 1)
                tt(o_tok[:, t % 2, :].rearrange("p (h d) -> p h d", d=HD), src[:, :, 0:HD],
                   lin[:, t % 2, :].unsqueeze(2).broadcast_to([P, HEADS, HD]), ALU.mult).then_inc(o_tok_ready.sem, 1)

            def rope(b, t):
                wait(ve, qkv_done, b, t + 1)
                if t >= 2:
                    wait(ve, low_ready, b, t - 1)
                    wait(ve, rounded, b, 2 * (t - 1))
                wait(ve, rope_sum, b, t)
                src = ps_s[:, 0, :].rearrange("p (h s d) -> p h s d", s=2, d=HD // 2)
                a = work[:, 1 + t % 2, :].rearrange("p (h s d) -> p h s d", s=2, d=HD // 2)
                c = work[:, 3, :].rearrange("p (h s d) -> p h s d", s=2, d=HD // 2)
                full = [P, 2 * HEADS, 2, HD // 2]
                tt(work[:, 1 + t % 2, :].rearrange("p (g d) -> p g d", d=HD // 2),
                   ps_s[:, 0, :].rearrange("p (g d) -> p g d", d=HD // 2),
                   cos_t[:, t:t + 1, :].broadcast_to([P, 4 * HEADS, HD // 2]), ALU.mult)
                tt(c, src[:, :, ::-1, :], sin_t[:, t:t + 1, :, :].broadcast_to(full), ALU.mult).then_inc(roped.sem, 1)

            def low_qk(b, t):
                wait(ve, rounded, b, 2 * t + 2)
                src = work[:, 1 + t % 2, :].rearrange("p (s h d) -> p s h d", s=2, d=HD)
                tt(QS[:, :, HD:2 * HD].bitcast(F32R), src[:, 0], QS[:, :, 0:HD], ALU.subtract)
                tt(KS[:, :, 2 * HD:3 * HD].bitcast(F32R), src[:, 1], KS[:, :, 0:HD], ALU.subtract)\
                    .then_inc(low_ready.sem, 1)

            def residual(b, f):
                view = x1[:, 2 * f:2 * f + 2, :]
                if f == 0:
                    wait(ve, xres_loaded, b, 16)
                    wait(ve, gates_loaded, b, 32)
                t1 = work[:, 0, :].rearrange("p (t d) -> p t d", t=2)
                tt(view, view, gates[:, 1:2, :].broadcast_to([P, 2, DIM]), ALU.add).then_inc(xg_add.sem, 1)
                wait(ve, proj_done, b, f + 1)
                wait(ve, x1_ready, b, f)
                tt(t1, ps_t[:, f, :].rearrange("p (t d) -> p t d", t=2), gates[:, 0:1, :].broadcast_to([P, 2, DIM]),
                   ALU.mult).then_inc(ga_mul.sem, 1)
                wait(ve, ga_mul, b, f + 1)
                wait(ve, xg_add, b, f + 1)
                tt(view, view, t1, ALU.add).then_inc(x1_ready.sem, 1)

            def moe_scaled(b, f):
                wait(ve, down_done, b, f + 1)
                if f == 0:
                    wait(ve, gateb_loaded, b, 16)
                wait(ve, out_ready, b, f)
                tt(y_sb.rearrange("p (t d) -> p t d", t=2), ps_o[:].rearrange("p (t d) -> p t d", t=2),
                   gate_b[:, :].unsqueeze(1).broadcast_to([P, 2, DIM]), ALU.mult).then_inc(y_ready.sem, 1)

            def route(b):
                k = [0]

                def step(ins, then=wait):
                    k[0] += 1
                    ins.then_inc(router.sem, 1)
                    then(ve, router, b, k[0])

                G = GROUPS
                r = [R[:, i, :] for i in range(16)]
                te = lambda i: R[:, i, :].rearrange("p (t e) -> p t e", t=TILES)
                wait(ve, rexp_done, b, 1)
                step(ts(r[1], r[0], 1.0, None, ALU.add))
                step(nc.vector.reciprocal(r[2], r[1]))
                step(tt(te(3), te(2), rb[:, :].unsqueeze(1).broadcast_to([P, TILES, EXPERTS]), ALU.add))
                four = r[3].rearrange("p (g a c) -> p g a c", a=2, c=2)
                hi = r[4][:, 0:32].rearrange("p (g c) -> p g c", c=2)
                lo = r[5][:, 0:32].rearrange("p (g c) -> p g c", c=2)
                nc.vector.tensor_tensor(hi, four[:, :, 0, :], four[:, :, 1, :], ALU.max)
                step(tt(lo, four[:, :, 0, :], four[:, :, 1, :], ALU.min))
                one, two, three = (r[6][:, 16 * i:16 * i + 16].unsqueeze(2) for i in range(3))
                tt(one, hi[:, :, 0:1], hi[:, :, 1:2], ALU.max)
                tt(two, hi[:, :, 0:1], hi[:, :, 1:2], ALU.min)
                step(tt(three, lo[:, :, 0:1], lo[:, :, 1:2], ALU.max))
                second = r[7][:, 0:16].unsqueeze(2)
                step(tt(second, two, three, ALU.max))
                gs = r[7][:, 16:32]
                step(tt(gs.unsqueeze(2), one, second, ALU.add))
                gt_ = gs.rearrange("p (t g) -> p t g", t=TILES)
                other = gt_.unsqueeze(2).broadcast_to([P, TILES, G, G])
                own = gt_.unsqueeze(3).broadcast_to([P, TILES, G, G])
                c4 = lambda i: R[:, i, :].rearrange("p (t g o) -> p t g o", t=TILES, g=G)
                tt(c4(8), other, own, ALU.is_gt)
                step(tt(c4(9), other, own, ALU.is_equal))
                step(tt(c4(10), c4(9), before[:, :].rearrange("p (t g o) -> p t g o", t=TILES, g=G), ALU.mult))
                step(tt(r[11], r[8], r[10], ALU.add))
                rank = r[12][:, 0:16]
                step(nc.vector.reduce_sum(rank.unsqueeze(2), r[11].rearrange("p (x o) -> p x o", o=G), AX_X))
                chosen = r[12][:, 16:32]
                step(ts(chosen, rank, float(TOP_GROUPS), None, ALU.is_lt))
                four4 = lambda a: a.unsqueeze(2).broadcast_to([P, 16, G])
                pen = r[12][:, 32:48]
                ts(pen, chosen, -1.0, -NEG, ALU.add, ALU.mult)
                step(tt(r[4].rearrange("p (x o) -> p x o", o=G), r[3].rearrange("p (x o) -> p x o", o=G), four4(chosen), ALU.mult))
                step(tt(r[5].rearrange("p (x o) -> p x o", o=G), r[4].rearrange("p (x o) -> p x o", o=G), four4(pen), ALU.add), lambda *a: wait_apart(*a, ve_passed))
                for t in range(TILES):
                    ins = nc.vector.max(m8[:, t, :], r[5][:, t * EXPERTS:(t + 1) * EXPERTS])
                step(ins)
                th = m8[:, :, TOP_K - 1:TOP_K].broadcast_to([P, TILES, EXPERTS])
                body = lambda i: pfx[:, i, :, 8:8 + EXPERTS]
                tt(te(6), te(5), th, ALU.is_gt)
                step(tt(body(0), te(5), th, ALU.is_equal))
                step(nc.vector.reduce_sum(r[13][:, 0:TILES].unsqueeze(2), te(6), AX_X))
                step(nc.vector.tensor_copy(te(8), body(0)))
                for i, s in enumerate((1, 2, 4, 8)):
                    step(tt(body((i + 1) % 2), body(i % 2), pfx[:, i % 2, :, 8 - s:8 - s + EXPERTS], ALU.add))
                step(tt(te(9), body(0), r[13][:, 0:TILES].unsqueeze(2).broadcast_to([P, TILES, EXPERTS]), ALU.add))
                step(stt(out=r[10], in0=r[9], scalar=float(TOP_K), in1=r[8], op0=ALU.is_le, op1=ALU.mult))
                step(tt(r[11], r[10], r[6], ALU.add))
                step(tt(r[14], r[11], r[2], ALU.mult))
                step(nc.vector.reduce_sum(r[13][:, 4:8].unsqueeze(2), te(14), AX_X))
                step(ts(r[13][:, 8:12], r[13][:, 4:8], 1e-20, None, ALU.add))
                step(nc.vector.reciprocal(r[13][:, 12:16], r[13][:, 8:12]))
                step(ts(r[13][:, 16:20], r[13][:, 12:16], ROUTED_SCALE / 2, None, ALU.mult))
                step(tt(te(15), te(14), r[13][:, 16:20].unsqueeze(2).broadcast_to([P, TILES, EXPERTS]), ALU.mult))
                step(nc.vector.tensor_copy(cs[:, :, 0:EXPERTS].bitcast(F32R), te(15)))
                step(tt(cs[:, :, EXPERTS:2 * EXPERTS].bitcast(F32R), te(15), cs[:, :, 0:EXPERTS], ALU.subtract))
                while k[0] < ROUTER_STEPS:
                    step(nc.vector.tensor_copy(r[13][:, 20:21], r[13][:, 16:17]))
                assert k[0] == ROUTER_STEPS, k[0]

            def tail(b, moe, more):
                n, m = b + 1, b - 1
                if True:
                    wait(ve, a_ready, m, EXPERTS)
                o_token(b, 0)
                o_token(b, 1)
                if more:
                    rope(n, 0)
                    low_qk(n, 0)
                o_token(b, 2)
                o_token(b, 3)
                if more:
                    rope(n, 1)
                    low_qk(n, 1) if False else None
                residual(b, 0)
                if moe:
                    moe_scaled(m, 0)
                residual(b, 1)
                if more:
                    low_qk(n, 1)
                wait(ve, x1_ready, b, 2)
                norm(b, x1, ln2, rstd2, True)
                if more:
                    rope(n, 2)
                norm(b, x1, ln2, rstd2, False)
                if more:
                    low_qk(n, 2)
                    rope(n, 3)
                    low_qk(n, 3)
                route(b)
                if moe:
                    moe_scaled(m, 1)

            ve.wait_ge(setup_a.sem, 1)
            ts(c_d, c_e, 1.0, None, ALU.add).then_inc(setup_v.sem, 1)
            ve.wait_ge(setup_v.sem, 1)
            nc.vector.reciprocal(c_r, c_d).then_inc(setup_v.sem, 1)
            ve.wait_ge(setup_v.sem, 2)
            tt(c_s, c_r, c_sb, ALU.mult).then_inc(setup_v.sem, 1)
            ve.wait_ge(setup_t.sem, 1)
            src = ps_c[:, 0:8 * BATCH].rearrange("p (i b) -> p b i", i=8)
            for i, add in enumerate((1.0, 0.0, 1.0, 0.0)):
                ins = ts(mods[:, :, 2 * i:2 * i + 2], src[:, :, 2 * i:2 * i + 2], add, None, ALU.add)
            ins.then_inc(setup_v.sem, 1)
            ve.wait_ge(setup_t.sem, 2)
            ts(g16, ps_o[0:BATCH, :], 0.0, 2.0, ALU.is_ge, ALU.mult).then_inc(setup_v.sem, 1)
            ve.wait_ge(setup_v.sem, 5)
            ts(g16, g16, -1.0, None, ALU.add).then_inc(setup_v.sem, 1)
            ts(sg16, ps_o[0:BATCH, :], -1.0, None, ALU.mult).then_inc(setup_v.sem, 1)
            ve.wait_ge(setup_v.sem, 7)
            stt(out=sg16, in0=sg16, scalar=0.25, in1=ps_o[0:BATCH, :], op0=ALU.max, op1=ALU.max).then_inc(setup_v.sem, 1)
            ve.wait_ge(setup_v.sem, 8)
            tt(gfin[:, 0:2, :].rearrange("p t n -> p (t n)"), g16, sg16, ALU.mult).then_inc(setup_v.sem, 1)
            ve.wait_ge(setup_v.sem, 9)
            tt(gfin[:, 2, :], gfin[:, 0, :], b16, ALU.mult).then_inc(setup_v.sem, 1)
            ve.wait_ge(consts_in.sem, 96)
            ve.wait_ge(setup_v.sem, 10)
            nc.vector.tensor_copy(pick_r[:], pick_f[:]).then_inc(setup_v.sem, 1)
            nc.vector.memset(pfx[:], 0.0).then_inc(setup_v.sem, 1)
            ve.wait_ge(setup_v.sem, 12)
            ve.wait_ge(setup_p.sem, 7)
            norm1(0, True)
            norm1(0, False)
            nc.vector.tensor_copy(modA[:], mods[:, 0, 0:4]).then_inc(mod_a.sem, 1)
            for t in range(TILES):
                rope(0, t)
                low_qk(0, t)
            ve.wait_ge(gates_out.sem, 16)
            nc.vector.memset(vare[:], 0.0).then_inc(setup_v.sem, 1)
            nc.vector.memset(mmax[:], 0.0).then_inc(setup_v.sem, 1)

            def batch(b, moe, more):
                attention(b, moe, more)
                tail(b, moe, more)

            every_batch(ve, lambda b: batch(b, False, True), lambda b: batch(b, True, True),
                        lambda b: batch(b, True, False))
            for e in range(EXPERTS):
                gate_tanh(LAST, e)
                gate_up(LAST, e)
                weigh(LAST, e)
            for f in range(2):
                moe_scaled(LAST, f)

        @block.gpsimd
        def _(po):
            def mask_probs(b, h):
                wait_apart(po, exp_done, b, T_FILLS * (h + 1), po_passed)
                three = probs[:, h % 2, :]
                a = bass.AP(three.tensor, three.offset, [three.ap[0], [SEQ, 3], [1, P]])
                po.affine_select(out=a, in_=a, compare_op=ALU.is_ge, fill=0.0, base=0,
                                 pattern=[[0, 3], [1, P]], channel_multiplier=-1).then_inc(masked.sem, 1)
                d = probs[:, h % 2, KT_AT[3]:KT_AT[3] + P]
                po.affine_select(out=d, in_=d, compare_op=ALU.is_ge, fill=0.0, base=0,
                                 pattern=[[1, P]], channel_multiplier=-1).then_inc(masked.sem, 1)

            def rope_add(b, t):
                wait(po, roped, b, t + 1)
                buf = work[:, 1 + t % 2, :]
                po.tensor_tensor(buf, buf, work[:, 3, :], ALU.add).then_inc(rope_sum.sem, 1)

            def inv_std(b, sig, rs):
                wait(po, sig, b, 3)
                po.tensor_tensor(rstd[:], vare[:], half[:], ALU.pow).then_inc(rs.sem, 1)

            def add_stream(b, f):
                wait(po, y_ready, b, f + 1)
                if f == 0:
                    wait(po, prev_copied, b, 16)
                po.tensor_tensor(out_sb[:, 2 * f:2 * f + 2, :], x1_prev[:, 2 * f:2 * f + 2, :],
                                 y_sb.rearrange("p (t d) -> p t d", t=2), ALU.add).then_inc(out_ready.sem, 1)

            def attention(b, more):
                for p in range(PAIRS):
                    mask_probs(b, 2 * p)
                    mask_probs(b, 2 * p + 1)
                    if more and p == 3:
                        inv_std(b + 1, ln1, rstd1)

            def tail(b, moe, more):
                n, m = b + 1, b - 1
                if more:
                    rope_add(n, 0)
                    rope_add(n, 1)
                if moe:
                    add_stream(m, 0)
                inv_std(b, ln2, rstd2)
                if more:
                    rope_add(n, 2)
                    rope_add(n, 3)
                if moe:
                    add_stream(m, 1)

            po.memset(QS[:], 0.0).then_inc(setup_p.sem, 1)
            po.memset(KS[:], 0.0).then_inc(setup_p.sem, 1)
            po.memset(V[:], 0.0).then_inc(setup_p.sem, 1)
            po.memset(mt[:], 0.0)
            po.memset(half[:], -0.5)
            po.wait_ge(setup_p.sem, 3)
            po.memset(KS[:, :, MROW:MROW + 2], 1.0).then_inc(setup_p.sem, 1)
            po.memset(V[:, :, :, HD:HD + 1], 1.0).then_inc(setup_p.sem, 1)
            po.memset(before[:], 1.0).then_inc(setup_p.sem, 1)
            po.wait_ge(setup_p.sem, 6)
            bv = before[:, :].rearrange("p (t g o) -> p t g o", t=TILES, g=GROUPS)
            po.affine_select(out=bv, in_=bv, compare_op=ALU.is_gt, fill=0.0, base=0,
                             pattern=[[0, TILES], [1, GROUPS], [-1, GROUPS]], channel_multiplier=0).then_inc(setup_p.sem, 1)
            inv_std(0, ln1, rstd1)
            for t in range(TILES):
                rope_add(0, t)

            def batch(b, moe, more):
                attention(b, more)
                tail(b, moe, more)

            every_batch(po, lambda b: batch(b, False, True), lambda b: batch(b, True, True),
                        lambda b: batch(b, True, False))
            for f in range(2):
                add_stream(LAST, f)


def kernel(L0_attn_x, L0_attn_w_qkv, L0_attn_w_proj, L0_attn_b_proj, L0_ffn_router_weight, L0_ffn_router_bias,
           L0_ffn_w_gate, L0_ffn_w_up, L0_ffn_w_down, L0_c, L0_wmod):
    import concourse.bacc as bacc
    from concourse.bass_utils import run_bass_kernel_spmd

    def rows(w):
        w = np.asarray(w)
        return w.reshape(KC, P, w.shape[1]).transpose(1, 0, 2)

    inv_freq = (np.float32(1.0) / np.float32(10000.0) ** (np.arange(0, HD, 2, dtype=np.float32) / np.float32(HD))).astype(np.float32)
    angle = (np.arange(SEQ, dtype=np.float32)[:, None] * inv_freq[None, :]).astype(np.float32)
    cos = np.cos(angle.astype(np.float64)).astype(np.float32).reshape(TILES, P, HD // 2).transpose(1, 0, 2)
    sin = np.sin(angle.astype(np.float64)).astype(np.float32).reshape(TILES, P, HD // 2).transpose(1, 0, 2)
    tril = np.zeros((P, SEQ), np.float32)
    tril[:, SEQ - P:] = np.where(np.arange(P)[None, :] > np.arange(P)[:, None], np.float32(NEG), np.float32(0))
    pick = np.concatenate([np.eye(EXPERTS, dtype=np.float32)] * 2, axis=0)
    gate = np.asarray(L0_ffn_w_gate).reshape(EXPERTS, INNER, KC, P).transpose(3, 0, 2, 1)
    up = np.asarray(L0_ffn_w_up).reshape(EXPERTS, INNER, KC, P).transpose(3, 0, 2, 1)
    arrays = {
        "x": np.asarray(L0_attn_x),
        "wqkv": rows(L0_attn_w_qkv),
        "wproj": rows(L0_attn_w_proj),
        "bproj": np.asarray(L0_attn_b_proj)[None, :],
        "rw": rows(np.asarray(L0_ffn_router_weight).T),
        "rbias": np.asarray(L0_ffn_router_bias)[None, :],
        "wgu": np.stack([gate, up], axis=2),
        "wd": np.asarray(L0_ffn_w_down).transpose(2, 0, 1),
        "ct": np.asarray(L0_c).T.reshape(KC, P, BATCH).transpose(1, 0, 2).reshape(P, KC * BATCH),
        "wmod": rows(L0_wmod),
        "cosq": cos,
        "sinq": np.stack([-sin, sin], axis=2),
        "tril_bias": tril,
        "ident": np.eye(P, dtype=np.float32),
        "pick": pick,
    }
    arrays = {n: np.ascontiguousarray(a) for n, a in arrays.items()}
    nc = bacc.Bacc("TRN2", target_bir_lowering=False, num_devices=1)
    args = {n: nc.dram_tensor(n, a.shape, mybir.dt.from_np(a.dtype), kind="ExternalInput").ap() for n, a in arrays.items()}
    y = nc.dram_tensor("y", (BATCH, SEQ, DIM), F32, kind="ExternalOutput").ap()
    build(nc, out=y, **args)
    r = run_bass_kernel_spmd(nc, [arrays], core_ids=[0])
    return r.results[0]["y"]
```

```python
from contextlib import ExitStack

import numpy as np

import concourse.bass as bass
from concourse import mybir

ALU = mybir.AluOpType
ACT = mybir.ActivationFunctionType
F32 = mybir.dt.float32
F32R = mybir.dt.float32r
BF16 = mybir.dt.bfloat16
AX_X = mybir.AxisListType.X

P = 128
BATCH, SEQ, DIM = 16, 512, 256
HEADS, HD = 16, 16
EXPERTS, INNER = 16, 128
GROUPS, TOP_GROUPS, TOP_K = 4, 2, 4
ROUTED_SCALE = 2.5
EPS = 1e-5
TILES = SEQ // P
KC = DIM // P
PAIRS = HEADS // 2
STRIP = 64
MROW = 48
OG = 4
SCALE = HD ** -0.5
NEG = -1e9

S_FILLS = 7
T_FILLS = 3
KT_AT = {0: 0, 1: SEQ, 3: SEQ + 3 * P, 2: 2 * SEQ}
PROBS = 2 * SEQ + 2 * P
ROUTER_AT = (0, 7, 15, 20, 25)
ROUTER_STEPS = ROUTER_AT[-1]
EXPERT_W = 2 * KC * INNER + DIM
PRODUCTS = ((0, 0), (0, 1), (1, 0))
HALF = SEQ // 2
UNITS = 2 * EXPERTS
IN_TAIL = 16


class Signal:

    def __init__(self, sem, per):
        self.sem, self.per = sem, per

    def at(self, b, k):
        return b * self.per + k


def wait(eng, signal, b, k):
    value = signal.at(b, k)
    if isinstance(value, int) and value <= 0:
        return
    eng.wait_ge(signal.sem, value)


def wait_apart(eng, signal, b, k, passed):
    wait(eng, signal, b, k)
    eng.sem_inc(passed.sem, 1)


def build(nc, x, wqkv, wproj, bproj, rw, rbias, wex, ct, wmod, cosq, sinq, tril_bias, ident, pick, out):
    with ExitStack() as ctx:
        def sb(name, shape, dt=F32):
            return ctx.enter_context(nc.sbuf_tensor(name, shape, dt))

        def ps(name, shape):
            return ctx.enter_context(nc.psum_tensor(name, shape, F32))

        def signal(name, per):
            return Signal(ctx.enter_context(nc.semaphore(name)), per)

        w_qkv = sb("w_qkv", [P, KC, 3 * DIM])
        w_proj = sb("w_proj", [P, KC, DIM])
        w_router = sb("w_router", [P, KC, EXPERTS])
        w_part = [sb(n, [P, EXPERTS, EXPERT_W], F32R) for n in ("w_high", "w_low")]
        cos_t = sb("cos_t", [P, TILES, HD // 2])
        sin_t = sb("sin_t", [P, TILES, 2, HD // 2])
        mask = sb("mask", [P, SEQ])
        idn = sb("idn", [P, P])
        pick_f = sb("pick_f", [2 * EXPERTS, EXPERTS])
        pick_r = sb("pick_r", [2 * EXPERTS, EXPERTS], F32R)
        rb = sb("rb", [P, EXPERTS])
        half = sb("half", [P, TILES])
        mods = sb("mods", [P, BATCH, 8])
        act = sb("act", [P, 2, HALF])
        a_part = [sb(n, [P, 2, HALF], F32R) for n in ("a_high", "a_low")]
        x_in = sb("x_in", [P, TILES, DIM])
        x1 = sb("x1", [P, TILES, DIM])
        x1_prev = sb("x1_prev", [P, TILES, DIM])
        h2_part = [sb(n, [P, KC, SEQ], F32R) for n in ("h2_high", "h2_low")]
        QT = sb("QT", [P, PAIRS, SEQ], F32R)
        KT = sb("KT", [P, PAIRS, SEQ], F32R)
        V = sb("V", [P, TILES, HEADS, HD + 1])
        probs = sb("probs", [P, 2, PROBS])
        OT = sb("OT", [P, HEADS // OG, SEQ])
        work = sb("work", [P, 2, SEQ])
        y_sb = sb("y_sb", [P, SEQ])
        o_tok = sb("o_tok", [P, TILES, DIM])
        gates = sb("gates", [P, 2, DIM])
        gate_b = sb("gate_b", [P, DIM])
        mmax = sb("mmax", [P, HEADS, TILES])
        mt = sb("mt", [P, TILES, P])
        cT = sb("cT", [2 * EXPERTS, SEQ], F32R)
        modA = sb("modA", [P, 4])
        modB = sb("modB", [P, 4])
        stats = sb("stats", [P, TILES, 6])
        mv = sb("mv", [P, TILES, 2])
        vare = sb("vare", [P, TILES])
        rstd = sb("rstd", [P, TILES])
        lin = sb("lin", [P, 2, HEADS])
        before = sb("before", [P, TILES * GROUPS * GROUPS])
        top4 = sb("top4", [P, TILES, 8])
        m8 = sb("m8", [P, TILES, 8])
        cs = sb("cs", [P, TILES, 2 * EXPERTS])
        stacks = OT[:, :, :].rearrange("p g n -> p (g n)").rearrange("p (s h r) -> p s h r", s=2, r=STRIP)
        QS, KS = stacks[:, 0], stacks[:, 1]
        flat = probs[:, :, :].rearrange("p a n -> p (a n)")
        h1T = flat[:, 0:KC * SEQ].rearrange("p (c n) -> p c n", c=KC)
        onT = flat[:, KC * SEQ:2 * KC * SEQ].rearrange("p (c n) -> p c n", c=KC)
        h2T = onT
        R = flat[:, 0:KC * SEQ].rearrange("p (i n) -> p i n", i=16)
        w_mod = [flat[:, 0:6 * DIM], OT[:, :, :].rearrange("p g n -> p (g n)")[:, 0:6 * DIM]]
        c_sb, c_e, c_d, c_r, c_s = (flat[:, 6 * DIM + i * 32:6 * DIM + i * 32 + 32] for i in range(5))
        gfin = flat[0:BATCH, 6 * DIM + 160:9 * DIM + 160].rearrange("p (t n) -> p t n", t=3)
        g16, sg16 = work[0:BATCH, 0, :], work[0:BATCH, 1, :]
        b16 = o_tok[0:BATCH, 0, :]
        stage = [t[:, :, :].rearrange("p t d -> p (t d)")[:, 0:EXPERT_W] for t in (x1, x1_prev)]

        ps_s = ps("ps_s", [P, 2, SEQ])
        ps_t = ps("ps_t", [P, 2, SEQ])
        ps_o = ps("ps_o", [P, SEQ])
        ps_g = ps("ps_g", [P, SEQ])
        ps_y = ps("ps_y", [P, SEQ])
        ps_u = ps("ps_u", [P, SEQ])
        gate_dram = nc.dram_tensor("gate_dram", (BATCH, 3, DIM), F32).ap()

        weights_in = signal("weights_in", 0)
        consts_in = signal("consts_in", 0)
        mod_in = signal("mod_in", 0)
        expert_in = [signal(f"expert_in{i}", 0) for i in range(2)]
        w_high_done = signal("w_high_done", 0)
        w_low_done = signal("w_low_done", 0)
        setup_v = signal("setup_v", 0)
        o_cleared = signal("o_cleared", 0)
        setup_p = signal("setup_p", 0)
        setup_a = signal("setup_a", 0)
        setup_t = signal("setup_t", 0)
        gates_out = signal("gates_out", 0)
        x_loaded = signal("x_loaded", 16)
        xres_loaded = signal("xres_loaded", 16)
        prev_copied = signal("prev_copied", 16)
        gates_loaded = signal("gates_loaded", 32)
        gateb_loaded = signal("gateb_loaded", 16)
        stored = signal("stored", 32)
        consts_set = signal("consts_set", 3)
        s_filled = signal("s_filled", PAIRS * S_FILLS)
        t_filled = signal("t_filled", HEADS * T_FILLS)
        pv_done = signal("pv_done", HEADS)
        g_done, u_done = (signal(n, UNITS) for n in ("g_done", "u_done"))
        d_done = signal("d_done", UNITS)
        h1_tr = signal("h1_tr", KC)
        o_tr = signal("o_tr", TILES)
        qkv_done = signal("qkv_done", TILES)
        on_tr = signal("on_tr", 2)
        proj_done = signal("proj_done", 2)
        h2_tr = signal("h2_tr", KC)
        logits_done = signal("logits_done", 1)
        c_tr = signal("c_tr", 1)
        stack_tr = signal("stack_tr", 4 * TILES)
        exp_done = signal("exp_done", HEADS * T_FILLS)
        ot_ready = signal("ot_ready", HEADS // OG)
        tanh_done = signal("tanh_done", UNITS)
        a_high_done = signal("a_high_done", UNITS)
        a_low_done = signal("a_low_done", UNITS)
        h2_high = signal("h2_high", KC)
        h2_low = signal("h2_low", KC)
        h1_ready = signal("h1_ready", KC)
        rounded = signal("rounded", 2 * TILES)
        v_ready = signal("v_ready", TILES)
        on_ready = signal("on_ready", 2)
        stack_ready = signal("stack_ready", 4 * TILES)
        h2_ready = signal("h2_ready", KC)
        rexp_done = signal("rexp_done", 1)
        ct_ready = signal("ct_ready", 1)
        s_used = signal("s_used", PAIRS * S_FILLS)
        m_high = signal("m_high", PAIRS)
        m_ready = signal("m_ready", PAIRS)
        gt_done, gw_done, a_ready = (signal(n, UNITS) for n in ("gt_done", "gw_done", "a_ready"))
        ln1 = signal("ln1", 4)
        ln2 = signal("ln2", 4)
        mod_a = signal("mod_a", 1)
        mod_b = signal("mod_b", 1)
        linv = signal("linv", TILES)
        o_tok_ready = signal("o_tok_ready", TILES)
        roped = signal("roped", TILES)
        low_ready = signal("low_ready", TILES)
        ga_mul = signal("ga_mul", 2)
        xg_add = signal("xg_add", 2)
        x1_ready = signal("x1_ready", 2)
        router = signal("router", ROUTER_STEPS)
        y_ready = signal("y_ready", 2)
        masked = signal("masked", 2 * HEADS)
        rope_sum = signal("rope_sum", TILES)
        rstd1 = signal("rstd1", 1)
        rstd2 = signal("rstd2", 1)
        out_ready = signal("out_ready", 2)

        ve_passed = signal("ve_passed", 0)
        po_passed = signal("po_passed", 0)

        LAST = BATCH - 1

        def every_batch(eng, first, middle, last):
            first(0)
            with eng.Fori(1, LAST) as b:
                middle(b)
            last(LAST)

        block = ctx.enter_context(nc.Block())

        def after_pair(p):
            return [2 * p, 2 * p + 1]

        assert [u for p in range(PAIRS) for u in after_pair(p)] == list(range(UNITS - IN_TAIL))

        @block.sync
        def _(sp):
            def dram_x(b):
                return x[b].rearrange("(t p) d -> p t d", p=P)

            def gate_rows(b, lo, hi):
                src = gate_dram[b, lo:hi, :]
                return bass.AP(src.tensor, src.offset, [[0, P], [DIM, hi - lo], [1, DIM]]) if isinstance(b, int) \
                    else gate_dram[bass.ds(b, 1), lo:hi, :].broadcast_to([P, hi - lo, DIM])

            sp.dma_start(x_in[:], dram_x(0)).then_inc(x_loaded.sem, 16)
            sp.dma_start(c_sb, ct).then_inc(mod_in.sem, 16)
            sp.dma_start(idn[:], ident).then_inc(consts_in.sem, 16)
            sp.dma_start(cos_t[:], cosq).then_inc(consts_in.sem, 16)
            sp.dma_start(sin_t[:], sinq).then_inc(consts_in.sem, 16)
            sp.dma_start(mask[:], tril_bias).then_inc(consts_in.sem, 16)
            sp.dma_start(pick_f[:], pick).then_inc(consts_in.sem, 16)
            sp.dma_start(rb[:], rbias.broadcast_to([P, EXPERTS])).then_inc(consts_in.sem, 16)
            for c in range(KC):
                sp.dma_start(w_mod[c], wmod[:, c, :]).then_inc(mod_in.sem, 16)
            sp.dma_start(b16, bproj.broadcast_to([BATCH, DIM])).then_inc(mod_in.sem, 16)
            sp.dma_start(w_qkv[:], wqkv).then_inc(weights_in.sem, 16)
            sp.dma_start(w_proj[:], wproj).then_inc(weights_in.sem, 16)
            sp.dma_start(w_router[:], rw).then_inc(weights_in.sem, 16)
            sp.wait_ge(setup_v.sem, 10)
            sp.dma_start(gate_dram, gfin).then_inc(gates_out.sem, 16)

            def experts_weights():
                for e in range(EXPERTS):
                    if e >= 2:
                        sp.wait_ge(w_low_done.sem, e - 1)
                    sp.dma_start(stage[e % 2], wex[:, e, :]).then_inc(expert_in[e % 2].sem, 16)
                sp.wait_ge(gates_out.sem, 16)
                sp.wait_ge(w_low_done.sem, EXPERTS)

            def set_aside(b):
                wait(sp, x1_ready, b, 2)
                wait(sp, ln2, b, 4)
                wait(sp, stored, b - 1, 32)
                sp.dma_start(x1_prev[:], x1[:]).then_inc(prev_copied.sem, 16)
                wait(sp, y_ready, b - 1, 2)
                sp.dma_start(gate_b[:], gate_rows(b, 1, 2).rearrange("p o d -> p (o d)")).then_inc(gateb_loaded.sem, 16)

            def store(b):
                dst = out[b].rearrange("(t p) d -> p t d", p=P)
                for f in range(2):
                    wait(sp, out_ready, b, f + 1)
                    sp.dma_start(dst[:, 2 * f:2 * f + 2, :], x1_prev[:, 2 * f:2 * f + 2, :]).then_inc(stored.sem, 16)

            def batch(b, moe, more):
                if more:
                    wait(sp, h1_tr, b, KC)
                    wait(sp, h2_tr, b - 1, KC)
                    sp.dma_start(x_in[:], dram_x(b + 1)).then_inc(x_loaded.sem, 16)
                if moe:
                    set_aside(b - 1)
                    wait(sp, prev_copied, b - 1, 16)
                else:
                    experts_weights()
                sp.dma_start(x1[:], dram_x(b)).then_inc(xres_loaded.sem, 16)
                wait(sp, x1_ready, b - 1, 2)
                sp.dma_start(gates[:, 0, :], gate_rows(b, 0, 1).rearrange("p o d -> p (o d)")).then_inc(gates_loaded.sem, 16)
                sp.dma_start(gates[:, 1, :], gate_rows(b, 2, 3).rearrange("p o d -> p (o d)")).then_inc(gates_loaded.sem, 16)
                if moe:
                    store(b - 1)

            every_batch(sp, lambda b: batch(b, False, True), lambda b: batch(b, True, True),
                        lambda b: batch(b, True, False))
            set_aside(LAST)
            store(LAST)
            sp.wait_ge(stored.sem, 32 * BATCH)

        @block.tensor
        def _(pe):
            mm = nc.tensor.matmul

            def fill_s(b, p, k):
                f = p * S_FILLS + k
                wait(pe, s_used, b, f - 1)
                bank = ps_s[:, f % 2, :]
                if k == S_FILLS - 1:
                    wait(pe, m_ready, b, p + 1)
                    for t in range(TILES):
                        ins = nc.tensor.transpose(bank[:, t * P:(t + 1) * P], mt[:, t, :], idn[:])
                else:
                    r0 = STRIP * (k // 3)
                    for qt, at, n in (((3, 0, SEQ),), ((2, 0, 3 * P),), ((0, 0, 2 * P), (1, 2 * P, 2 * P)))[k % 3]:
                        ins = mm(bank[:, at:at + n], QT[r0:r0 + MROW, p, qt * P:(qt + 1) * P],
                                 KT[r0:r0 + MROW, p, 0:n], start=True, stop=True)
                ins.then_inc(s_filled.sem, 1)

            def fill_t(b, h, k):
                f = h * T_FILLS + k
                if k == 0 and h % 2 == 0:
                    wait(pe, s_used, b, (h // 2 + 1) * S_FILLS)
                wait(pe, exp_done, b, f - 1)
                if f < 2:
                    wait(pe, ct_ready, b - 1, 1)
                bank = ps_t[:, f % 2, :]
                r0, p = STRIP * (h % 2), h // 2
                for kt, at, q0 in (((0, 0, 0),), ((3, 2 * P, 2 * P), (1, 0, P)), ((2, 0, 2 * P),))[k]:
                    ins = mm(bank[:, at:at + SEQ - q0], KT[r0:r0 + STRIP, p, kt * P:(kt + 1) * P],
                             QT[r0:r0 + STRIP, p, q0:SEQ], start=True, stop=True)
                ins.then_inc(t_filled.sem, 1)

            def values(b, h):
                wait(pe, masked, b, 2 * h + 2)
                wait(pe, exp_done, b, T_FILLS * (h + 1))
                if h == 0:
                    wait(pe, v_ready, b, TILES)
                if h % OG == 0:
                    wait(pe, ot_ready, b, h // OG)
                r0 = 32 * (h % OG)
                for kt in range(TILES):
                    n = SEQ - kt * P
                    ins = mm(ps_o[r0:r0 + HD + 1, kt * P:SEQ], V[:, kt, h, :], probs[:, h % 2, KT_AT[kt]:KT_AT[kt] + n],
                             start=kt == 0, stop=kt == TILES - 1)
                ins.then_inc(pv_done.sem, 1)

            def gate_or_up(b, u, which):
                e, t0 = u % EXPERTS, HALF * (u // EXPERTS)
                n = 0
                for c in range(KC):
                    w0 = (KC * which + c) * INNER
                    for a, x_ in PRODUCTS:
                        n += 1
                        ins = mm((ps_g, ps_u)[which][:, 0:HALF], w_part[a][:, e, w0:w0 + INNER],
                                 h2_part[x_][:, c, t0:t0 + HALF], start=n == 1, stop=n == KC * len(PRODUCTS))
                ins.then_inc((g_done, u_done)[which].sem, 1)

            def gate(b, u):
                if u == 0:
                    wait(pe, h2_low, b, KC)
                wait(pe, gw_done, b, u)
                weight(b, u)
                gate_or_up(b, u, 0)

            def up(b, u):
                wait(pe, a_ready, b, u)
                gate_or_up(b, u, 1)

            def weight(b, u):
                if u == 0:
                    wait(pe, ct_ready, b, 1)
                t0 = HALF * (u // EXPERTS)
                mm(ps_g[:, HALF:SEQ], pick_r[:, u % EXPERTS:u % EXPERTS + 1].broadcast_to([2 * EXPERTS, P]),
                   cT[:, t0:t0 + HALF], start=True, stop=True)

            def down(b, u):
                e = u % EXPERTS
                wait(pe, a_low_done, b, u + 1)
                if e == 0:
                    if u:
                        wait(pe, y_ready, b, 1)
                    else:
                        wait(pe, y_ready, b - 1, 2)
                for t in range(2):
                    for n, (a, w) in enumerate(PRODUCTS):
                        ins = mm(ps_y[:, t * DIM:(t + 1) * DIM], a_part[a][:, u % 2, t * P:(t + 1) * P],
                                 w_part[w][:, e, 2 * KC * INNER:EXPERT_W], start=e == 0 and t == 0 and n == 0,
                                 stop=e == EXPERTS - 1 and n == len(PRODUCTS) - 1, skip_group_check=True)
                ins.then_inc(d_done.sem, 1)

            def unit(b, u):
                gate(b, u)
                up(b, u)
                if u:
                    down(b, u - 1)

            def attention(b, moe):
                m = b - 1
                for p in range(PAIRS):
                    h0, h1, more = 2 * p, 2 * p + 1, p + 1 < PAIRS
                    u = after_pair(p)
                    if p == 0:
                        fill_s(b, 1, 0)
                    fill_t(b, h0, 0)
                    if more:
                        fill_s(b, p + 1, 1)
                    if moe:
                        gate(m, u[0])
                    fill_t(b, h0, 1)
                    if more:
                        fill_s(b, p + 1, 2)
                    if moe:
                        up(m, u[0])
                    fill_t(b, h0, 2)
                    if more:
                        fill_s(b, p + 1, 3)
                    if p:
                        values(b, h0 - 1)
                    if more:
                        fill_s(b, p + 1, 4)
                    if moe and u[0]:
                        down(m, u[0] - 1)
                    if more:
                        fill_s(b, p + 1, 5)
                    fill_t(b, h1, 0)
                    if moe:
                        gate(m, u[1])
                    fill_t(b, h1, 1)
                    if moe:
                        up(m, u[1])
                    if more:
                        fill_s(b, p + 1, 6)
                    fill_t(b, h1, 2)
                    if p + 2 < PAIRS:
                        fill_s(b, p + 2, 0)
                    values(b, h0)
                    if moe:
                        down(m, u[1] - 1)
                values(b, HEADS - 1)

            def h1_transposes(b):
                wait(pe, ln1, b, 4)
                for c in range(KC):
                    bank = ps_s[:, c, :]
                    for t in range(TILES):
                        ins = nc.tensor.transpose(bank[:, t * P:(t + 1) * P], x_in[:, t, c * P:(c + 1) * P], idn[:])
                    ins.then_inc(h1_tr.sem, 1)

            def qkv(b, t):
                if t == 0:
                    wait(pe, h1_ready, b, KC)
                wait(pe, roped, b, t)
                wait(pe, v_ready, b, t)
                hT = [h1T[:, c, t * P:(t + 1) * P] for c in range(KC)]
                for c in range(KC):
                    mm(ps_s[:, 0, :], hT[c], w_qkv[:, c, 0:2 * DIM], start=c == 0, stop=c == KC - 1)
                at = (t % 2) * DIM
                for c in range(KC):
                    ins = mm(ps_s[:, 1, at:at + DIM], hT[c], w_qkv[:, c, 2 * DIM:3 * DIM], start=c == 0, stop=c == KC - 1)
                ins.then_inc(qkv_done.sem, 1)

            def stack(b, t, half_):
                wait(pe, rounded, b, 2 * t + 2)
                wait(pe, low_ready, b, t + 1)
                if t == 0:
                    wait(pe, consts_set, b, 3)
                    wait(pe, o_tok_ready, b - 1, TILES)
                for k in (2 * half_, 2 * half_ + 1):
                    f = 4 * t + k
                    if f >= 2:
                        wait(pe, stack_ready, b, f - 1)
                    bank, src = ps_t[:, f % 2, :], (QS, KS)[k // 2]
                    for j in range(4):
                        p = 4 * (k % 2) + j
                        ins = nc.tensor.transpose(
                            bank[:, j * P:(j + 1) * P], src[:, 2 * p:2 * p + 2, :].rearrange("p h r -> p (h r)"), idn[:])
                    ins.then_inc(stack_tr.sem, 1)

            def o_transposes(b, t):
                if t == 0:
                    wait(pe, ot_ready, b, HEADS // OG)
                    wait(pe, exp_done, b, HEADS * T_FILLS)
                if t >= 2:
                    wait(pe, o_tok_ready, b, t - 1)
                for g in range(HEADS // OG):
                    ins = nc.tensor.transpose(ps_t[:, t % 2, g * P:(g + 1) * P], OT[:, g, t * P:(t + 1) * P], idn[:])
                ins.then_inc(o_tr.sem, 1)

            def on_transposes(b, f):
                wait(pe, o_tok_ready, b, 2 * f + 2)
                if f:
                    wait(pe, ga_mul, b, 1)
                for t in (2 * f, 2 * f + 1):
                    for c in range(KC):
                        at = (t % 2) * DIM + c * P
                        ins = nc.tensor.transpose(ps_o[:, at:at + P], o_tok[:, t, c * P:(c + 1) * P], idn[:])
                    if t % 2:
                        ins.then_inc(on_tr.sem, 1)

            def project(b, f):
                wait(pe, on_ready, b, f + 1)
                for t in (2 * f, 2 * f + 1):
                    for c in range(KC):
                        ins = mm(ps_o[:, (t % 2) * DIM:(t % 2 + 1) * DIM], onT[:, c, t * P:(t + 1) * P],
                                 w_proj[:, c, :], start=c == 0, stop=c == KC - 1)
                ins.then_inc(proj_done.sem, 1)

            def h2_transposes(b, c):
                if c == 0:
                    wait(pe, ln2, b, 4)
                wait(pe, h2_ready, b, c)
                for t in range(TILES):
                    ins = nc.tensor.transpose(ps_o[:, t * P:(t + 1) * P], x_in[:, t, c * P:(c + 1) * P], idn[:])
                ins.then_inc(h2_tr.sem, 1)

            def logits(b):
                wait(pe, h2_ready, b, KC)
                for t in range(TILES):
                    for c in range(KC):
                        ins = mm(ps_o[:, t * EXPERTS:(t + 1) * EXPERTS], h2T[:, c, t * P:(t + 1) * P],
                                 w_router[:, c, :], start=c == 0, stop=c == KC - 1)
                ins.then_inc(logits_done.sem, 1)

            def weight_transposes(b):
                wait(pe, router, b, ROUTER_STEPS)
                for t in range(TILES):
                    ins = nc.tensor.transpose(ps_o[0:2 * EXPERTS, t * P:(t + 1) * P], cs[:, t, :], idn[:])
                ins.then_inc(c_tr.sem, 1)

            def tail(b, moe, more):
                n, m = b + 1, b - 1

                def tail_unit(u):
                    if moe:
                        unit(m, UNITS - IN_TAIL + u)

                if more:
                    wait(pe, s_used, b, PAIRS * S_FILLS)
                    h1_transposes(n)
                tail_unit(0)
                o_transposes(b, 0)
                o_transposes(b, 1)
                if more:
                    qkv(n, 0)
                tail_unit(1)
                o_transposes(b, 2)
                o_transposes(b, 3)
                tail_unit(2)
                if more:
                    qkv(n, 1)
                on_transposes(b, 0)
                tail_unit(3)
                project(b, 0)
                if more:
                    stack(n, 0, 0)
                tail_unit(4)
                if more:
                    stack(n, 0, 1)
                on_transposes(b, 1)
                tail_unit(5)
                project(b, 1)
                if more:
                    qkv(n, 2)
                tail_unit(6)
                if more:
                    stack(n, 1, 0)
                tail_unit(7)
                if more:
                    stack(n, 1, 1)
                    qkv(n, 3)
                tail_unit(8)
                h2_transposes(b, 0)
                if more:
                    stack(n, 2, 0)
                tail_unit(9)
                h2_transposes(b, 1)
                if more:
                    stack(n, 2, 1)
                logits(b)
                tail_unit(10)
                if more:
                    stack(n, 3, 0)
                tail_unit(11)
                if more:
                    stack(n, 3, 1)
                tail_unit(12)
                tail_unit(13)
                tail_unit(14)
                if more:
                    wait(pe, stack_ready, n, 4 * TILES)
                    fill_s(n, 0, 0)
                    fill_s(n, 0, 1)
                tail_unit(15)
                if more:
                    fill_s(n, 0, 2)
                    fill_s(n, 0, 3)
                weight_transposes(b)
                if more:
                    fill_s(n, 0, 4)
                if moe:
                    down(m, UNITS - 1)
                if more:
                    fill_s(n, 0, 5)
                    fill_s(n, 0, 6)

            pe.wait_ge(consts_in.sem, 96)
            h1_transposes(0)
            pe.wait_ge(mod_in.sem, 64)
            pe.wait_ge(setup_v.sem, 3)
            scT = c_s.rearrange("p (c b) -> p c b", c=KC)
            for i, (a, col) in enumerate([(1, 0), (1, 1), (0, 0), (0, 1), (4, 0), (4, 1), (3, 0), (3, 1)]):
                for c in range(KC):
                    ins = mm(ps_u[:, i * BATCH:(i + 1) * BATCH], w_mod[c][:, a * DIM + col * P:a * DIM + (col + 1) * P],
                             scT[:, c, :], start=c == 0, stop=c == KC - 1)
            ins.then_inc(setup_t.sem, 1)
            pe.wait_ge(o_cleared.sem, 1)
            for i, a in enumerate((2, 5)):
                for c in range(KC):
                    ins = mm(ps_o[0:BATCH, i * DIM:(i + 1) * DIM], scT[:, c, :], w_mod[c][:, a * DIM:(a + 1) * DIM],
                             start=c == 0, stop=c == KC - 1)
            ins.then_inc(setup_t.sem, 1)
            pe.wait_ge(weights_in.sem, 48)
            for t in range(TILES + 1):
                if t < TILES:
                    qkv(0, t)
                if t:
                    stack(0, t - 1, 0)
                    stack(0, t - 1, 1)
            wait(pe, stack_ready, 0, 4 * TILES)
            for k in range(S_FILLS):
                fill_s(0, 0, k)
            pe.wait_ge(setup_v.sem, 11)

            def batch(b, moe, more):
                attention(b, moe)
                tail(b, moe, more)

            every_batch(pe, lambda b: batch(b, False, True), lambda b: batch(b, True, True),
                        lambda b: batch(b, True, False))
            for u in range(UNITS):
                unit(LAST, u)
            down(LAST, UNITS - 1)

        @block.scalar
        def _(ac):
            def copy(dst, src):
                return nc.scalar.activation(dst, src, ACT.Copy)

            def exps(b, h, k):
                f = h * T_FILLS + k
                wait(ac, t_filled, b, f + 1)
                if k == 0:
                    wait(ac, pv_done, b, h - 1)
                if f == 0:
                    wait(ac, h2_low, b - 1, KC)
                at, n = ((0, SEQ), (SEQ, SEQ), (2 * SEQ, 2 * P))[k]
                nc.scalar.activation(probs[:, h % 2, at:at + n], ps_t[:, f % 2, 0:n], ACT.Exp, scale=SCALE)\
                    .then_inc(exp_done.sem, 1)

            def high(b, u):
                wait(ac, a_ready, b, u + 1)
                if u >= 2:
                    wait(ac, d_done, b, u - 1)
                else:
                    wait(ac, d_done, b - 1, UNITS)
                copy(a_part[0][:, u % 2, :], act[:, u % 2, :]).then_inc(a_high_done.sem, 1)

            def tanh(b, u):
                wait(ac, g_done, b, u + 1)
                if u >= 2:
                    wait(ac, a_low_done, b, u - 1)
                else:
                    wait(ac, a_low_done, b - 1, UNITS)
                nc.scalar.activation(act[:, u % 2, :], ps_g[:, 0:HALF], ACT.Tanh, scale=0.5).then_inc(tanh_done.sem, 1)

            def unit(b, u):
                if u:
                    high(b, u - 1)
                tanh(b, u)

            def o_out(b, g):
                wait(ac, pv_done, b, OG * (g + 1))
                wait(ac, stack_tr, b, 4 * TILES)
                copy(OT[:, g, :], ps_o[:]).then_inc(ot_ready.sem, 1)

            def split_weights(e):
                ac.wait_ge(expert_in[e % 2].sem, 16 * (e // 2 + 1))
                copy(w_part[0][:, e, :], stage[e % 2]).then_inc(w_high_done.sem, 1)

            def attention(b, moe):
                m = b - 1
                for p in range(PAIRS):
                    u = after_pair(p)
                    exps(b, 2 * p, 0)
                    if moe:
                        unit(m, u[0])
                    else:
                        split_weights(u[0])
                    exps(b, 2 * p, 1)
                    exps(b, 2 * p, 2)
                    if p and (2 * p - 1) % OG == OG - 1:
                        o_out(b, (2 * p - 1) // OG)
                    exps(b, 2 * p + 1, 0)
                    if moe:
                        unit(m, u[1])
                    else:
                        split_weights(u[1])
                    exps(b, 2 * p + 1, 1)
                    exps(b, 2 * p + 1, 2)
                o_out(b, HEADS // OG - 1)

            def h1_out(b, c):
                if c == 0:
                    wait(ac, mod_a, b, 1)
                    wait(ac, pv_done, b - 1, HEADS)
                wait(ac, h1_tr, b, c + 1)
                nc.scalar.activation(h1T[:, c, :], ps_s[:, c, :], ACT.Identity,
                                     scale=modA[:, c:c + 1], bias=modA[:, 2 + c:3 + c]).then_inc(h1_ready.sem, 1)

            def v_out(b, t):
                wait(ac, qkv_done, b, t + 1)
                wait(ac, pv_done, b - 1, HEADS)
                copy(V[:, t, :, 0:HD], ps_s[:, 1, (t % 2) * DIM:(t % 2 + 1) * DIM].rearrange("p (h d) -> p h d", d=HD))\
                    .then_inc(v_ready.sem, 1)

            def round_qk(b, t):
                wait(ac, rope_sum, b, t + 1)
                wait(ac, stack_tr, b, 4 * t)
                if t == 0:
                    wait(ac, o_tr, b - 1, TILES)
                src = work[:, 0, :].rearrange("p (s h d) -> p s h d", s=2, d=HD)
                for i, (dst, step) in enumerate(((QS, 2), (KS, 1))):
                    view = dst[:, :, 0:MROW].rearrange("p h (s d) -> p s h d", d=HD)[:, 0:step + 1:step]
                    nc.scalar.activation(view.bitcast(F32R), src[:, i:i + 1].broadcast_to([P, 2, HEADS, HD]), ACT.Copy)\
                        .then_inc(rounded.sem, 1)

            def stack_out(b, t, half_):
                for k in (2 * half_, 2 * half_ + 1):
                    f = 4 * t + k
                    wait(ac, stack_tr, b, f + 1)
                    if t == 0 and k == 0:
                        wait(ac, t_filled, b - 1, HEADS * T_FILLS)
                    dst = (QT, KT)[k // 2][:, 4 * (k % 2):4 * (k % 2) + 4, t * P:(t + 1) * P]
                    copy(dst, ps_t[:, f % 2, :].rearrange("p (j n) -> p j n", j=4)).then_inc(stack_ready.sem, 1)

            def on_out(b, f):
                wait(ac, on_tr, b, f + 1)
                src = ps_o[:].rearrange("p (t c n) -> p c t n", t=2, c=KC)
                dst = onT[:, :, 2 * f * P:(2 * f + 2) * P].rearrange("p c (t n) -> p c t n", t=2)
                copy(dst, src).then_inc(on_ready.sem, 1)

            def h2_out(b, c):
                if c == 0:
                    wait(ac, mod_b, b, 1)
                    wait(ac, proj_done, b, 2)
                wait(ac, h2_tr, b, c + 1)
                nc.scalar.activation(h2T[:, c, :], ps_o[:], ACT.Identity,
                                     scale=modB[:, c:c + 1], bias=modB[:, 2 + c:3 + c]).then_inc(h2_ready.sem, 1)

            def h2_round(b):
                wait(ac, h2_ready, b, KC)
                wait(ac, u_done, b - 1, UNITS)
                for c in range(KC):
                    copy(h2_part[0][:, c, :], h2T[:, c, :]).then_inc(h2_high.sem, 1)

            def tail(b, moe, more):
                n, m = b + 1, b - 1

                def tail_high(u):
                    if moe:
                        high(m, UNITS - IN_TAIL + u)

                def tail_tanh(u):
                    if moe:
                        tanh(m, UNITS - IN_TAIL + u)

                tail_high(-1)
                if more:
                    h1_out(n, 0)
                tail_tanh(0)
                if more:
                    h1_out(n, 1)
                tail_high(0)
                tail_tanh(1)
                if more:
                    v_out(n, 0)
                tail_high(1)
                tail_tanh(2)
                tail_high(2)
                on_out(b, 0)
                if more:
                    round_qk(n, 0)
                tail_tanh(3)
                if more:
                    v_out(n, 1)
                tail_high(3)
                if more:
                    stack_out(n, 0, 0)
                tail_tanh(4)
                if more:
                    stack_out(n, 0, 1)
                tail_high(4)
                on_out(b, 1)
                if more:
                    round_qk(n, 1)
                tail_tanh(5)
                tail_high(5)
                tail_tanh(6)
                if more:
                    v_out(n, 2)
                tail_high(6)
                if more:
                    stack_out(n, 1, 0)
                tail_tanh(7)
                if more:
                    stack_out(n, 1, 1)
                tail_high(7)
                if more:
                    round_qk(n, 2)
                tail_tanh(8)
                if more:
                    v_out(n, 3)
                tail_high(8)
                h2_out(b, 0)
                if more:
                    stack_out(n, 2, 0)
                tail_tanh(9)
                h2_out(b, 1)
                if more:
                    stack_out(n, 2, 1)
                tail_high(9)
                if more:
                    round_qk(n, 3)
                wait(ac, logits_done, b, 1)
                nc.scalar.activation(R[:, 15, :], ps_o[:, 0:TILES * EXPERTS], ACT.Exp, scale=-1.0)\
                    .then_inc(rexp_done.sem, 1)
                tail_tanh(10)
                tail_high(10)
                if more:
                    stack_out(n, 3, 0)
                tail_tanh(11)
                if more:
                    stack_out(n, 3, 1)
                for u in range(12, IN_TAIL):
                    tail_high(u - 1)
                    tail_tanh(u)
                tail_high(IN_TAIL - 1)
                h2_round(b)
                wait(ac, c_tr, b, 1)
                wait(ac, g_done, b - 1, UNITS)
                copy(cT[:], ps_o[0:2 * EXPERTS, :]).then_inc(ct_ready.sem, 1)

            ac.wait_ge(mod_in.sem, 64)
            nc.scalar.activation(c_e, c_sb, ACT.Exp, scale=-1.0).then_inc(setup_a.sem, 1)
            ac.wait_ge(setup_p.sem, 5)
            ac.wait_ge(gates_out.sem, 16)
            h1_out(0, 0)
            h1_out(0, 1)
            v_out(0, 0)
            for t in range(TILES):
                round_qk(0, t)
                if t + 1 < TILES:
                    v_out(0, t + 1)
                stack_out(0, t, 0)
                stack_out(0, t, 1)

            def batch(b, moe, more):
                attention(b, moe)
                tail(b, moe, more)

            every_batch(ac, lambda b: batch(b, False, True), lambda b: batch(b, True, True),
                        lambda b: batch(b, True, False))
            for u in range(UNITS):
                unit(LAST, u)
            high(LAST, UNITS - 1)

        @block.vector
        def _(ve):
            tt, ts, stt = nc.vector.tensor_tensor, nc.vector.tensor_scalar, nc.vector.scalar_tensor_tensor

            def row_max(b, p, k):
                f = p * S_FILLS + k
                wait_apart(ve, s_filled, b, f + 1, ve_passed)
                h = 2 * p + k // 3
                for qt, at in (((3, 0),), ((2, 0),), ((0, 0), (1, 2 * P)))[k % 3]:
                    n = (qt + 1) * P
                    ins = nc.vector.tensor_tensor_reduce(
                        out=ps_s[:, f % 2, at:at + n], in0=ps_s[:, f % 2, at:at + n], in1=mask[:, SEQ - n:SEQ], scale=1.0,
                        scalar=-3.0e38, op0=ALU.add, op1=ALU.max, accum_out=mmax[:, h, qt:qt + 1])
                ins.then_inc(s_used.sem, 1)

            def maxima(b, p):
                wait(ve, s_used, b, p * S_FILLS + 6)
                wait(ve, s_filled, b, p * S_FILLS)
                src = mmax[:, 2 * p:2 * p + 2, :]
                dst = mt[:, :, :].rearrange("p t (h r) -> p h t r", h=2)
                high, low = dst[:, :, :, MROW:MROW + 1], dst[:, :, :, MROW + 1:MROW + 2]
                src = src.unsqueeze(3)
                ts(high.bitcast(F32R), src, -1.0, None, ALU.mult).then_inc(m_high.sem, 1)
                wait(ve, m_high, b, p + 1)
                stt(out=low.bitcast(F32R).rearrange("p h t o -> p h (t o)"), in0=src.rearrange("p h t o -> p h (t o)"),
                    scalar=-1.0, in1=high.rearrange("p h t o -> p h (t o)"), op0=ALU.mult, op1=ALU.subtract)\
                    .then_inc(m_ready.sem, 1)

            def maxima_in(b, p):
                f = p * S_FILLS + S_FILLS - 1
                wait(ve, s_filled, b, f + 1)
                tt(QT[:, p, :], ps_s[:, f % 2, :], QT[:, p, :].bitcast(F32), ALU.add).then_inc(s_used.sem, 1)

            def gate_tanh(b, u):
                wait(ve, tanh_done, b, u + 1)
                buf = act[:, u % 2, :]
                stt(out=buf, in0=buf, scalar=1.0, in1=ps_g[:, 0:HALF], op0=ALU.add, op1=ALU.mult)\
                    .then_inc(gt_done.sem, 1)

            def weigh(b, u):
                wait(ve, gt_done, b, u + 1)
                buf = act[:, u % 2, :]
                tt(buf, buf, ps_g[:, HALF:SEQ], ALU.mult).then_inc(gw_done.sem, 1)

            def gate_up(b, u):
                wait(ve, u_done, b, u + 1)
                wait(ve, gw_done, b, u + 1)
                buf = act[:, u % 2, :]
                tt(buf, buf, ps_u[:, 0:HALF], ALU.mult).then_inc(a_ready.sem, 1)
                if u % EXPERTS == 0 and u:
                    scaled(b, 0)

            def unit(b, u):
                gate_tanh(b, u)
                weigh(b, u)
                gate_up(b, u)

            def scaled(b, f):
                wait(ve, d_done, b, EXPERTS * (f + 1))
                if f == 0:
                    wait(ve, gateb_loaded, b, 16)
                    wait(ve, out_ready, b - 1, 2)
                else:
                    wait(ve, out_ready, b, 1)
                tt(y_sb[:, :].rearrange("p (t d) -> p t d", t=2), ps_y[:].rearrange("p (t d) -> p t d", t=2),
                   gate_b[:, :].unsqueeze(1).broadcast_to([P, 2, DIM]), ALU.mult).then_inc(y_ready.sem, 1)

            def norm(b, src, dst, sig, rs, first):
                if first:
                    for t in range(TILES):
                        ins = nc.vector.bn_stats(stats[:, t, :], src[:, t, :])
                    ins.then_inc(sig.sem, 1)
                    wait_apart(ve, sig, b, 1, ve_passed)
                    for t in range(TILES):
                        ins = nc.vector.bn_aggr(mv[:, t, :], stats[:, t, :])
                    ins.then_inc(sig.sem, 1)
                    wait(ve, sig, b, 2)
                    ts(vare[:], mv[:, :, 1], EPS, None, ALU.add).then_inc(sig.sem, 1)
                else:
                    wait(ve, rs, b, 1)
                    for t in range(TILES):
                        ins = ts(dst[:, t, :], src[:, t, :], mv[:, t, 0:1], rstd[:, t:t + 1], ALU.subtract, ALU.mult)
                    ins.then_inc(sig.sem, 1)

            def norm1(b, first):
                if first:
                    wait(ve, x_loaded, b, 16)
                    wait(ve, rstd2, b - 2, 1)
                norm(b, x_in, x_in, ln1, rstd1, first)

            def attention(b, moe, more):
                m = b - 1

                def reds(*ks):
                    if p + 1 < PAIRS:
                        for k in ks:
                            row_max(b, p + 1, k)
                for p in range(PAIRS):
                    u = after_pair(p)
                    reds(0, 1)
                    if moe:
                        gate_tanh(m, u[0])
                    reds(2, 3)
                    if moe:
                        weigh(m, u[0])
                    reds(4)
                    if moe:
                        gate_up(m, u[0])
                    reds(5)
                    if p + 1 < PAIRS:
                        maxima(b, p + 1)
                    if moe:
                        gate_tanh(m, u[1])
                        weigh(m, u[1])
                    if p + 1 < PAIRS:
                        maxima_in(b, p + 1)
                    if moe:
                        gate_up(m, u[1])
                    if more and p == 2:
                        norm1(b + 1, True)
                    if more and p == 4:
                        norm1(b + 1, False)
                    if more and p == 5:
                        wait(ve, h1_ready, b, KC)
                        nc.vector.tensor_copy(modA[:], mods_of(b + 1, 0)).then_inc(mod_a.sem, 1)
                    if p == 5:
                        wait(ve, h2_ready, b - 1, KC)
                        nc.vector.tensor_copy(modB[:], mods_of(b, 4)).then_inc(mod_b.sem, 1)

            def first_scores(b, k0):
                for k in range(k0, S_FILLS - 1):
                    row_max(b, 0, k)
                maxima(b, 0)
                maxima_in(b, 0)

            def mods_of(b, lo):
                if isinstance(b, int):
                    return mods[:, b, lo:lo + 4]
                return mods[:, bass.ds(b, 1), lo:lo + 4].rearrange("p o n -> p (o n)")

            def o_token(b, t):
                wait(ve, o_tr, b, t + 1)
                wait(ve, on_tr, b - 1, 2)
                src = ps_t[:, t % 2, :].rearrange("p (h r) -> p h r", r=32)
                nc.vector.reciprocal(lin[:, t % 2, :].unsqueeze(2), src[:, :, HD:HD + 1]).then_inc(linv.sem, 1)
                wait(ve, linv, b, t + 1)
                tt(o_tok[:, t, :].rearrange("p (h d) -> p h d", d=HD), src[:, :, 0:HD],
                   lin[:, t % 2, :].unsqueeze(2).broadcast_to([P, HEADS, HD]), ALU.mult).then_inc(o_tok_ready.sem, 1)

            def rope(b, t):
                wait(ve, qkv_done, b, t + 1)
                wait(ve, low_ready, b, t)
                wait(ve, rounded, b, 2 * t)
                wait(ve, rope_sum, b, t)
                src = ps_s[:, 0, :].rearrange("p (h s d) -> p h s d", s=2, d=HD // 2)
                c = work[:, 1, :].rearrange("p (h s d) -> p h s d", s=2, d=HD // 2)
                full = [P, 2 * HEADS, 2, HD // 2]
                tt(work[:, 0, :].rearrange("p (g d) -> p g d", d=HD // 2),
                   ps_s[:, 0, :].rearrange("p (g d) -> p g d", d=HD // 2),
                   cos_t[:, t:t + 1, :].broadcast_to([P, 4 * HEADS, HD // 2]), ALU.mult)
                tt(c, src[:, :, ::-1, :], sin_t[:, t:t + 1, :, :].broadcast_to(full), ALU.mult).then_inc(roped.sem, 1)

            def low_qk(b, t):
                wait(ve, rounded, b, 2 * t + 2)
                src = work[:, 0, :].rearrange("p (s h d) -> p s h d", s=2, d=HD)
                tt(QS[:, :, HD:2 * HD].bitcast(F32R), src[:, 0], QS[:, :, 0:HD], ALU.subtract)
                tt(KS[:, :, 2 * HD:3 * HD].bitcast(F32R), src[:, 1], KS[:, :, 0:HD], ALU.subtract)\
                    .then_inc(low_ready.sem, 1)

            def residual(b, f):
                view = x1[:, 2 * f:2 * f + 2, :]
                if f == 0:
                    wait(ve, xres_loaded, b, 16)
                    wait(ve, gates_loaded, b, 32)
                t1 = y_sb[:, :].rearrange("p (t d) -> p t d", t=2)
                tt(view, view, gates[:, 1:2, :].broadcast_to([P, 2, DIM]), ALU.add).then_inc(xg_add.sem, 1)
                wait(ve, proj_done, b, f + 1)
                wait(ve, x1_ready, b, f)
                wait(ve, out_ready, b - 1, 1)
                tt(t1, ps_o[:].rearrange("p (t d) -> p t d", t=2), gates[:, 0:1, :].broadcast_to([P, 2, DIM]),
                   ALU.mult).then_inc(ga_mul.sem, 1)
                wait(ve, ga_mul, b, f + 1)
                wait(ve, xg_add, b, f + 1)
                tt(view, view, t1, ALU.add).then_inc(x1_ready.sem, 1)

            def route(b, part):
                k = [ROUTER_AT[part]]

                def step(ins, then=wait):
                    k[0] += 1
                    ins.then_inc(router.sem, 1)
                    then(ve, router, b, k[0])

                G = GROUPS
                r = [R[:, i, :] for i in range(16)]
                te = lambda i: R[:, i, :].rearrange("p (t e) -> p t e", t=TILES)
                gs = r[7][:, 16:32]
                if part == 0:
                    wait(ve, rexp_done, b, 1)
                    step(ts(r[1], r[15], 1.0, None, ALU.add))
                    step(nc.vector.reciprocal(r[2], r[1]))
                    step(tt(te(3), te(2), rb[:, :].unsqueeze(1).broadcast_to([P, TILES, EXPERTS]), ALU.add))
                    four = r[3].rearrange("p (g a c) -> p g a c", a=2, c=2)
                    hi = r[4][:, 0:32].rearrange("p (g c) -> p g c", c=2)
                    lo = r[5][:, 0:32].rearrange("p (g c) -> p g c", c=2)
                    nc.vector.tensor_tensor(hi, four[:, :, 0, :], four[:, :, 1, :], ALU.max)
                    step(tt(lo, four[:, :, 0, :], four[:, :, 1, :], ALU.min))
                    one, two, three = (r[6][:, 16 * i:16 * i + 16].unsqueeze(2) for i in range(3))
                    tt(one, hi[:, :, 0:1], hi[:, :, 1:2], ALU.max)
                    tt(two, hi[:, :, 0:1], hi[:, :, 1:2], ALU.min)
                    step(tt(three, lo[:, :, 0:1], lo[:, :, 1:2], ALU.max))
                    second = r[7][:, 0:16].unsqueeze(2)
                    step(tt(second, two, three, ALU.max))
                    step(tt(gs.unsqueeze(2), one, second, ALU.add))
                elif part == 1:
                    gt_ = gs.rearrange("p (t g) -> p t g", t=TILES)
                    other = gt_.unsqueeze(2).broadcast_to([P, TILES, G, G])
                    own = gt_.unsqueeze(3).broadcast_to([P, TILES, G, G])
                    c4 = lambda i: R[:, i, :].rearrange("p (t g o) -> p t g o", t=TILES, g=G)
                    tt(c4(8), other, own, ALU.is_gt)
                    step(tt(c4(9), other, own, ALU.is_equal))
                    step(tt(c4(10), c4(9), before[:, :].rearrange("p (t g o) -> p t g o", t=TILES, g=G), ALU.mult))
                    step(tt(r[11], r[8], r[10], ALU.add))
                    rank = r[12][:, 0:16]
                    step(nc.vector.reduce_sum(rank.unsqueeze(2), r[11].rearrange("p (x o) -> p x o", o=G), AX_X))
                    chosen = r[12][:, 16:32]
                    step(ts(chosen, rank, float(TOP_GROUPS), None, ALU.is_lt))
                    four4 = lambda a: a.unsqueeze(2).broadcast_to([P, 16, G])
                    pen = r[12][:, 32:48]
                    ts(pen, chosen, -1.0, -NEG, ALU.add, ALU.mult)
                    step(tt(r[4].rearrange("p (x o) -> p x o", o=G), r[3].rearrange("p (x o) -> p x o", o=G), four4(chosen), ALU.mult))
                    step(tt(r[5].rearrange("p (x o) -> p x o", o=G), r[4].rearrange("p (x o) -> p x o", o=G), four4(pen), ALU.add), lambda *a: wait_apart(*a, ve_passed))
                    for t in range(TILES):
                        ins = nc.vector.max(m8[:, t, :], r[5][:, t * EXPERTS:(t + 1) * EXPERTS])
                    step(ins)
                elif part == 2:
                    step(nc.vector.tensor_copy(top4[:, :, 0:TOP_K], m8[:, :, 0:TOP_K]),
                         lambda *a: wait_apart(*a, ve_passed))
                    for t in range(TILES):
                        ins = nc.vector.match_replace(r[6][:, t * EXPERTS:(t + 1) * EXPERTS], top4[:, t, :],
                                                      r[5][:, t * EXPERTS:(t + 1) * EXPERTS], NEG)
                    step(ins)
                    step(tt(r[11], r[6], r[5], ALU.not_equal))
                    step(tt(r[14], r[11], r[2], ALU.mult))
                    step(nc.vector.reduce_sum(r[13][:, 4:8].unsqueeze(2), te(14), AX_X))
                else:
                    step(ts(r[13][:, 8:12], r[13][:, 4:8], 1e-20, 2 / ROUTED_SCALE, ALU.add, ALU.mult))
                    step(nc.vector.reciprocal(r[13][:, 12:16], r[13][:, 8:12]))
                    step(tt(te(15), te(14), r[13][:, 12:16].unsqueeze(2).broadcast_to([P, TILES, EXPERTS]), ALU.mult))
                    step(nc.vector.tensor_copy(cs[:, :, 0:EXPERTS].bitcast(F32R), te(15)))
                    step(tt(cs[:, :, EXPERTS:2 * EXPERTS].bitcast(F32R), te(15), cs[:, :, 0:EXPERTS], ALU.subtract))
                assert k[0] == ROUTER_AT[part + 1], k[0]

            def tail(b, moe, more):
                n, m = b + 1, b - 1

                def units(*us):
                    if moe:
                        for u in us:
                            unit(m, UNITS - IN_TAIL + u)

                units(0)
                o_token(b, 0)
                o_token(b, 1)
                units(1)
                if more:
                    rope(n, 0)
                o_token(b, 2)
                o_token(b, 3)
                units(2)
                if more:
                    low_qk(n, 0)
                units(3)
                if more:
                    rope(n, 1)
                residual(b, 0)
                units(4)
                if more:
                    low_qk(n, 1)
                units(5)
                residual(b, 1)
                wait(ve, x1_ready, b, 2)
                units(6)
                if more:
                    rope(n, 2)
                norm(b, x1, x_in, ln2, rstd2, True)
                units(7)
                norm(b, x1, x_in, ln2, rstd2, False)
                if more:
                    low_qk(n, 2)
                units(8)
                if more:
                    rope(n, 3)
                units(9)
                if more:
                    low_qk(n, 3)
                units(10)
                route(b, 0)
                units(11)
                route(b, 1)
                units(12)
                route(b, 2)
                units(13)
                route(b, 3)
                units(14)
                if more:
                    row_max(n, 0, 0)
                    row_max(n, 0, 1)
                units(15)
                if more:
                    first_scores(n, 2)
                if moe:
                    scaled(m, 1)

            nc.vector.memset(ps_o[:], 0.0).then_inc(o_cleared.sem, 1)
            norm1(0, True)
            ve.wait_ge(setup_a.sem, 1)
            ts(c_d, c_e, 1.0, None, ALU.add).then_inc(setup_v.sem, 1)
            ve.wait_ge(setup_v.sem, 1)
            nc.vector.reciprocal(c_r, c_d).then_inc(setup_v.sem, 1)
            ve.wait_ge(setup_v.sem, 2)
            tt(c_s, c_r, c_sb, ALU.mult).then_inc(setup_v.sem, 1)
            norm1(0, False)
            ve.wait_ge(setup_t.sem, 1)
            src = ps_u[:, 0:8 * BATCH].rearrange("p (i b) -> p b i", i=8)
            for i, add in enumerate((1.0, 0.0, 1.0, 0.0)):
                ins = ts(mods[:, :, 2 * i:2 * i + 2], src[:, :, 2 * i:2 * i + 2], add, None, ALU.add)
            ins.then_inc(setup_v.sem, 1)
            ve.wait_ge(setup_t.sem, 2)
            ts(g16, ps_o[0:BATCH, :], 0.0, 2.0, ALU.is_ge, ALU.mult).then_inc(setup_v.sem, 1)
            ve.wait_ge(setup_v.sem, 5)
            ts(g16, g16, -1.0, None, ALU.add).then_inc(setup_v.sem, 1)
            ts(sg16, ps_o[0:BATCH, :], -1.0, None, ALU.mult).then_inc(setup_v.sem, 1)
            ve.wait_ge(setup_v.sem, 7)
            stt(out=sg16, in0=sg16, scalar=0.25, in1=ps_o[0:BATCH, :], op0=ALU.max, op1=ALU.max).then_inc(setup_v.sem, 1)
            ve.wait_ge(setup_v.sem, 8)
            tt(gfin[:, 0:2, :].rearrange("p t n -> p (t n)"), g16, sg16, ALU.mult).then_inc(setup_v.sem, 1)
            ve.wait_ge(setup_v.sem, 9)
            tt(gfin[:, 2, :], gfin[:, 0, :], b16, ALU.mult).then_inc(setup_v.sem, 1)
            ve.wait_ge(consts_in.sem, 96)
            ve.wait_ge(setup_v.sem, 10)
            nc.vector.tensor_copy(pick_r[:], pick_f[:]).then_inc(setup_v.sem, 1)
            nc.vector.memset(top4[:], NEG).then_inc(setup_v.sem, 1)
            ve.wait_ge(setup_v.sem, 12)
            ve.wait_ge(setup_p.sem, 5)
            nc.vector.tensor_copy(modA[:], mods[:, 0, 0:4]).then_inc(mod_a.sem, 1)
            for t in range(TILES):
                rope(0, t)
                low_qk(0, t)
            first_scores(0, 0)

            def batch(b, moe, more):
                attention(b, moe, more)
                tail(b, moe, more)

            every_batch(ve, lambda b: batch(b, False, True), lambda b: batch(b, True, True),
                        lambda b: batch(b, True, False))
            for u in range(UNITS):
                unit(LAST, u)
            scaled(LAST, 1)

        @block.gpsimd
        def _(po):
            def mask_probs(b, h):
                wait_apart(po, exp_done, b, T_FILLS * (h + 1), po_passed)
                buf = probs[:, h % 2, :]
                a = bass.AP(buf.tensor, buf.offset, [buf.ap[0], [SEQ, 3], [1, P]])
                po.affine_select(out=a, in_=a, compare_op=ALU.is_ge, fill=0.0, base=0,
                                 pattern=[[0, 3], [1, P]], channel_multiplier=-1).then_inc(masked.sem, 1)
                d = probs[:, h % 2, KT_AT[3]:KT_AT[3] + P]
                po.affine_select(out=d, in_=d, compare_op=ALU.is_ge, fill=0.0, base=0,
                                 pattern=[[1, P]], channel_multiplier=-1).then_inc(masked.sem, 1)

            def rope_add(b, t):
                wait(po, roped, b, t + 1)
                po.tensor_tensor(work[:, 0, :], work[:, 0, :], work[:, 1, :], ALU.add).then_inc(rope_sum.sem, 1)

            def inv_std(b, sig, rs):
                wait(po, sig, b, 3)
                po.tensor_tensor(rstd[:], vare[:], half[:], ALU.pow).then_inc(rs.sem, 1)

            def low(b, u):
                wait(po, a_high_done, b, u + 1)
                po.tensor_tensor(a_part[1][:, u % 2, :], act[:, u % 2, :], a_part[0][:, u % 2, :].bitcast(F32),
                                 ALU.subtract).then_inc(a_low_done.sem, 1)
                if u == EXPERTS:
                    add_stream(b, 0)

            def add_stream(b, f):
                if f == 0:
                    wait(po, prev_copied, b, 16)
                wait(po, y_ready, b, f + 1)
                x_ = x1_prev[:, 2 * f:2 * f + 2, :].rearrange("p t d -> p (t d)")
                po.tensor_tensor(x_, x_, y_sb[:], ALU.add).then_inc(out_ready.sem, 1)

            def h2_rest(b, c):
                wait(po, h2_high, b, c + 1)
                po.tensor_tensor(h2_part[1][:, c, :], h2T[:, c, :], h2_part[0][:, c, :].bitcast(F32), ALU.subtract)\
                    .then_inc(h2_low.sem, 1)

            def split_weights(e):
                po.wait_ge(w_high_done.sem, e + 1)
                po.tensor_tensor(w_part[1][:, e, :], stage[e % 2], w_part[0][:, e, :].bitcast(F32), ALU.subtract)\
                    .then_inc(w_low_done.sem, 1)

            def stack_constants(b):
                wait_apart(po, o_tr, b - 1, TILES, po_passed)
                po.memset(QS[:, :, MROW:STRIP], 0.0).then_inc(consts_set.sem, 1)
                po.memset(KS[:, :, MROW:MROW + 2], 1.0).then_inc(consts_set.sem, 1)
                po.memset(KS[:, :, MROW + 2:STRIP], 0.0).then_inc(consts_set.sem, 1)

            def attention(b, moe, more):
                m = b - 1
                for p in range(PAIRS):
                    u = after_pair(p)
                    if moe and u[0]:
                        low(m, u[0] - 1)
                    mask_probs(b, 2 * p)
                    if moe:
                        low(m, u[1] - 1)
                    else:
                        split_weights(u[0])
                    mask_probs(b, 2 * p + 1)
                    if not moe:
                        split_weights(u[1])
                    if more and p == 3:
                        inv_std(b + 1, ln1, rstd1)

            def tail(b, moe, more):
                n, m = b + 1, b - 1

                def lows(*us):
                    if moe:
                        for u in us:
                            low(m, UNITS - IN_TAIL + u)

                lows(-1, 0, 1)
                if more:
                    rope_add(n, 0)
                lows(2)
                if more:
                    stack_constants(n)
                lows(3)
                if more:
                    rope_add(n, 1)
                lows(4, 5, 6)
                if more:
                    rope_add(n, 2)
                inv_std(b, ln2, rstd2)
                lows(7, 8)
                if more:
                    rope_add(n, 3)
                lows(*range(9, IN_TAIL))
                h2_rest(b, 0)
                h2_rest(b, 1)
                if moe:
                    add_stream(m, 1)

            po.memset(half[:], -0.5).then_inc(setup_p.sem, 1)
            po.wait_ge(setup_p.sem, 1)
            inv_std(0, ln1, rstd1)
            po.memset(V[:, :, :, HD:HD + 1], 1.0).then_inc(setup_p.sem, 1)
            po.memset(mt[:], 0.0).then_inc(setup_p.sem, 1)
            po.memset(before[:], 1.0).then_inc(setup_p.sem, 1)
            po.wait_ge(setup_p.sem, 4)
            bv = before[:, :].rearrange("p (t g o) -> p t g o", t=TILES, g=GROUPS)
            po.affine_select(out=bv, in_=bv, compare_op=ALU.is_gt, fill=0.0, base=0,
                             pattern=[[0, TILES], [1, GROUPS], [-1, GROUPS]], channel_multiplier=0).then_inc(setup_p.sem, 1)
            po.wait_ge(setup_t.sem, 2)
            stack_constants(0)
            for t in range(TILES):
                rope_add(0, t)

            def batch(b, moe, more):
                attention(b, moe, more)
                tail(b, moe, more)

            every_batch(po, lambda b: batch(b, False, True), lambda b: batch(b, True, True),
                        lambda b: batch(b, True, False))
            for u in range(UNITS):
                low(LAST, u)
            add_stream(LAST, 1)


def kernel(L0_attn_x, L0_attn_w_qkv, L0_attn_w_proj, L0_attn_b_proj, L0_ffn_router_weight, L0_ffn_router_bias,
           L0_ffn_w_gate, L0_ffn_w_up, L0_ffn_w_down, L0_c, L0_wmod):
    import concourse.bacc as bacc
    from concourse.bass_utils import run_bass_kernel_spmd

    def rows(w):
        w = np.asarray(w)
        return w.reshape(KC, P, w.shape[1]).transpose(1, 0, 2)

    inv_freq = (np.float32(1.0) / np.float32(10000.0) ** (np.arange(0, HD, 2, dtype=np.float32) / np.float32(HD))).astype(np.float32)
    angle = (np.arange(SEQ, dtype=np.float32)[:, None] * inv_freq[None, :]).astype(np.float32)
    cos = np.cos(angle.astype(np.float64)).astype(np.float32).reshape(TILES, P, HD // 2).transpose(1, 0, 2)
    sin = np.sin(angle.astype(np.float64)).astype(np.float32).reshape(TILES, P, HD // 2).transpose(1, 0, 2)
    tril = np.zeros((P, SEQ), np.float32)
    tril[:, SEQ - P:] = np.where(np.arange(P)[None, :] > np.arange(P)[:, None], np.float32(NEG), np.float32(0))
    pick = np.concatenate([np.eye(EXPERTS, dtype=np.float32)] * 2, axis=0)
    gate = np.asarray(L0_ffn_w_gate).reshape(EXPERTS, INNER, KC, P).transpose(3, 0, 2, 1)
    up = np.asarray(L0_ffn_w_up).reshape(EXPERTS, INNER, KC, P).transpose(3, 0, 2, 1)
    arrays = {
        "x": np.asarray(L0_attn_x),
        "wqkv": rows(L0_attn_w_qkv),
        "wproj": rows(L0_attn_w_proj),
        "bproj": np.asarray(L0_attn_b_proj)[None, :],
        "rw": rows(np.asarray(L0_ffn_router_weight).T),
        "rbias": np.asarray(L0_ffn_router_bias)[None, :],
        "wex": np.concatenate([gate.reshape(P, EXPERTS, KC * INNER), up.reshape(P, EXPERTS, KC * INNER),
                               np.asarray(L0_ffn_w_down).transpose(2, 0, 1)], axis=2),
        "ct": np.asarray(L0_c).T.reshape(KC, P, BATCH).transpose(1, 0, 2).reshape(P, KC * BATCH),
        "wmod": rows(L0_wmod),
        "cosq": cos,
        "sinq": np.stack([-sin, sin], axis=2),
        "tril_bias": tril,
        "ident": np.eye(P, dtype=np.float32),
        "pick": pick,
    }
    arrays = {n: np.ascontiguousarray(a) for n, a in arrays.items()}
    nc = bacc.Bacc("TRN2", target_bir_lowering=False, num_devices=1)
    args = {n: nc.dram_tensor(n, a.shape, mybir.dt.from_np(a.dtype), kind="ExternalInput").ap() for n, a in arrays.items()}
    y = nc.dram_tensor("y", (BATCH, SEQ, DIM), F32, kind="ExternalOutput").ap()
    build(nc, out=y, **args)
    r = run_bass_kernel_spmd(nc, [arrays], core_ids=[0])
    return r.results[0]["y"]
```

```python
from contextlib import ExitStack

import numpy as np

import concourse.bass as bass
from concourse import mybir

ALU = mybir.AluOpType
ACT = mybir.ActivationFunctionType
F32 = mybir.dt.float32
F32R = mybir.dt.float32r
BF16 = mybir.dt.bfloat16
AX_X = mybir.AxisListType.X

P = 128
BATCH, SEQ, DIM = 16, 512, 256
HEADS, HD = 16, 16
EXPERTS, INNER = 16, 128
GROUPS, TOP_GROUPS, TOP_K = 4, 2, 4
ROUTED_SCALE = 2.5
EPS = 1e-5
TILES = SEQ // P
KC = DIM // P
PAIRS = HEADS // 2
STRIP = 64
MROW = 48
OG = 4
SCALE = HD ** -0.5
NEG = -1e9

S_FILLS = 7
T_FILLS = 3
KT_AT = {0: 0, 1: SEQ, 3: SEQ + 3 * P, 2: 2 * SEQ}
PROBS = 2 * SEQ + 2 * P
ROUTER_STEPS = 25
EXPERT_W = 2 * KC * INNER + DIM
PRODUCTS = ((0, 0), (0, 1), (1, 0))
HALF = SEQ // 2
UNITS = 2 * EXPERTS
IN_TAIL = 16


class Signal:

    def __init__(self, sem, per):
        self.sem, self.per = sem, per

    def at(self, b, k):
        return b * self.per + k


def wait(eng, signal, b, k):
    value = signal.at(b, k)
    if isinstance(value, int) and value <= 0:
        return
    eng.wait_ge(signal.sem, value)


def wait_apart(eng, signal, b, k, passed):
    wait(eng, signal, b, k)
    eng.sem_inc(passed.sem, 1)


def build(nc, x, wqkv, wproj, bproj, rw, rbias, wex, ct, wmod, cosq, sinq, tril_bias, ident, pick, out):
    with ExitStack() as ctx:
        def sb(name, shape, dt=F32):
            return ctx.enter_context(nc.sbuf_tensor(name, shape, dt))

        def ps(name, shape):
            return ctx.enter_context(nc.psum_tensor(name, shape, F32))

        def signal(name, per):
            return Signal(ctx.enter_context(nc.semaphore(name)), per)

        w_qkv = sb("w_qkv", [P, KC, 3 * DIM])
        w_proj = sb("w_proj", [P, KC, DIM])
        w_router = sb("w_router", [P, KC, EXPERTS])
        w_part = [sb(n, [P, EXPERTS, EXPERT_W], F32R) for n in ("w_high", "w_low")]
        cos_t = sb("cos_t", [P, TILES, HD // 2])
        sin_t = sb("sin_t", [P, TILES, 2, HD // 2])
        mask = sb("mask", [P, SEQ])
        idn = sb("idn", [P, P])
        pick_f = sb("pick_f", [2 * EXPERTS, EXPERTS])
        pick_r = sb("pick_r", [2 * EXPERTS, EXPERTS], F32R)
        rb = sb("rb", [P, EXPERTS])
        half = sb("half", [P, TILES])
        mods = sb("mods", [P, BATCH, 8])
        act = sb("act", [P, 2, HALF])
        a_part = [sb(n, [P, 2, HALF], F32R) for n in ("a_high", "a_low")]
        x_in = sb("x_in", [P, TILES, DIM])
        x1 = sb("x1", [P, TILES, DIM])
        x1_prev = sb("x1_prev", [P, TILES, DIM])
        h2_part = [sb(n, [P, KC, SEQ], F32R) for n in ("h2_high", "h2_low")]
        QT = sb("QT", [P, PAIRS, SEQ], F32R)
        KT = sb("KT", [P, PAIRS, SEQ], F32R)
        V = sb("V", [P, TILES, HEADS, HD + 1])
        probs = sb("probs", [P, 2, PROBS])
        OT = sb("OT", [P, HEADS // OG, SEQ])
        work = sb("work", [P, 2, SEQ])
        y_sb = sb("y_sb", [P, SEQ])
        o_tok = sb("o_tok", [P, TILES, DIM])
        gates = sb("gates", [P, 2, DIM])
        gate_b = sb("gate_b", [P, DIM])
        mmax = sb("mmax", [P, HEADS, TILES])
        mt = sb("mt", [P, TILES, P])
        cT = sb("cT", [2 * EXPERTS, SEQ], F32R)
        modA = sb("modA", [P, 4])
        modB = sb("modB", [P, 4])
        stats = sb("stats", [P, TILES, 6])
        mv = sb("mv", [P, TILES, 2])
        vare = sb("vare", [P, TILES])
        rstd = sb("rstd", [P, TILES])
        lin = sb("lin", [P, 2, HEADS])
        before = sb("before", [P, TILES * GROUPS * GROUPS])
        top4 = sb("top4", [P, TILES, 8])
        m8 = sb("m8", [P, TILES, 8])
        cs = sb("cs", [P, TILES, 2 * EXPERTS])
        stacks = OT[:, :, :].rearrange("p g n -> p (g n)").rearrange("p (s h r) -> p s h r", s=2, r=STRIP)
        QS, KS = stacks[:, 0], stacks[:, 1]
        flat = probs[:, :, :].rearrange("p a n -> p (a n)")
        h1T = flat[:, 0:KC * SEQ].rearrange("p (c n) -> p c n", c=KC)
        onT = flat[:, KC * SEQ:2 * KC * SEQ].rearrange("p (c n) -> p c n", c=KC)
        h2T = onT
        R = flat[:, 0:KC * SEQ].rearrange("p (i n) -> p i n", i=16)
        w_mod = [flat[:, 0:6 * DIM], OT[:, :, :].rearrange("p g n -> p (g n)")[:, 0:6 * DIM]]
        c_sb, c_e, c_d, c_r, c_s = (flat[:, 6 * DIM + i * 32:6 * DIM + i * 32 + 32] for i in range(5))
        gfin = flat[0:BATCH, 6 * DIM + 160:9 * DIM + 160].rearrange("p (t n) -> p t n", t=3)
        g16, sg16 = work[0:BATCH, 0, :], work[0:BATCH, 1, :]
        b16 = o_tok[0:BATCH, 0, :]
        stage = [t[:, :, :].rearrange("p t d -> p (t d)")[:, 0:EXPERT_W] for t in (x1, x1_prev)]

        ps_s = ps("ps_s", [P, 2, SEQ])
        ps_t = ps("ps_t", [P, 2, SEQ])
        ps_o = ps("ps_o", [P, SEQ])
        ps_g = ps("ps_g", [P, SEQ])
        ps_y = ps("ps_y", [P, SEQ])
        ps_u = ps("ps_u", [P, SEQ])
        gate_dram = nc.dram_tensor("gate_dram", (BATCH, 3, DIM), F32).ap()

        weights_in = signal("weights_in", 0)
        consts_in = signal("consts_in", 0)
        mod_in = signal("mod_in", 0)
        expert_in = [signal(f"expert_in{i}", 0) for i in range(2)]
        w_high_done = signal("w_high_done", 0)
        w_low_done = signal("w_low_done", 0)
        setup_v = signal("setup_v", 0)
        o_cleared = signal("o_cleared", 0)
        setup_p = signal("setup_p", 0)
        setup_a = signal("setup_a", 0)
        setup_t = signal("setup_t", 0)
        gates_out = signal("gates_out", 0)
        x_loaded = signal("x_loaded", 16)
        xres_loaded = signal("xres_loaded", 16)
        prev_copied = signal("prev_copied", 16)
        gates_loaded = signal("gates_loaded", 32)
        gateb_loaded = signal("gateb_loaded", 16)
        stored = signal("stored", 32)
        consts_set = signal("consts_set", 3)
        s_filled = signal("s_filled", PAIRS * S_FILLS)
        t_filled = signal("t_filled", HEADS * T_FILLS)
        pv_done = signal("pv_done", HEADS)
        g_done, u_done = (signal(n, UNITS) for n in ("g_done", "u_done"))
        d_done = signal("d_done", UNITS)
        h1_tr = signal("h1_tr", KC)
        o_tr = signal("o_tr", TILES)
        qkv_done = signal("qkv_done", TILES)
        on_tr = signal("on_tr", 2)
        proj_done = signal("proj_done", 2)
        h2_tr = signal("h2_tr", KC)
        logits_done = signal("logits_done", 1)
        c_tr = signal("c_tr", 1)
        stack_tr = signal("stack_tr", 4 * TILES)
        exp_done = signal("exp_done", HEADS * T_FILLS)
        ot_ready = signal("ot_ready", HEADS // OG)
        tanh_done = signal("tanh_done", UNITS)
        a_high_done = signal("a_high_done", UNITS)
        a_low_done = signal("a_low_done", UNITS)
        h2_high = signal("h2_high", KC)
        h2_low = signal("h2_low", KC)
        h1_ready = signal("h1_ready", KC)
        rounded = signal("rounded", 2 * TILES)
        v_ready = signal("v_ready", TILES)
        on_ready = signal("on_ready", 2)
        stack_ready = signal("stack_ready", 4 * TILES)
        h2_ready = signal("h2_ready", KC)
        rexp_done = signal("rexp_done", 1)
        ct_ready = signal("ct_ready", 1)
        s_used = signal("s_used", PAIRS * S_FILLS)
        m_high = signal("m_high", PAIRS)
        m_ready = signal("m_ready", PAIRS)
        gt_done, gw_done, a_ready = (signal(n, UNITS) for n in ("gt_done", "gw_done", "a_ready"))
        ln1 = signal("ln1", 4)
        ln2 = signal("ln2", 4)
        mod_a = signal("mod_a", 1)
        mod_b = signal("mod_b", 1)
        linv = signal("linv", TILES)
        o_tok_ready = signal("o_tok_ready", TILES)
        roped = signal("roped", TILES)
        low_ready = signal("low_ready", TILES)
        ga_mul = signal("ga_mul", 2)
        xg_add = signal("xg_add", 2)
        x1_ready = signal("x1_ready", 2)
        router = signal("router", ROUTER_STEPS)
        y_ready = signal("y_ready", 2)
        masked = signal("masked", 2 * HEADS)
        rope_sum = signal("rope_sum", TILES)
        rstd1 = signal("rstd1", 1)
        rstd2 = signal("rstd2", 1)
        out_ready = signal("out_ready", 2)

        ve_passed = signal("ve_passed", 0)
        po_passed = signal("po_passed", 0)

        LAST = BATCH - 1

        def every_batch(eng, first, middle, last):
            first(0)
            with eng.Fori(1, LAST) as b:
                middle(b)
            last(LAST)

        block = ctx.enter_context(nc.Block())

        def after_pair(p):
            return [2 * p, 2 * p + 1]

        assert [u for p in range(PAIRS) for u in after_pair(p)] == list(range(UNITS - IN_TAIL))

        def unit_banks(b, u):
            if isinstance(b, int) and b == LAST and u % 2:
                return ps_s[:, 0, :], ps_s[:, 1, :]
            return ps_g, ps_u

        def bank_free(b, u):
            return u - 1 if isinstance(b, int) and b == LAST and u else u

        @block.sync
        def _(sp):
            def dram_x(b):
                return x[b].rearrange("(t p) d -> p t d", p=P)

            def gate_rows(b, lo, hi):
                src = gate_dram[b, lo:hi, :]
                return bass.AP(src.tensor, src.offset, [[0, P], [DIM, hi - lo], [1, DIM]]) if isinstance(b, int) \
                    else gate_dram[bass.ds(b, 1), lo:hi, :].broadcast_to([P, hi - lo, DIM])

            sp.dma_start(x_in[:], dram_x(0)).then_inc(x_loaded.sem, 16)
            sp.dma_start(c_sb, ct).then_inc(mod_in.sem, 16)
            sp.dma_start(idn[:], ident).then_inc(consts_in.sem, 16)
            sp.dma_start(cos_t[:], cosq).then_inc(consts_in.sem, 16)
            sp.dma_start(sin_t[:], sinq).then_inc(consts_in.sem, 16)
            sp.dma_start(mask[:], tril_bias).then_inc(consts_in.sem, 16)
            sp.dma_start(pick_f[:], pick).then_inc(consts_in.sem, 16)
            sp.dma_start(rb[:], rbias.broadcast_to([P, EXPERTS])).then_inc(consts_in.sem, 16)
            for c in range(KC):
                sp.dma_start(w_mod[c], wmod[:, c, :]).then_inc(mod_in.sem, 16)
            sp.dma_start(b16, bproj.broadcast_to([BATCH, DIM])).then_inc(mod_in.sem, 16)
            sp.dma_start(w_qkv[:], wqkv).then_inc(weights_in.sem, 16)
            sp.dma_start(w_proj[:], wproj).then_inc(weights_in.sem, 16)
            sp.dma_start(w_router[:], rw).then_inc(weights_in.sem, 16)
            sp.wait_ge(setup_v.sem, 10)
            sp.dma_start(gate_dram, gfin).then_inc(gates_out.sem, 16)

            def experts_weights():
                for e in range(EXPERTS):
                    if e >= 2:
                        sp.wait_ge(w_low_done.sem, e - 1)
                    sp.dma_start(stage[e % 2], wex[:, e, :]).then_inc(expert_in[e % 2].sem, 16)
                sp.wait_ge(gates_out.sem, 16)
                sp.wait_ge(w_low_done.sem, EXPERTS)

            def set_aside(b):
                sp.wait_ge(x1_ready.sem, x1_ready.at(b, 2))
                sp.wait_ge(ln2.sem, ln2.at(b, 4))
                wait(sp, stored, b - 1, 32)
                sp.dma_start(x1_prev[:], x1[:]).then_inc(prev_copied.sem, 16)
                wait(sp, y_ready, b - 1, 2)
                sp.dma_start(gate_b[:], gate_rows(b, 1, 2).rearrange("p o d -> p (o d)")).then_inc(gateb_loaded.sem, 16)

            def store(b):
                dst = out[b].rearrange("(t p) d -> p t d", p=P)
                for f in range(2):
                    sp.wait_ge(out_ready.sem, out_ready.at(b, f + 1))
                    sp.dma_start(dst[:, 2 * f:2 * f + 2, :], x1_prev[:, 2 * f:2 * f + 2, :]).then_inc(stored.sem, 16)

            def batch(b, moe, more):
                if more:
                    sp.wait_ge(h1_tr.sem, h1_tr.at(b, KC))
                    wait(sp, h2_tr, b - 1, KC)
                    sp.dma_start(x_in[:], dram_x(b + 1)).then_inc(x_loaded.sem, 16)
                if moe:
                    set_aside(b - 1)
                    wait(sp, prev_copied, b - 1, 16)
                else:
                    experts_weights()
                sp.dma_start(x1[:], dram_x(b)).then_inc(xres_loaded.sem, 16)
                wait(sp, x1_ready, b - 1, 2)
                sp.dma_start(gates[:, 0, :], gate_rows(b, 0, 1).rearrange("p o d -> p (o d)")).then_inc(gates_loaded.sem, 16)
                sp.dma_start(gates[:, 1, :], gate_rows(b, 2, 3).rearrange("p o d -> p (o d)")).then_inc(gates_loaded.sem, 16)
                if moe:
                    store(b - 1)

            every_batch(sp, lambda b: batch(b, False, True), lambda b: batch(b, True, True),
                        lambda b: batch(b, True, False))
            set_aside(LAST)
            store(LAST)
            sp.wait_ge(stored.sem, 32 * BATCH)

        @block.tensor
        def _(pe):
            mm = nc.tensor.matmul

            def fill_s(b, p, k):
                f = p * S_FILLS + k
                wait(pe, s_used, b, f - 1)
                bank = ps_s[:, f % 2, :]
                if k == S_FILLS - 1:
                    pe.wait_ge(m_ready.sem, m_ready.at(b, p + 1))
                    for t in range(TILES):
                        ins = nc.tensor.transpose(bank[:, t * P:(t + 1) * P], mt[:, t, :], idn[:])
                else:
                    r0 = STRIP * (k // 3)
                    for qt, at, n in (((3, 0, SEQ),), ((2, 0, 3 * P),), ((0, 0, 2 * P), (1, 2 * P, 2 * P)))[k % 3]:
                        ins = mm(bank[:, at:at + n], QT[r0:r0 + MROW, p, qt * P:(qt + 1) * P],
                                 KT[r0:r0 + MROW, p, 0:n], start=True, stop=True)
                ins.then_inc(s_filled.sem, 1)

            def fill_t(b, h, k):
                f = h * T_FILLS + k
                if k == 0 and h % 2 == 0:
                    pe.wait_ge(s_used.sem, s_used.at(b, (h // 2 + 1) * S_FILLS))
                wait(pe, exp_done, b, f - 1)
                if f < 2:
                    wait(pe, ct_ready, b - 1, 1)
                bank = ps_t[:, f % 2, :]
                r0, p = STRIP * (h % 2), h // 2
                for kt, at, q0 in (((0, 0, 0),), ((3, 2 * P, 2 * P), (1, 0, P)), ((2, 0, 2 * P),))[k]:
                    ins = mm(bank[:, at:at + SEQ - q0], KT[r0:r0 + STRIP, p, kt * P:(kt + 1) * P],
                             QT[r0:r0 + STRIP, p, q0:SEQ], start=True, stop=True)
                ins.then_inc(t_filled.sem, 1)

            def values(b, h):
                pe.wait_ge(masked.sem, masked.at(b, 2 * h + 2))
                pe.wait_ge(exp_done.sem, exp_done.at(b, T_FILLS * (h + 1)))
                if h == 0:
                    pe.wait_ge(v_ready.sem, v_ready.at(b, TILES))
                if h % OG == 0:
                    wait(pe, ot_ready, b, h // OG)
                r0 = 32 * (h % OG)
                for kt in range(TILES):
                    n = SEQ - kt * P
                    ins = mm(ps_o[r0:r0 + HD + 1, kt * P:SEQ], V[:, kt, h, :], probs[:, h % 2, KT_AT[kt]:KT_AT[kt] + n],
                             start=kt == 0, stop=kt == TILES - 1)
                ins.then_inc(pv_done.sem, 1)

            def gate_or_up(b, u, which):
                e, t0 = u % EXPERTS, HALF * (u // EXPERTS)
                n = 0
                for c in range(KC):
                    w0 = (KC * which + c) * INNER
                    for a, x_ in PRODUCTS:
                        n += 1
                        ins = mm(unit_banks(b, u)[which][:, 0:HALF], w_part[a][:, e, w0:w0 + INNER],
                                 h2_part[x_][:, c, t0:t0 + HALF], start=n == 1, stop=n == KC * len(PRODUCTS))
                ins.then_inc((g_done, u_done)[which].sem, 1)

            def gate(b, u):
                if u == 0:
                    pe.wait_ge(h2_low.sem, h2_low.at(b, KC))
                wait(pe, gw_done, b, bank_free(b, u))
                weight(b, u)
                gate_or_up(b, u, 0)

            def up(b, u):
                wait(pe, a_ready, b, bank_free(b, u))
                gate_or_up(b, u, 1)

            def weight(b, u):
                if u == 0:
                    pe.wait_ge(ct_ready.sem, ct_ready.at(b, 1))
                t0 = HALF * (u // EXPERTS)
                mm(unit_banks(b, u)[0][:, HALF:SEQ], pick_r[:, u % EXPERTS:u % EXPERTS + 1].broadcast_to([2 * EXPERTS, P]),
                   cT[:, t0:t0 + HALF], start=True, stop=True)

            def down(b, u):
                e = u % EXPERTS
                pe.wait_ge(a_low_done.sem, a_low_done.at(b, u + 1))
                if e == 0:
                    if u:
                        pe.wait_ge(y_ready.sem, y_ready.at(b, 1))
                    else:
                        wait(pe, y_ready, b - 1, 2)
                for t in range(2):
                    for n, (a, w) in enumerate(PRODUCTS):
                        ins = mm(ps_y[:, t * DIM:(t + 1) * DIM], a_part[a][:, u % 2, t * P:(t + 1) * P],
                                 w_part[w][:, e, 2 * KC * INNER:EXPERT_W], start=e == 0 and t == 0 and n == 0,
                                 stop=e == EXPERTS - 1 and n == len(PRODUCTS) - 1, skip_group_check=True)
                ins.then_inc(d_done.sem, 1)

            def unit(b, u):
                gate(b, u)
                up(b, u)
                if u >= 2:
                    down(b, u - 2)

            def h1_transposes(b):
                pe.wait_ge(ln1.sem, ln1.at(b, 4))
                for c in range(KC):
                    bank = ps_s[:, c, :]
                    for t in range(TILES):
                        ins = nc.tensor.transpose(bank[:, t * P:(t + 1) * P], x_in[:, t, c * P:(c + 1) * P], idn[:])
                    ins.then_inc(h1_tr.sem, 1)

            def attention(b, moe, more_batches):
                m = b - 1
                for p in range(PAIRS):
                    h0, h1, more = 2 * p, 2 * p + 1, p + 1 < PAIRS
                    u = after_pair(p)
                    if p == 0:
                        fill_s(b, 1, 0)
                        if moe:
                            gate(m, u[0])
                    fill_t(b, h0, 0)
                    if more:
                        fill_s(b, p + 1, 1)
                    if moe and p:
                        gate(m, u[0])
                    fill_t(b, h0, 1)
                    if more:
                        fill_s(b, p + 1, 2)
                    if moe:
                        up(m, u[0])
                    fill_t(b, h0, 2)
                    if more:
                        fill_s(b, p + 1, 3)
                    if p:
                        values(b, h0 - 1)
                    if moe and p:
                        down(m, u[0] - 2)
                    if more:
                        fill_s(b, p + 1, 4)
                    fill_t(b, h1, 0)
                    if more:
                        fill_s(b, p + 1, 5)
                    if moe:
                        gate(m, u[1])
                    fill_t(b, h1, 1)
                    if moe:
                        up(m, u[1])
                    if more:
                        fill_s(b, p + 1, 6)
                    fill_t(b, h1, 2)
                    if p + 2 < PAIRS:
                        fill_s(b, p + 2, 0)
                    values(b, h0)
                    if moe and p:
                        down(m, u[1] - 2)
                if more_batches:
                    pe.wait_ge(s_used.sem, s_used.at(b, PAIRS * S_FILLS))
                    h1_transposes(b + 1)
                values(b, HEADS - 1)

            def qkv(b, t):
                if t == 0:
                    pe.wait_ge(h1_ready.sem, h1_ready.at(b, KC))
                wait(pe, roped, b, t)
                wait(pe, v_ready, b, t)
                hT = [h1T[:, c, t * P:(t + 1) * P] for c in range(KC)]
                for c in range(KC):
                    mm(ps_s[:, 0, :], hT[c], w_qkv[:, c, 0:2 * DIM], start=c == 0, stop=c == KC - 1)
                at = (t % 2) * DIM
                for c in range(KC):
                    ins = mm(ps_s[:, 1, at:at + DIM], hT[c], w_qkv[:, c, 2 * DIM:3 * DIM], start=c == 0, stop=c == KC - 1)
                ins.then_inc(qkv_done.sem, 1)

            def stack(b, t, part):
                pe.wait_ge(rounded.sem, rounded.at(b, 2 * t + 2))
                pe.wait_ge(low_ready.sem, low_ready.at(b, t + 1))
                if t == 0:
                    pe.wait_ge(consts_set.sem, consts_set.at(b, 3))
                    wait(pe, o_tok_ready, b - 1, TILES)
                for k in (2 * part, 2 * part + 1):
                    f = 4 * t + k
                    if f >= 2:
                        wait(pe, stack_ready, b, f - 1)
                    bank, src = ps_t[:, f % 2, :], (QS, KS)[k // 2]
                    for j in range(4):
                        p = 4 * (k % 2) + j
                        ins = nc.tensor.transpose(
                            bank[:, j * P:(j + 1) * P], src[:, 2 * p:2 * p + 2, :].rearrange("p h r -> p (h r)"), idn[:])
                    ins.then_inc(stack_tr.sem, 1)

            def o_transposes(b, t):
                if t == 0:
                    pe.wait_ge(ot_ready.sem, ot_ready.at(b, HEADS // OG))
                    pe.wait_ge(exp_done.sem, exp_done.at(b, HEADS * T_FILLS))
                if t >= 2:
                    wait(pe, o_tok_ready, b, t - 1)
                for g in range(HEADS // OG):
                    ins = nc.tensor.transpose(ps_t[:, t % 2, g * P:(g + 1) * P], OT[:, g, t * P:(t + 1) * P], idn[:])
                ins.then_inc(o_tr.sem, 1)

            def on_transposes(b, f):
                pe.wait_ge(o_tok_ready.sem, o_tok_ready.at(b, 2 * f + 2))
                if f:
                    pe.wait_ge(ga_mul.sem, ga_mul.at(b, 1))
                for t in (2 * f, 2 * f + 1):
                    for c in range(KC):
                        at = (t % 2) * DIM + c * P
                        ins = nc.tensor.transpose(ps_o[:, at:at + P], o_tok[:, t, c * P:(c + 1) * P], idn[:])
                    if t % 2:
                        ins.then_inc(on_tr.sem, 1)

            def project(b, f):
                pe.wait_ge(on_ready.sem, on_ready.at(b, f + 1))
                for t in (2 * f, 2 * f + 1):
                    for c in range(KC):
                        ins = mm(ps_o[:, (t % 2) * DIM:(t % 2 + 1) * DIM], onT[:, c, t * P:(t + 1) * P],
                                 w_proj[:, c, :], start=c == 0, stop=c == KC - 1)
                ins.then_inc(proj_done.sem, 1)

            def h2_transposes(b, c):
                if c == 0:
                    pe.wait_ge(ln2.sem, ln2.at(b, 4))
                wait(pe, h2_ready, b, c)
                for t in range(TILES):
                    ins = nc.tensor.transpose(ps_o[:, t * P:(t + 1) * P], x_in[:, t, c * P:(c + 1) * P], idn[:])
                ins.then_inc(h2_tr.sem, 1)

            def logits(b):
                pe.wait_ge(h2_ready.sem, h2_ready.at(b, KC))
                for t in range(TILES):
                    for c in range(KC):
                        ins = mm(ps_o[:, t * EXPERTS:(t + 1) * EXPERTS], h2T[:, c, t * P:(t + 1) * P],
                                 w_router[:, c, :], start=c == 0, stop=c == KC - 1)
                ins.then_inc(logits_done.sem, 1)

            def weight_transposes(b):
                pe.wait_ge(router.sem, router.at(b, ROUTER_STEPS))
                for t in range(TILES):
                    ins = nc.tensor.transpose(ps_o[0:2 * EXPERTS, t * P:(t + 1) * P], cs[:, t, :], idn[:])
                ins.then_inc(c_tr.sem, 1)

            def tail(b, moe, more):
                n, m = b + 1, b - 1

                def tail_unit(u):
                    if moe:
                        unit(m, UNITS - IN_TAIL + u)

                tail_unit(0)
                o_transposes(b, 0)
                o_transposes(b, 1)
                if more:
                    qkv(n, 0)
                tail_unit(1)
                o_transposes(b, 2)
                o_transposes(b, 3)
                tail_unit(2)
                if more:
                    qkv(n, 1)
                on_transposes(b, 0)
                tail_unit(3)
                project(b, 0)
                if more:
                    stack(n, 0, 0)
                tail_unit(4)
                if more:
                    stack(n, 0, 1)
                on_transposes(b, 1)
                tail_unit(5)
                project(b, 1)
                if more:
                    qkv(n, 2)
                tail_unit(6)
                if more:
                    stack(n, 1, 0)
                tail_unit(7)
                if more:
                    stack(n, 1, 1)
                    qkv(n, 3)
                tail_unit(8)
                h2_transposes(b, 0)
                if more:
                    stack(n, 2, 0)
                tail_unit(9)
                h2_transposes(b, 1)
                if more:
                    stack(n, 2, 1)
                logits(b)
                tail_unit(10)
                if more:
                    stack(n, 3, 0)
                tail_unit(11)
                if more:
                    stack(n, 3, 1)
                tail_unit(12)
                if more:
                    pe.wait_ge(stack_ready.sem, stack_ready.at(n, 4 * TILES))
                    fill_s(n, 0, 0)
                tail_unit(13)
                if more:
                    fill_s(n, 0, 1)
                tail_unit(14)
                if more:
                    fill_s(n, 0, 2)
                    fill_s(n, 0, 3)
                tail_unit(15)
                if more:
                    fill_s(n, 0, 4)
                    fill_s(n, 0, 5)
                if moe:
                    down(m, UNITS - 2)
                weight_transposes(b)
                if more:
                    fill_s(n, 0, 6)
                if moe:
                    down(m, UNITS - 1)

            pe.wait_ge(consts_in.sem, 96)
            h1_transposes(0)
            pe.wait_ge(mod_in.sem, 64)
            pe.wait_ge(setup_v.sem, 3)
            scT = c_s.rearrange("p (c b) -> p c b", c=KC)
            for i, (a, col) in enumerate([(1, 0), (1, 1), (0, 0), (0, 1), (4, 0), (4, 1), (3, 0), (3, 1)]):
                for c in range(KC):
                    ins = mm(ps_u[:, i * BATCH:(i + 1) * BATCH], w_mod[c][:, a * DIM + col * P:a * DIM + (col + 1) * P],
                             scT[:, c, :], start=c == 0, stop=c == KC - 1)
            ins.then_inc(setup_t.sem, 1)
            pe.wait_ge(o_cleared.sem, 1)
            for i, a in enumerate((2, 5)):
                for c in range(KC):
                    ins = mm(ps_o[0:BATCH, i * DIM:(i + 1) * DIM], scT[:, c, :], w_mod[c][:, a * DIM:(a + 1) * DIM],
                             start=c == 0, stop=c == KC - 1)
            ins.then_inc(setup_t.sem, 1)
            pe.wait_ge(weights_in.sem, 48)
            for t in range(TILES + 1):
                if t < TILES:
                    qkv(0, t)
                if t:
                    stack(0, t - 1, 0)
                    stack(0, t - 1, 1)
            pe.wait_ge(stack_ready.sem, stack_ready.at(0, 4 * TILES))
            for k in range(S_FILLS):
                fill_s(0, 0, k)
            pe.wait_ge(setup_v.sem, 11)

            def batch(b, moe, more):
                attention(b, moe, more)
                tail(b, moe, more)

            every_batch(pe, lambda b: batch(b, False, True), lambda b: batch(b, True, True),
                        lambda b: batch(b, True, False))
            pe.wait_ge(s_used.sem, s_used.at(LAST, PAIRS * S_FILLS))
            for u in range(UNITS):
                unit(LAST, u)
            down(LAST, UNITS - 2)
            down(LAST, UNITS - 1)

        @block.scalar
        def _(ac):
            def copy(dst, src):
                return nc.scalar.activation(dst, src, ACT.Copy)

            def exps(b, h, k):
                f = h * T_FILLS + k
                ac.wait_ge(t_filled.sem, t_filled.at(b, f + 1))
                if k == 0:
                    wait(ac, pv_done, b, h - 1)
                if f == 0:
                    wait(ac, h2_low, b - 1, KC)
                at, n = ((0, SEQ), (SEQ, SEQ), (2 * SEQ, 2 * P))[k]
                nc.scalar.activation(probs[:, h % 2, at:at + n], ps_t[:, f % 2, 0:n], ACT.Exp, scale=SCALE)\
                    .then_inc(exp_done.sem, 1)

            def high(b, u):
                ac.wait_ge(a_ready.sem, a_ready.at(b, u + 1))
                if u >= 2:
                    wait(ac, d_done, b, u - 1)
                else:
                    wait(ac, d_done, b - 1, UNITS)
                copy(a_part[0][:, u % 2, :], act[:, u % 2, :]).then_inc(a_high_done.sem, 1)

            def tanh(b, u):
                ac.wait_ge(g_done.sem, g_done.at(b, u + 1))
                if u >= 2:
                    wait(ac, a_low_done, b, u - 1)
                else:
                    wait(ac, a_low_done, b - 1, UNITS)
                nc.scalar.activation(act[:, u % 2, :], unit_banks(b, u)[0][:, 0:HALF], ACT.Tanh, scale=0.5).then_inc(tanh_done.sem, 1)

            def unit(b, u):
                if u:
                    high(b, u - 1)
                tanh(b, u)

            def o_out(b, g):
                ac.wait_ge(pv_done.sem, pv_done.at(b, OG * (g + 1)))
                ac.wait_ge(stack_tr.sem, stack_tr.at(b, 4 * TILES))
                copy(OT[:, g, :], ps_o[:]).then_inc(ot_ready.sem, 1)

            def split_weights(e):
                ac.wait_ge(expert_in[e % 2].sem, 16 * (e // 2 + 1))
                copy(w_part[0][:, e, :], stage[e % 2]).then_inc(w_high_done.sem, 1)

            def attention(b, moe):
                m = b - 1
                for p in range(PAIRS):
                    u = after_pair(p)
                    exps(b, 2 * p, 0)
                    if moe:
                        unit(m, u[0])
                    else:
                        split_weights(u[0])
                    exps(b, 2 * p, 1)
                    exps(b, 2 * p, 2)
                    if p and (2 * p - 1) % OG == OG - 1:
                        o_out(b, (2 * p - 1) // OG)
                    exps(b, 2 * p + 1, 0)
                    if moe:
                        unit(m, u[1])
                    else:
                        split_weights(u[1])
                    exps(b, 2 * p + 1, 1)
                    exps(b, 2 * p + 1, 2)
                o_out(b, HEADS // OG - 1)

            def h1_out(b, c):
                if c == 0:
                    ac.wait_ge(mod_a.sem, mod_a.at(b, 1))
                    wait(ac, pv_done, b - 1, HEADS)
                ac.wait_ge(h1_tr.sem, h1_tr.at(b, c + 1))
                nc.scalar.activation(h1T[:, c, :], ps_s[:, c, :], ACT.Identity,
                                     scale=modA[:, c:c + 1], bias=modA[:, 2 + c:3 + c]).then_inc(h1_ready.sem, 1)

            def v_out(b, t):
                ac.wait_ge(qkv_done.sem, qkv_done.at(b, t + 1))
                wait(ac, pv_done, b - 1, HEADS)
                copy(V[:, t, :, 0:HD], ps_s[:, 1, (t % 2) * DIM:(t % 2 + 1) * DIM].rearrange("p (h d) -> p h d", d=HD))\
                    .then_inc(v_ready.sem, 1)

            def round_qk(b, t):
                ac.wait_ge(rope_sum.sem, rope_sum.at(b, t + 1))
                wait(ac, stack_tr, b, 4 * t)
                if t == 0:
                    wait(ac, o_tr, b - 1, TILES)
                src = work[:, 0, :].rearrange("p (s h d) -> p s h d", s=2, d=HD)
                for i, (dst, step) in enumerate(((QS, 2), (KS, 1))):
                    view = dst[:, :, 0:MROW].rearrange("p h (s d) -> p s h d", d=HD)[:, 0:step + 1:step]
                    nc.scalar.activation(view.bitcast(F32R), src[:, i:i + 1].broadcast_to([P, 2, HEADS, HD]), ACT.Copy)\
                        .then_inc(rounded.sem, 1)

            def stack_out(b, t, part):
                for k in (2 * part, 2 * part + 1):
                    f = 4 * t + k
                    ac.wait_ge(stack_tr.sem, stack_tr.at(b, f + 1))
                    if t == 0 and k == 0:
                        wait(ac, t_filled, b - 1, HEADS * T_FILLS)
                    dst = (QT, KT)[k // 2][:, 4 * (k % 2):4 * (k % 2) + 4, t * P:(t + 1) * P]
                    copy(dst, ps_t[:, f % 2, :].rearrange("p (j n) -> p j n", j=4)).then_inc(stack_ready.sem, 1)

            def on_out(b, f):
                ac.wait_ge(on_tr.sem, on_tr.at(b, f + 1))
                src = ps_o[:].rearrange("p (t c n) -> p c t n", t=2, c=KC)
                dst = onT[:, :, 2 * f * P:(2 * f + 2) * P].rearrange("p c (t n) -> p c t n", t=2)
                copy(dst, src).then_inc(on_ready.sem, 1)

            def h2_out(b, c):
                if c == 0:
                    ac.wait_ge(mod_b.sem, mod_b.at(b, 1))
                    ac.wait_ge(proj_done.sem, proj_done.at(b, 2))
                ac.wait_ge(h2_tr.sem, h2_tr.at(b, c + 1))
                nc.scalar.activation(h2T[:, c, :], ps_o[:], ACT.Identity,
                                     scale=modB[:, c:c + 1], bias=modB[:, 2 + c:3 + c]).then_inc(h2_ready.sem, 1)

            def h2_round(b):
                ac.wait_ge(h2_ready.sem, h2_ready.at(b, KC))
                wait(ac, u_done, b - 1, UNITS)
                for c in range(KC):
                    copy(h2_part[0][:, c, :], h2T[:, c, :]).then_inc(h2_high.sem, 1)

            def tail(b, moe, more):
                n, m = b + 1, b - 1

                def tail_high(u):
                    if moe:
                        high(m, UNITS - IN_TAIL + u)

                def tail_tanh(u):
                    if moe:
                        tanh(m, UNITS - IN_TAIL + u)

                tail_high(-1)
                if more:
                    h1_out(n, 0)
                tail_tanh(0)
                if more:
                    h1_out(n, 1)
                tail_high(0)
                tail_tanh(1)
                if more:
                    v_out(n, 0)
                tail_high(1)
                tail_tanh(2)
                tail_high(2)
                on_out(b, 0)
                if more:
                    round_qk(n, 0)
                tail_tanh(3)
                if more:
                    v_out(n, 1)
                tail_high(3)
                if more:
                    stack_out(n, 0, 0)
                tail_tanh(4)
                if more:
                    stack_out(n, 0, 1)
                tail_high(4)
                on_out(b, 1)
                if more:
                    round_qk(n, 1)
                tail_tanh(5)
                tail_high(5)
                tail_tanh(6)
                if more:
                    v_out(n, 2)
                tail_high(6)
                if more:
                    stack_out(n, 1, 0)
                tail_tanh(7)
                if more:
                    stack_out(n, 1, 1)
                tail_high(7)
                if more:
                    round_qk(n, 2)
                tail_tanh(8)
                if more:
                    v_out(n, 3)
                tail_high(8)
                h2_out(b, 0)
                if more:
                    stack_out(n, 2, 0)
                tail_tanh(9)
                h2_out(b, 1)
                if more:
                    stack_out(n, 2, 1)
                tail_high(9)
                if more:
                    round_qk(n, 3)
                ac.wait_ge(logits_done.sem, logits_done.at(b, 1))
                nc.scalar.activation(R[:, 15, :], ps_o[:, 0:TILES * EXPERTS], ACT.Exp, scale=-1.0)\
                    .then_inc(rexp_done.sem, 1)
                tail_tanh(10)
                tail_high(10)
                if more:
                    stack_out(n, 3, 0)
                tail_tanh(11)
                if more:
                    stack_out(n, 3, 1)
                for u in range(12, IN_TAIL):
                    tail_high(u - 1)
                    tail_tanh(u)
                h2_round(b)
                tail_high(IN_TAIL - 1)
                ac.wait_ge(c_tr.sem, c_tr.at(b, 1))
                wait(ac, g_done, b - 1, UNITS)
                copy(cT[:], ps_o[0:2 * EXPERTS, :]).then_inc(ct_ready.sem, 1)

            ac.wait_ge(mod_in.sem, 64)
            nc.scalar.activation(c_e, c_sb, ACT.Exp, scale=-1.0).then_inc(setup_a.sem, 1)
            ac.wait_ge(setup_p.sem, 5)
            ac.wait_ge(setup_t.sem, 2)
            h1_out(0, 0)
            h1_out(0, 1)
            v_out(0, 0)
            for t in range(TILES):
                round_qk(0, t)
                if t + 1 < TILES:
                    v_out(0, t + 1)
                stack_out(0, t, 0)
                stack_out(0, t, 1)
            ac.wait_ge(gates_out.sem, 16)

            def batch(b, moe, more):
                attention(b, moe)
                tail(b, moe, more)

            every_batch(ac, lambda b: batch(b, False, True), lambda b: batch(b, True, True),
                        lambda b: batch(b, True, False))
            for u in range(UNITS):
                unit(LAST, u)
            high(LAST, UNITS - 1)

        @block.vector
        def _(ve):
            tt, ts, stt = nc.vector.tensor_tensor, nc.vector.tensor_scalar, nc.vector.scalar_tensor_tensor

            def row_max(b, p, k):
                f = p * S_FILLS + k
                wait_apart(ve, s_filled, b, f + 1, ve_passed)
                h = 2 * p + k // 3
                for qt, at in (((3, 0),), ((2, 0),), ((0, 0), (1, 2 * P)))[k % 3]:
                    n = (qt + 1) * P
                    ins = nc.vector.tensor_tensor_reduce(
                        out=ps_s[:, f % 2, at:at + n], in0=ps_s[:, f % 2, at:at + n], in1=mask[:, SEQ - n:SEQ], scale=1.0,
                        scalar=-3.0e38, op0=ALU.add, op1=ALU.max, accum_out=mmax[:, h, qt:qt + 1])
                ins.then_inc(s_used.sem, 1)

            def maxima(b, p):
                ve.wait_ge(s_used.sem, s_used.at(b, p * S_FILLS + 6))
                wait(ve, s_filled, b, p * S_FILLS)
                src = mmax[:, 2 * p:2 * p + 2, :]
                dst = mt[:, :, :].rearrange("p t (h r) -> p h t r", h=2)
                high, low = dst[:, :, :, MROW:MROW + 1], dst[:, :, :, MROW + 1:MROW + 2]
                src = src.unsqueeze(3)
                ts(high.bitcast(F32R), src, -1.0, None, ALU.mult).then_inc(m_high.sem, 1)
                ve.wait_ge(m_high.sem, m_high.at(b, p + 1))
                stt(out=low.bitcast(F32R).rearrange("p h t o -> p h (t o)"), in0=src.rearrange("p h t o -> p h (t o)"),
                    scalar=-1.0, in1=high.rearrange("p h t o -> p h (t o)"), op0=ALU.mult, op1=ALU.subtract)\
                    .then_inc(m_ready.sem, 1)

            def maxima_in(b, p):
                f = p * S_FILLS + S_FILLS - 1
                ve.wait_ge(s_filled.sem, s_filled.at(b, f + 1))
                tt(QT[:, p, :], ps_s[:, f % 2, :], QT[:, p, :].bitcast(F32), ALU.add).then_inc(s_used.sem, 1)

            def gate_tanh(b, u):
                ve.wait_ge(tanh_done.sem, tanh_done.at(b, u + 1))
                buf = act[:, u % 2, :]
                stt(out=buf, in0=buf, scalar=1.0, in1=unit_banks(b, u)[0][:, 0:HALF], op0=ALU.add, op1=ALU.mult)\
                    .then_inc(gt_done.sem, 1)

            def weigh(b, u):
                ve.wait_ge(gt_done.sem, gt_done.at(b, u + 1))
                buf = act[:, u % 2, :]
                tt(buf, buf, unit_banks(b, u)[0][:, HALF:SEQ], ALU.mult).then_inc(gw_done.sem, 1)

            def gate_up(b, u):
                ve.wait_ge(u_done.sem, u_done.at(b, u + 1))
                ve.wait_ge(gw_done.sem, gw_done.at(b, u + 1))
                buf = act[:, u % 2, :]
                tt(buf, buf, unit_banks(b, u)[1][:, 0:HALF], ALU.mult).then_inc(a_ready.sem, 1)
                if u == EXPERTS + 1:
                    scaled(b, 0)

            def unit(b, u):
                gate_tanh(b, u)
                weigh(b, u)
                gate_up(b, u)

            def scaled(b, f):
                ve.wait_ge(d_done.sem, d_done.at(b, EXPERTS * (f + 1)))
                if f == 0:
                    ve.wait_ge(gateb_loaded.sem, gateb_loaded.at(b, 16))
                    wait(ve, out_ready, b - 1, 2)
                else:
                    ve.wait_ge(out_ready.sem, out_ready.at(b, 1))
                tt(y_sb[:, :].rearrange("p (t d) -> p t d", t=2), ps_y[:].rearrange("p (t d) -> p t d", t=2),
                   gate_b[:, :].unsqueeze(1).broadcast_to([P, 2, DIM]), ALU.mult).then_inc(y_ready.sem, 1)

            def norm(b, src, dst, sig, rs, first):
                if first:
                    for t in range(TILES):
                        ins = nc.vector.bn_stats(stats[:, t, :], src[:, t, :])
                    ins.then_inc(sig.sem, 1)
                    wait_apart(ve, sig, b, 1, ve_passed)
                    for t in range(TILES):
                        ins = nc.vector.bn_aggr(mv[:, t, :], stats[:, t, :])
                    ins.then_inc(sig.sem, 1)
                    ve.wait_ge(sig.sem, sig.at(b, 2))
                    ts(vare[:], mv[:, :, 1], EPS, None, ALU.add).then_inc(sig.sem, 1)
                else:
                    ve.wait_ge(rs.sem, rs.at(b, 1))
                    for t in range(TILES):
                        ins = ts(dst[:, t, :], src[:, t, :], mv[:, t, 0:1], rstd[:, t:t + 1], ALU.subtract, ALU.mult)
                    ins.then_inc(sig.sem, 1)

            def norm1(b, first):
                if first:
                    ve.wait_ge(x_loaded.sem, x_loaded.at(b, 16))
                    wait(ve, rstd2, b - 2, 1)
                norm(b, x_in, x_in, ln1, rstd1, first)

            def attention(b, moe, more):
                m = b - 1

                def reds(*ks):
                    if p + 1 < PAIRS:
                        for k in ks:
                            row_max(b, p + 1, k)
                for p in range(PAIRS):
                    u = after_pair(p)
                    reds(0, 1)
                    if moe:
                        gate_tanh(m, u[0])
                    reds(2, 3)
                    if moe:
                        weigh(m, u[0])
                    reds(4)
                    if moe:
                        gate_up(m, u[0])
                    reds(5)
                    if p + 1 < PAIRS:
                        maxima(b, p + 1)
                    if moe:
                        gate_tanh(m, u[1])
                        weigh(m, u[1])
                    if p + 1 < PAIRS:
                        maxima_in(b, p + 1)
                    if moe:
                        gate_up(m, u[1])
                    if more and p == 2:
                        norm1(b + 1, True)
                    if more and p == 4:
                        norm1(b + 1, False)
                    if more and p == 5:
                        ve.wait_ge(h1_ready.sem, h1_ready.at(b, KC))
                        nc.vector.tensor_copy(modA[:], mods_of(b + 1, 0)).then_inc(mod_a.sem, 1)
                    if p == 5:
                        wait(ve, h2_ready, b - 1, KC)
                        nc.vector.tensor_copy(modB[:], mods_of(b, 4)).then_inc(mod_b.sem, 1)

            def mods_of(b, lo):
                if isinstance(b, int):
                    return mods[:, b, lo:lo + 4]
                return mods[:, bass.ds(b, 1), lo:lo + 4].rearrange("p o n -> p (o n)")

            def o_token(b, t):
                ve.wait_ge(o_tr.sem, o_tr.at(b, t + 1))
                wait(ve, on_tr, b - 1, 2)
                src = ps_t[:, t % 2, :].rearrange("p (h r) -> p h r", r=32)
                nc.vector.reciprocal(lin[:, t % 2, :].unsqueeze(2), src[:, :, HD:HD + 1]).then_inc(linv.sem, 1)
                ve.wait_ge(linv.sem, linv.at(b, t + 1))
                tt(o_tok[:, t, :].rearrange("p (h d) -> p h d", d=HD), src[:, :, 0:HD],
                   lin[:, t % 2, :].unsqueeze(2).broadcast_to([P, HEADS, HD]), ALU.mult).then_inc(o_tok_ready.sem, 1)

            def rope(b, t):
                ve.wait_ge(qkv_done.sem, qkv_done.at(b, t + 1))
                wait(ve, low_ready, b, t)
                wait(ve, rounded, b, 2 * t)
                wait(ve, rope_sum, b, t)
                src = ps_s[:, 0, :].rearrange("p (h s d) -> p h s d", s=2, d=HD // 2)
                c = work[:, 1, :].rearrange("p (h s d) -> p h s d", s=2, d=HD // 2)
                full = [P, 2 * HEADS, 2, HD // 2]
                tt(work[:, 0, :].rearrange("p (g d) -> p g d", d=HD // 2),
                   ps_s[:, 0, :].rearrange("p (g d) -> p g d", d=HD // 2),
                   cos_t[:, t:t + 1, :].broadcast_to([P, 4 * HEADS, HD // 2]), ALU.mult)
                tt(c, src[:, :, ::-1, :], sin_t[:, t:t + 1, :, :].broadcast_to(full), ALU.mult).then_inc(roped.sem, 1)

            def low_qk(b, t):
                ve.wait_ge(rounded.sem, rounded.at(b, 2 * t + 2))
                src = work[:, 0, :].rearrange("p (s h d) -> p s h d", s=2, d=HD)
                tt(QS[:, :, HD:2 * HD].bitcast(F32R), src[:, 0], QS[:, :, 0:HD], ALU.subtract)
                tt(KS[:, :, 2 * HD:3 * HD].bitcast(F32R), src[:, 1], KS[:, :, 0:HD], ALU.subtract)\
                    .then_inc(low_ready.sem, 1)

            def residual(b, f):
                view = x1[:, 2 * f:2 * f + 2, :]
                if f == 0:
                    ve.wait_ge(xres_loaded.sem, xres_loaded.at(b, 16))
                    ve.wait_ge(gates_loaded.sem, gates_loaded.at(b, 32))
                t1 = y_sb[:, :].rearrange("p (t d) -> p t d", t=2)
                tt(view, view, gates[:, 1:2, :].broadcast_to([P, 2, DIM]), ALU.add).then_inc(xg_add.sem, 1)
                ve.wait_ge(proj_done.sem, proj_done.at(b, f + 1))
                wait(ve, x1_ready, b, f)
                wait(ve, out_ready, b - 1, 1)
                tt(t1, ps_o[:].rearrange("p (t d) -> p t d", t=2), gates[:, 0:1, :].broadcast_to([P, 2, DIM]),
                   ALU.mult).then_inc(ga_mul.sem, 1)
                ve.wait_ge(ga_mul.sem, ga_mul.at(b, f + 1))
                ve.wait_ge(xg_add.sem, xg_add.at(b, f + 1))
                tt(view, view, t1, ALU.add).then_inc(x1_ready.sem, 1)

            def route(b, *steps):
                G = GROUPS
                r = [R[:, i, :] for i in range(16)]
                te = lambda i: R[:, i, :].rearrange("p (t e) -> p t e", t=TILES)
                by_group = lambda i: R[:, i, :].rearrange("p (x o) -> p x o", o=G)
                c4 = lambda i: R[:, i, :].rearrange("p (t g o) -> p t g o", t=TILES, g=G)
                pairs = r[3].rearrange("p (g a c) -> p g a c", a=2, c=2)
                hi = r[4][:, 0:32].rearrange("p (g c) -> p g c", c=2)
                lo = r[5][:, 0:32].rearrange("p (g c) -> p g c", c=2)
                one, two, three = (r[6][:, 16 * i:16 * i + 16].unsqueeze(2) for i in range(3))
                second, best_two = r[7][:, 0:16].unsqueeze(2), r[7][:, 16:32]
                own = best_two.rearrange("p (t g) -> p t g", t=TILES)
                other = own.unsqueeze(2).broadcast_to([P, TILES, G, G])
                own = own.unsqueeze(3).broadcast_to([P, TILES, G, G])
                rank, chosen, penalty = (r[12][:, 16 * i:16 * i + 16] for i in range(3))
                to_experts = lambda a: a.unsqueeze(2).broadcast_to([P, 16, G])
                sums, scaled_sums, factor = (r[13][:, 4 * i:4 * i + 4] for i in range(3))
                tiles = range(TILES)
                at = lambda i, t: R[:, i, t * EXPERTS:(t + 1) * EXPERTS]
                for k in steps:
                    if k == 0:
                        ve.wait_ge(rexp_done.sem, rexp_done.at(b, 1))
                    elif k in (14, 16):
                        wait_apart(ve, router, b, k, ve_passed)
                    else:
                        wait(ve, router, b, k)
                    if k == 0:
                        ins = ts(r[1], r[15], 1.0, None, ALU.add)
                    elif k == 1:
                        ins = nc.vector.reciprocal(r[2], r[1])
                    elif k == 2:
                        ins = tt(te(3), te(2), rb[:, :].unsqueeze(1).broadcast_to([P, TILES, EXPERTS]), ALU.add)
                    elif k == 3:
                        tt(hi, pairs[:, :, 0, :], pairs[:, :, 1, :], ALU.max)
                        ins = tt(lo, pairs[:, :, 0, :], pairs[:, :, 1, :], ALU.min)
                    elif k == 4:
                        tt(one, hi[:, :, 0:1], hi[:, :, 1:2], ALU.max)
                        tt(two, hi[:, :, 0:1], hi[:, :, 1:2], ALU.min)
                        ins = tt(three, lo[:, :, 0:1], lo[:, :, 1:2], ALU.max)
                    elif k == 5:
                        ins = tt(second, two, three, ALU.max)
                    elif k == 6:
                        ins = tt(best_two.unsqueeze(2), one, second, ALU.add)
                    elif k == 7:
                        tt(c4(8), other, own, ALU.is_gt)
                        ins = tt(c4(9), other, own, ALU.is_equal)
                    elif k == 8:
                        ins = tt(c4(10), c4(9), before[:, :].rearrange("p (t g o) -> p t g o", t=TILES, g=G), ALU.mult)
                    elif k == 9:
                        ins = tt(r[11], r[8], r[10], ALU.add)
                    elif k == 10:
                        ins = nc.vector.reduce_sum(rank.unsqueeze(2), by_group(11), AX_X)
                    elif k == 11:
                        ins = ts(chosen, rank, float(TOP_GROUPS), None, ALU.is_lt)
                    elif k == 12:
                        ts(penalty, chosen, -1.0, -NEG, ALU.add, ALU.mult)
                        ins = tt(by_group(4), by_group(3), to_experts(chosen), ALU.mult)
                    elif k == 13:
                        ins = tt(by_group(5), by_group(4), to_experts(penalty), ALU.add)
                    elif k == 14:
                        for t in tiles:
                            ins = nc.vector.max(m8[:, t, :], at(5, t))
                    elif k == 15:
                        ins = nc.vector.tensor_copy(top4[:, :, 0:TOP_K], m8[:, :, 0:TOP_K])
                    elif k == 16:
                        for t in tiles:
                            ins = nc.vector.match_replace(at(6, t), top4[:, t, :], at(5, t), NEG)
                    elif k == 17:
                        ins = tt(r[11], r[6], r[5], ALU.not_equal)
                    elif k == 18:
                        ins = tt(r[14], r[11], r[2], ALU.mult)
                    elif k == 19:
                        ins = nc.vector.reduce_sum(sums.unsqueeze(2), te(14), AX_X)
                    elif k == 20:
                        ins = ts(scaled_sums, sums, 1e-20, 2 / ROUTED_SCALE, ALU.add, ALU.mult)
                    elif k == 21:
                        ins = nc.vector.reciprocal(factor, scaled_sums)
                    elif k == 22:
                        ins = tt(te(15), te(14), factor.unsqueeze(2).broadcast_to([P, TILES, EXPERTS]), ALU.mult)
                    elif k == 23:
                        ins = nc.vector.tensor_copy(cs[:, :, 0:EXPERTS].bitcast(F32R), te(15))
                    else:
                        ins = tt(cs[:, :, EXPERTS:2 * EXPERTS].bitcast(F32R), te(15), cs[:, :, 0:EXPERTS], ALU.subtract)
                    ins.then_inc(router.sem, 1)

            def tail(b, moe, more):
                n, m = b + 1, b - 1

                def units(*us):
                    if moe:
                        for u in us:
                            unit(m, UNITS - IN_TAIL + u)

                units(0)
                o_token(b, 0)
                o_token(b, 1)
                units(1)
                if more:
                    rope(n, 0)
                o_token(b, 2)
                o_token(b, 3)
                units(2)
                if more:
                    low_qk(n, 0)
                units(3)
                if more:
                    rope(n, 1)
                residual(b, 0)
                units(4)
                if more:
                    low_qk(n, 1)
                units(5)
                residual(b, 1)
                ve.wait_ge(x1_ready.sem, x1_ready.at(b, 2))
                units(6)
                if more:
                    rope(n, 2)
                norm(b, x1, x_in, ln2, rstd2, True)
                units(7)
                norm(b, x1, x_in, ln2, rstd2, False)
                if more:
                    low_qk(n, 2)
                units(8)
                if more:
                    rope(n, 3)
                units(9)
                if more:
                    low_qk(n, 3)

                def routed_unit(u, *steps):
                    v = UNITS - IN_TAIL + u
                    route(b, *steps[:-3])
                    if moe:
                        gate_tanh(m, v)
                    route(b, steps[-3])
                    if moe:
                        weigh(m, v)
                    route(b, steps[-2])
                    if moe:
                        gate_up(m, v)
                    route(b, steps[-1])

                routed_unit(10, 0, 1, 2, 3, 4)
                routed_unit(11, 5, 6, 7, 8, 9, 10)
                routed_unit(12, 11, 12, 13, 14, 15)
                if more:
                    row_max(n, 0, 0)
                routed_unit(13, 16, 17, 18)
                if more:
                    row_max(n, 0, 1)
                routed_unit(14, 19, 20, 21)
                if more:
                    row_max(n, 0, 2)
                    row_max(n, 0, 3)
                routed_unit(15, 22, 23, 24)
                if more:
                    for k in range(4, S_FILLS - 1):
                        row_max(n, 0, k)
                    maxima(n, 0)
                    maxima_in(n, 0)
                if moe:
                    scaled(m, 1)

            nc.vector.memset(ps_o[:], 0.0).then_inc(o_cleared.sem, 1)
            norm1(0, True)
            ve.wait_ge(setup_a.sem, 1)
            ts(c_d, c_e, 1.0, None, ALU.add).then_inc(setup_v.sem, 1)
            ve.wait_ge(setup_v.sem, 1)
            nc.vector.reciprocal(c_r, c_d).then_inc(setup_v.sem, 1)
            ve.wait_ge(setup_v.sem, 2)
            tt(c_s, c_r, c_sb, ALU.mult).then_inc(setup_v.sem, 1)
            norm1(0, False)
            ve.wait_ge(setup_t.sem, 1)
            src = ps_u[:, 0:8 * BATCH].rearrange("p (i b) -> p b i", i=8)
            for i, add in enumerate((1.0, 0.0, 1.0, 0.0)):
                ins = ts(mods[:, :, 2 * i:2 * i + 2], src[:, :, 2 * i:2 * i + 2], add, None, ALU.add)
            ins.then_inc(setup_v.sem, 1)
            ve.wait_ge(setup_v.sem, 4)
            nc.vector.tensor_copy(modA[:], mods[:, 0, 0:4]).then_inc(mod_a.sem, 1)
            ve.wait_ge(setup_t.sem, 2)
            ts(g16, ps_o[0:BATCH, :], 0.0, 2.0, ALU.is_ge, ALU.mult).then_inc(setup_v.sem, 1)
            ve.wait_ge(setup_v.sem, 5)
            ts(g16, g16, -1.0, None, ALU.add).then_inc(setup_v.sem, 1)
            ts(sg16, ps_o[0:BATCH, :], -1.0, None, ALU.mult).then_inc(setup_v.sem, 1)
            ve.wait_ge(setup_v.sem, 7)
            stt(out=sg16, in0=sg16, scalar=0.25, in1=ps_o[0:BATCH, :], op0=ALU.max, op1=ALU.max).then_inc(setup_v.sem, 1)
            ve.wait_ge(setup_v.sem, 8)
            tt(gfin[:, 0:2, :].rearrange("p t n -> p (t n)"), g16, sg16, ALU.mult).then_inc(setup_v.sem, 1)
            ve.wait_ge(setup_v.sem, 9)
            tt(gfin[:, 2, :], gfin[:, 0, :], b16, ALU.mult).then_inc(setup_v.sem, 1)
            ve.wait_ge(consts_in.sem, 96)
            ve.wait_ge(setup_v.sem, 10)
            nc.vector.tensor_copy(pick_r[:], pick_f[:]).then_inc(setup_v.sem, 1)
            nc.vector.memset(top4[:], NEG).then_inc(setup_v.sem, 1)
            ve.wait_ge(setup_v.sem, 12)
            ve.wait_ge(setup_p.sem, 5)
            for t in range(TILES):
                rope(0, t)
                low_qk(0, t)
            for k in range(S_FILLS - 1):
                row_max(0, 0, k)
            maxima(0, 0)
            maxima_in(0, 0)

            def batch(b, moe, more):
                attention(b, moe, more)
                tail(b, moe, more)

            every_batch(ve, lambda b: batch(b, False, True), lambda b: batch(b, True, True),
                        lambda b: batch(b, True, False))
            for u in range(UNITS):
                unit(LAST, u)
            scaled(LAST, 1)

        @block.gpsimd
        def _(po):
            def mask_probs(b, h):
                wait_apart(po, exp_done, b, T_FILLS * (h + 1), po_passed)
                buf = probs[:, h % 2, :]
                a = bass.AP(buf.tensor, buf.offset, [buf.ap[0], [SEQ, 3], [1, P]])
                po.affine_select(out=a, in_=a, compare_op=ALU.is_ge, fill=0.0, base=0,
                                 pattern=[[0, 3], [1, P]], channel_multiplier=-1).then_inc(masked.sem, 1)
                d = probs[:, h % 2, KT_AT[3]:KT_AT[3] + P]
                po.affine_select(out=d, in_=d, compare_op=ALU.is_ge, fill=0.0, base=0,
                                 pattern=[[1, P]], channel_multiplier=-1).then_inc(masked.sem, 1)

            def rope_add(b, t):
                po.wait_ge(roped.sem, roped.at(b, t + 1))
                po.tensor_tensor(work[:, 0, :], work[:, 0, :], work[:, 1, :], ALU.add).then_inc(rope_sum.sem, 1)

            def inv_std(b, sig, rs):
                po.wait_ge(sig.sem, sig.at(b, 3))
                po.tensor_tensor(rstd[:], vare[:], half[:], ALU.pow).then_inc(rs.sem, 1)

            def low(b, u):
                po.wait_ge(a_high_done.sem, a_high_done.at(b, u + 1))
                po.tensor_tensor(a_part[1][:, u % 2, :], act[:, u % 2, :], a_part[0][:, u % 2, :].bitcast(F32),
                                 ALU.subtract).then_inc(a_low_done.sem, 1)
                if u == EXPERTS + 1:
                    add_stream(b, 0)

            def add_stream(b, f):
                if f == 0:
                    po.wait_ge(prev_copied.sem, prev_copied.at(b, 16))
                po.wait_ge(y_ready.sem, y_ready.at(b, f + 1))
                x_ = x1_prev[:, 2 * f:2 * f + 2, :].rearrange("p t d -> p (t d)")
                po.tensor_tensor(x_, x_, y_sb[:], ALU.add).then_inc(out_ready.sem, 1)

            def h2_rest(b, c):
                po.wait_ge(h2_high.sem, h2_high.at(b, c + 1))
                po.tensor_tensor(h2_part[1][:, c, :], h2T[:, c, :], h2_part[0][:, c, :].bitcast(F32), ALU.subtract)\
                    .then_inc(h2_low.sem, 1)

            def split_weights(e):
                po.wait_ge(w_high_done.sem, e + 1)
                po.tensor_tensor(w_part[1][:, e, :], stage[e % 2], w_part[0][:, e, :].bitcast(F32), ALU.subtract)\
                    .then_inc(w_low_done.sem, 1)

            def stack_constants(b):
                wait_apart(po, o_tr, b - 1, TILES, po_passed)
                po.memset(QS[:, :, MROW:STRIP], 0.0).then_inc(consts_set.sem, 1)
                po.memset(KS[:, :, MROW:MROW + 2], 1.0).then_inc(consts_set.sem, 1)
                po.memset(KS[:, :, MROW + 2:STRIP], 0.0).then_inc(consts_set.sem, 1)

            def attention(b, moe, more):
                m = b - 1
                for p in range(PAIRS):
                    u = after_pair(p)
                    if moe and u[0]:
                        low(m, u[0] - 1)
                    mask_probs(b, 2 * p)
                    if moe:
                        low(m, u[1] - 1)
                    else:
                        split_weights(u[0])
                    mask_probs(b, 2 * p + 1)
                    if not moe:
                        split_weights(u[1])
                    if more and p == 3:
                        inv_std(b + 1, ln1, rstd1)

            def tail(b, moe, more):
                n, m = b + 1, b - 1

                def lows(*us):
                    if moe:
                        for u in us:
                            low(m, UNITS - IN_TAIL + u)

                lows(-1, 0, 1)
                if more:
                    rope_add(n, 0)
                lows(2)
                if more:
                    stack_constants(n)
                lows(3)
                if more:
                    rope_add(n, 1)
                lows(4, 5, 6)
                if more:
                    rope_add(n, 2)
                inv_std(b, ln2, rstd2)
                lows(7, 8)
                if more:
                    rope_add(n, 3)
                lows(*range(9, IN_TAIL - 1))
                h2_rest(b, 0)
                lows(IN_TAIL - 1)
                h2_rest(b, 1)
                if moe:
                    add_stream(m, 1)

            po.memset(half[:], -0.5).then_inc(setup_p.sem, 1)
            po.wait_ge(setup_p.sem, 1)
            inv_std(0, ln1, rstd1)
            po.memset(V[:, :, :, HD:HD + 1], 1.0).then_inc(setup_p.sem, 1)
            po.memset(mt[:], 0.0).then_inc(setup_p.sem, 1)
            po.memset(before[:], 1.0).then_inc(setup_p.sem, 1)
            po.wait_ge(setup_p.sem, 4)
            bv = before[:, :].rearrange("p (t g o) -> p t g o", t=TILES, g=GROUPS)
            po.affine_select(out=bv, in_=bv, compare_op=ALU.is_gt, fill=0.0, base=0,
                             pattern=[[0, TILES], [1, GROUPS], [-1, GROUPS]], channel_multiplier=0).then_inc(setup_p.sem, 1)
            po.wait_ge(setup_t.sem, 2)
            stack_constants(0)
            for t in range(TILES):
                rope_add(0, t)

            def batch(b, moe, more):
                attention(b, moe, more)
                tail(b, moe, more)

            every_batch(po, lambda b: batch(b, False, True), lambda b: batch(b, True, True),
                        lambda b: batch(b, True, False))
            for u in range(UNITS):
                low(LAST, u)
            add_stream(LAST, 1)


def kernel(L0_attn_x, L0_attn_w_qkv, L0_attn_w_proj, L0_attn_b_proj, L0_ffn_router_weight, L0_ffn_router_bias,
           L0_ffn_w_gate, L0_ffn_w_up, L0_ffn_w_down, L0_c, L0_wmod):
    import concourse.bacc as bacc
    from concourse.bass_utils import run_bass_kernel_spmd

    def rows(w):
        w = np.asarray(w)
        return w.reshape(KC, P, w.shape[1]).transpose(1, 0, 2)

    inv_freq = (np.float32(1.0) / np.float32(10000.0) ** (np.arange(0, HD, 2, dtype=np.float32) / np.float32(HD))).astype(np.float32)
    angle = (np.arange(SEQ, dtype=np.float32)[:, None] * inv_freq[None, :]).astype(np.float32)
    cos = np.cos(angle.astype(np.float64)).astype(np.float32).reshape(TILES, P, HD // 2).transpose(1, 0, 2)
    sin = np.sin(angle.astype(np.float64)).astype(np.float32).reshape(TILES, P, HD // 2).transpose(1, 0, 2)
    tril = np.zeros((P, SEQ), np.float32)
    tril[:, SEQ - P:] = np.where(np.arange(P)[None, :] > np.arange(P)[:, None], np.float32(NEG), np.float32(0))
    pick = np.concatenate([np.eye(EXPERTS, dtype=np.float32)] * 2, axis=0)
    gate = np.asarray(L0_ffn_w_gate).reshape(EXPERTS, INNER, KC, P).transpose(3, 0, 2, 1)
    up = np.asarray(L0_ffn_w_up).reshape(EXPERTS, INNER, KC, P).transpose(3, 0, 2, 1)
    arrays = {
        "x": np.asarray(L0_attn_x),
        "wqkv": rows(L0_attn_w_qkv),
        "wproj": rows(L0_attn_w_proj),
        "bproj": np.asarray(L0_attn_b_proj)[None, :],
        "rw": rows(np.asarray(L0_ffn_router_weight).T),
        "rbias": np.asarray(L0_ffn_router_bias)[None, :],
        "wex": np.concatenate([gate.reshape(P, EXPERTS, KC * INNER), up.reshape(P, EXPERTS, KC * INNER),
                               np.asarray(L0_ffn_w_down).transpose(2, 0, 1)], axis=2),
        "ct": np.asarray(L0_c).T.reshape(KC, P, BATCH).transpose(1, 0, 2).reshape(P, KC * BATCH),
        "wmod": rows(L0_wmod),
        "cosq": cos,
        "sinq": np.stack([-sin, sin], axis=2),
        "tril_bias": tril,
        "ident": np.eye(P, dtype=np.float32),
        "pick": pick,
    }
    arrays = {n: np.ascontiguousarray(a) for n, a in arrays.items()}
    nc = bacc.Bacc("TRN2", target_bir_lowering=False, num_devices=1)
    args = {n: nc.dram_tensor(n, a.shape, mybir.dt.from_np(a.dtype), kind="ExternalInput").ap() for n, a in arrays.items()}
    y = nc.dram_tensor("y", (BATCH, SEQ, DIM), F32, kind="ExternalOutput").ap()
    build(nc, out=y, **args)
    r = run_bass_kernel_spmd(nc, [arrays], core_ids=[0])
    return r.results[0]["y"]
```
